# Optimizing a Trainium2 kernel written in Bass

```python
import numpy as np
import jax
import jax.numpy as jnp

def _softmax(x, axis=-1):
    return jax.nn.softmax(x, axis=axis)

def _gelu(x):
    return jax.nn.gelu(x, approximate=True)

def _silu(x):
    return jax.nn.silu(x)

def _sigmoid(x):
    return jax.nn.sigmoid(x)

def _layernorm(x, axis=-1, eps=1e-05):
    m = jnp.mean(x, axis=axis, keepdims=True)
    v = jnp.var(x, axis=axis, keepdims=True)
    return (x - m) / jnp.sqrt(v + eps)

def _scatter_add(tgt, idx, src, axis=0):
    return tgt.at[idx].add(src)

def _segment_sum(src, seg, n):
    return jax.ops.segment_sum(src, seg, n)
kernel_name = 'mk_lm_tower_d2_tok_ids512_r4_0eac89'

def setup_inputs(seed: int=0):
    np.random.seed(seed)
    _w = jnp.asarray

    def _rec_inputs():
        import jax
        import jax.numpy as jnp
        _rk = jax.random.key(seed)
        x = jax.random.randint(jax.random.fold_in(_rk, 1), (8, 1024), 0, 51, jnp.int32)
        return x
    x = _rec_inputs()

    def _L0_tok_setup():
        import jax, jax.numpy as jnp
        import numpy as np
        C, L = (32, 1024)
        NUM_BINS, HID, D = (51, 128, 128)
        key = jax.random.key(seed)
        k1, k2, k3, k4, k5, k6 = jax.random.split(key, 6)
        expr_tokens = jax.random.randint(k1, (C, L), 0, NUM_BINS, dtype=jnp.int64)
        bin_embeddings = jax.random.normal(k2, (NUM_BINS, D), dtype=jnp.float32)
        w1 = jax.random.normal(k3, (1, HID), dtype=jnp.float32) * 1.0
        b1 = jax.random.normal(k4, (HID,), dtype=jnp.float32) * 0.1
        w2 = jax.random.normal(k5, (HID, D), dtype=jnp.float32) * (1.0 / np.sqrt(HID))
        b2 = jax.random.normal(k6, (D,), dtype=jnp.float32) * 0.1
        return {'expr_tokens': expr_tokens, 'bin_embeddings': bin_embeddings, 'w1': w1, 'b1': b1, 'w2': w2, 'b2': b2}
    _L0_tok_all = _L0_tok_setup()
    _L0_tok_in = {k: v for k, v in _L0_tok_all.items() if k in ('bin_embeddings', 'w1', 'b1', 'w2', 'b2')}
    del _L0_tok_all

    def _L0_attn_setup():
        import jax, jax.numpy as jnp
        import numpy as np
        B, T, C, H = (4, 256, 128, 4)
        D = C // H
        N_LAYER, LAYER_ID = (12, 1)

        def layernorm(x, g, b, eps=1e-05):
            m = x.mean(-1, keepdims=True)
            v = ((x - m) ** 2).mean(-1, keepdims=True)
            return g * (x - m) / jnp.sqrt(v + eps) + b

        def rmsnorm(x, scale, eps=1e-08):
            norm = jnp.sqrt(jnp.sum(x * x, axis=-1, keepdims=True)) / x.shape[-1] ** 0.5
            return scale * (x / (norm + eps))

        def lnssm_scan(q, k, v, lam):
            qT, kT, vT = (jnp.moveaxis(a, 1, 0) for a in (q, k, v))
            Bq = q.shape[0]
            A0 = jnp.zeros((Bq, q.shape[2], q.shape[3], q.shape[3]), q.dtype)
            z0 = jnp.zeros((Bq, q.shape[2], q.shape[3]), q.dtype)

            def step(carry, inp):
                A, z = carry
                qt, kt, vt = inp
                A = lam[None, :, :, None] * A + kt[..., None] * vt[..., None, :]
                z = lam[None] * z + kt
                St = jnp.einsum('bhi,bhij->bhj', qt, A)
                Zt = jnp.einsum('bhi,bhi->bh', qt, z)
                return ((A, z), (St, Zt))
            _, (S, Zs) = jax.lax.scan(step, (A0, z0), (qT, kT, vT))
            return (jnp.moveaxis(S, 0, 1), jnp.moveaxis(Zs, 0, 1))
        key = jax.random.key(seed)
        ks = jax.random.split(key, 10)
        w = lambda k, shape: 0.02 * jax.random.normal(k, shape, dtype=jnp.float32)
        r01 = LAYER_ID / (N_LAYER - 1)
        r1a0 = 1.0 - LAYER_ID / N_LAYER
        i = np.arange(C, dtype=np.float32)
        time_decay = (-5.0 + 8.0 * (i / (C - 1)) ** (0.7 + 1.3 * r01)).astype(np.float32)
        xv = i / C
        tm_q = (xv ** r1a0).astype(np.float32)[None, None, :]
        tm_k = (xv ** r1a0).astype(np.float32)[None, None, :]
        tm_v = (xv ** r1a0 + 0.3 * r01).astype(np.float32)[None, None, :]
        tm_g = (xv ** (0.5 * r1a0)).astype(np.float32)[None, None, :]
        return dict(x=jax.random.normal(ks[0], (B, T, C), dtype=jnp.float32), ln1_g=jnp.ones((C,), jnp.float32), ln1_b=jnp.zeros((C,), jnp.float32), ln2_g=jnp.ones((C,), jnp.float32), ln2_b=jnp.zeros((C,), jnp.float32), time_decay=jnp.asarray(time_decay), tm_q=jnp.asarray(tm_q), tm_k=jnp.asarray(tm_k), tm_v=jnp.asarray(tm_v), tm_g=jnp.asarray(tm_g), Wq=w(ks[1], (C, C)), Wk=w(ks[2], (C, C)), Wv=w(ks[3], (C, C)), Wg=w(ks[4], (C, C)), Wo=w(ks[5], (C, C)), rms_scale=jnp.ones((C,), jnp.float32), W1=w(ks[6], (4 * C, C)), W2=w(ks[7], (C, 4 * C)))
    _L0_attn_all = _L0_attn_setup()
    _L0_attn_in = {k: v for k, v in _L0_attn_all.items() if k in ('ln1_g', 'ln1_b', 'ln2_g', 'ln2_b', 'time_decay', 'tm_q', 'tm_k', 'tm_v', 'tm_g', 'Wq', 'Wk', 'Wv', 'Wg', 'Wo', 'rms_scale', 'W1', 'W2')}
    del _L0_attn_all

    def _L0_ffn_setup():
        import jax, jax.numpy as jnp
        import numpy as np
        B, T, D = (4, 2048, 128)
        E, F, CAP = (8, 512, 1024)
        key = jax.random.key(seed)
        ks = jax.random.split(key, 6)
        s = 0.02
        return {'x': jax.random.normal(ks[0], (B, T, D), dtype=jnp.float32), 'Wr': jax.random.normal(ks[1], (D, E), dtype=jnp.float32) * s, 'W1': jax.random.normal(ks[2], (E, D, F), dtype=jnp.float32) * s, 'b1': jax.random.normal(ks[3], (E, F), dtype=jnp.float32) * s, 'W2': jax.random.normal(ks[4], (E, F, D), dtype=jnp.float32) * s, 'b2': jax.random.normal(ks[5], (E, D), dtype=jnp.float32) * s}
    _L0_ffn_all = _L0_ffn_setup()
    _L0_ffn_in = {k: v for k, v in _L0_ffn_all.items() if k in ('Wr', 'W1', 'b1', 'W2', 'b2')}
    del _L0_ffn_all

    def _L1_attn_setup():
        import math
        import jax, jax.numpy as jnp
        import numpy as np
        H, N, L_MAX = (128, 64, 512)
        BATCH = 8

        def _s4_forward(u, Lambda_re, Lambda_im, P, B, C, D, log_step):
            L = u.shape[1]
            Lam = jnp.minimum(Lambda_re, -0.0001) + 1j * Lambda_im
            Pc = P[..., 0] + 1j * P[..., 1]
            Bc = B[..., 0] + 1j * B[..., 1]
            Cc = C[..., 0] + 1j * C[..., 1]
            step = jnp.exp(log_step)[:, None]
            Omega = jnp.exp(jnp.arange(L) * (-2j * jnp.pi / L)).astype(jnp.complex64)
            g = 2.0 / step * ((1.0 - Omega) / (1.0 + Omega))
            c_scale = 2.0 / (1.0 + Omega)
            rec = 1.0 / (g[:, :, None] - Lam[:, None, :])

            def cau(v):
                return jnp.einsum('hn,hln->hl', v, rec)
            a0, a1 = (jnp.conj(Cc), jnp.conj(Pc))
            b0, b1 = (Bc, Pc)
            k00 = cau(a0 * b0)
            k01 = cau(a0 * b1)
            k10 = cau(a1 * b0)
            k11 = cau(a1 * b1)
            at_roots = c_scale[None, :] * (k00 - k01 * k10 / (1.0 + k11))
            K = jnp.fft.ifft(at_roots, n=L, axis=1).real.astype(u.dtype)
            fft_size = 2 * L
            U = jnp.fft.rfft(u, n=fft_size, axis=1)
            Kf = jnp.fft.rfft(K, n=fft_size, axis=1)
            Y = jnp.fft.irfft(U * Kf.T[None, :, :], n=fft_size, axis=1)[:, :L, :]
            return Y.astype(u.dtype) + u * D[None, None, :]
        key = jax.random.key(seed)
        ks = jax.random.split(key, 8)
        u = jax.random.normal(ks[0], (BATCH, L_MAX, H), dtype=jnp.float32)
        Lambda_re = -(jax.random.uniform(ks[1], (H, N), dtype=jnp.float32) * 0.5 + 0.05)
        Lambda_im = jax.random.normal(ks[2], (H, N), dtype=jnp.float32) * 3.0
        P = jax.random.normal(ks[3], (H, N, 2), dtype=jnp.float32)
        B = jax.random.normal(ks[4], (H, N, 2), dtype=jnp.float32)
        C = jax.random.normal(ks[5], (H, N, 2), dtype=jnp.float32) * 0.5 ** 0.5
        D = jnp.ones((H,), dtype=jnp.float32)
        log_step = jax.random.uniform(ks[6], (H,), dtype=jnp.float32) * (math.log(0.1) - math.log(0.001)) + math.log(0.001)
        return {'u': u, 'Lambda_re': Lambda_re, 'Lambda_im': Lambda_im, 'P': P, 'B': B, 'C': C, 'D': D, 'log_step': log_step}
    _L1_attn_all = _L1_attn_setup()
    _L1_attn_in = {k: v for k, v in _L1_attn_all.items() if k in ('Lambda_re', 'Lambda_im', 'P', 'B', 'C', 'D', 'log_step')}
    del _L1_attn_all

    def _L1_ffn_setup():
        import jax, jax.numpy as jnp
        import numpy as np
        B, T, H = (8, 2048, 128)
        E, R = (4, 16)
        SCALE = 0.04
        key = jax.random.key(seed)
        ks = jax.random.split(key, 7)
        return {'x': jax.random.normal(ks[0], (B, T, H), jnp.float32), 'gate_w': jax.random.normal(ks[1], (E, H), jnp.float32) * SCALE, 'thr_w': jax.random.normal(ks[2], (1, H), jnp.float32) * SCALE, 'fc1_w': jax.random.normal(ks[3], (E, H, H), jnp.float32) * SCALE, 'lora_A': jax.random.normal(ks[4], (E, H, R), jnp.float32) * SCALE, 'lora_B': jax.random.normal(ks[5], (E, R, H), jnp.float32) * SCALE, 'fc2_w': jax.random.normal(ks[6], (E, H, H), jnp.float32) * SCALE}
    _L1_ffn_all = _L1_ffn_setup()
    _L1_ffn_in = {k: v for k, v in _L1_ffn_all.items() if k in ('gate_w', 'thr_w', 'fc1_w', 'lora_A', 'lora_B', 'fc2_w')}
    del _L1_ffn_all
    return {'x': x, 'L0_tok_bin_embeddings': _L0_tok_in['bin_embeddings'], 'L0_tok_w1': _L0_tok_in['w1'], 'L0_tok_b1': _L0_tok_in['b1'], 'L0_tok_w2': _L0_tok_in['w2'], 'L0_tok_b2': _L0_tok_in['b2'], 'L0_attn_ln1_g': _L0_attn_in['ln1_g'], 'L0_attn_ln1_b': _L0_attn_in['ln1_b'], 'L0_attn_ln2_g': _L0_attn_in['ln2_g'], 'L0_attn_ln2_b': _L0_attn_in['ln2_b'], 'L0_attn_time_decay': _L0_attn_in['time_decay'], 'L0_attn_tm_q': _L0_attn_in['tm_q'], 'L0_attn_tm_k': _L0_attn_in['tm_k'], 'L0_attn_tm_v': _L0_attn_in['tm_v'], 'L0_attn_tm_g': _L0_attn_in['tm_g'], 'L0_attn_Wq': _L0_attn_in['Wq'], 'L0_attn_Wk': _L0_attn_in['Wk'], 'L0_attn_Wv': _L0_attn_in['Wv'], 'L0_attn_Wg': _L0_attn_in['Wg'], 'L0_attn_Wo': _L0_attn_in['Wo'], 'L0_attn_rms_scale': _L0_attn_in['rms_scale'], 'L0_attn_W1': _L0_attn_in['W1'], 'L0_attn_W2': _L0_attn_in['W2'], 'L0_ffn_Wr': _L0_ffn_in['Wr'], 'L0_ffn_W1': _L0_ffn_in['W1'], 'L0_ffn_b1': _L0_ffn_in['b1'], 'L0_ffn_W2': _L0_ffn_in['W2'], 'L0_ffn_b2': _L0_ffn_in['b2'], 'L1_attn_Lambda_re': _L1_attn_in['Lambda_re'], 'L1_attn_Lambda_im': _L1_attn_in['Lambda_im'], 'L1_attn_P': _L1_attn_in['P'], 'L1_attn_B': _L1_attn_in['B'], 'L1_attn_C': _L1_attn_in['C'], 'L1_attn_D': _L1_attn_in['D'], 'L1_attn_log_step': _L1_attn_in['log_step'], 'L1_ffn_gate_w': _L1_ffn_in['gate_w'], 'L1_ffn_thr_w': _L1_ffn_in['thr_w'], 'L1_ffn_fc1_w': _L1_ffn_in['fc1_w'], 'L1_ffn_lora_A': _L1_ffn_in['lora_A'], 'L1_ffn_lora_B': _L1_ffn_in['lora_B'], 'L1_ffn_fc2_w': _L1_ffn_in['fc2_w']}

def reference(x, L0_tok_bin_embeddings, L0_tok_w1, L0_tok_b1, L0_tok_w2, L0_tok_b2, L0_attn_ln1_g, L0_attn_ln1_b, L0_attn_ln2_g, L0_attn_ln2_b, L0_attn_time_decay, L0_attn_tm_q, L0_attn_tm_k, L0_attn_tm_v, L0_attn_tm_g, L0_attn_Wq, L0_attn_Wk, L0_attn_Wv, L0_attn_Wg, L0_attn_Wo, L0_attn_rms_scale, L0_attn_W1, L0_attn_W2, L0_ffn_Wr, L0_ffn_W1, L0_ffn_b1, L0_ffn_W2, L0_ffn_b2, L1_attn_Lambda_re, L1_attn_Lambda_im, L1_attn_P, L1_attn_B, L1_attn_C, L1_attn_D, L1_attn_log_step, L1_ffn_gate_w, L1_ffn_thr_w, L1_ffn_fc1_w, L1_ffn_lora_A, L1_ffn_lora_B, L1_ffn_fc2_w):
    import jax
    import jax.numpy as jnp

    def _L0_tok_ref(expr_tokens, bin_embeddings, w1, b1, w2, b2):
        import jax, jax.numpy as jnp
        import numpy as np
        C, L = (32, 1024)
        NUM_BINS, HID, D = (51, 128, 128)
        zero_mask = expr_tokens == 0
        x = expr_tokens.astype(jnp.float32)[..., None]
        h = jax.nn.relu(jnp.matmul(x, w1) + b1)
        enc = jnp.matmul(h, w2) + b2
        bins = bin_embeddings[1:]
        sim = jnp.einsum('cld,nd->cln', enc, bins)
        probs = jax.nn.softmax(sim, axis=-1)
        emb = jnp.einsum('cln,nd->cld', probs, bins)
        out = jnp.where(zero_mask[..., None], bin_embeddings[0], emb)
        return out

    def _L0_attn_ref(x, ln1_g, ln1_b, ln2_g, ln2_b, time_decay, tm_q, tm_k, tm_v, tm_g, Wq, Wk, Wv, Wg, Wo, rms_scale, W1, W2):
        import jax, jax.numpy as jnp
        import numpy as np
        B, T, C, H = (4, 256, 128, 4)
        D = C // H
        N_LAYER, LAYER_ID = (12, 1)

        def layernorm(x, g, b, eps=1e-05):
            m = x.mean(-1, keepdims=True)
            v = ((x - m) ** 2).mean(-1, keepdims=True)
            return g * (x - m) / jnp.sqrt(v + eps) + b

        def rmsnorm(x, scale, eps=1e-08):
            norm = jnp.sqrt(jnp.sum(x * x, axis=-1, keepdims=True)) / x.shape[-1] ** 0.5
            return scale * (x / (norm + eps))

        def lnssm_scan(q, k, v, lam):
            qT, kT, vT = (jnp.moveaxis(a, 1, 0) for a in (q, k, v))
            Bq = q.shape[0]
            A0 = jnp.zeros((Bq, q.shape[2], q.shape[3], q.shape[3]), q.dtype)
            z0 = jnp.zeros((Bq, q.shape[2], q.shape[3]), q.dtype)

            def step(carry, inp):
                A, z = carry
                qt, kt, vt = inp
                A = lam[None, :, :, None] * A + kt[..., None] * vt[..., None, :]
                z = lam[None] * z + kt
                St = jnp.einsum('bhi,bhij->bhj', qt, A)
                Zt = jnp.einsum('bhi,bhi->bh', qt, z)
                return ((A, z), (St, Zt))
            _, (S, Zs) = jax.lax.scan(step, (A0, z0), (qT, kT, vT))
            return (jnp.moveaxis(S, 0, 1), jnp.moveaxis(Zs, 0, 1))
        Bx, Tx, Cx = x.shape
        Hh, Dd = (H, Cx // H)
        h = layernorm(x, ln1_g, ln1_b)
        xx = jnp.concatenate([jnp.zeros_like(h[:, :1]), h[:, :-1]], axis=1)
        xq = h * tm_q + xx * (1 - tm_q)
        xk = h * tm_k + xx * (1 - tm_k)
        xv_ = h * tm_v + xx * (1 - tm_v)
        xg = h * tm_g + xx * (1 - tm_g)
        q = xq @ Wq.T
        k = xk @ Wk.T
        v = xv_ @ Wv.T
        g = jax.nn.sigmoid(xg @ Wg.T)
        q = jnp.exp(rmsnorm(q, rms_scale))
        k = jnp.exp(rmsnorm(k, rms_scale))
        lam = jnp.exp(-jnp.exp(time_decay)).reshape(Hh, Dd)
        qh = q.reshape(Bx, Tx, Hh, Dd)
        kh = k.reshape(Bx, Tx, Hh, Dd)
        vh = v.reshape(Bx, Tx, Hh, Dd)
        S, Zs = lnssm_scan(qh, kh, vh, lam)
        att = (S / Zs[..., None]).reshape(Bx, Tx, Cx)
        att = g * att @ Wo.T
        x = x + att
        h2 = layernorm(x, ln2_g, ln2_b)
        x = x + jax.nn.gelu(h2 @ W1.T, approximate=False) @ W2.T
        return x

    def _L0_ffn_ref(x, Wr, W1, b1, W2, b2):
        import jax, jax.numpy as jnp
        import numpy as np
        B, T, D = (4, 2048, 128)
        E, F, CAP = (8, 512, 1024)
        Bb, Tt, Dd = x.shape
        N = Bb * Tt
        C = min(CAP, N)
        x_flat = x.reshape(N, Dd)
        logits = x_flat @ Wr
        probs = jax.nn.softmax(logits, axis=0)
        vals, idx = jax.lax.top_k(probs.T, C)
        selected = x_flat[idx]
        h = jax.nn.gelu(jnp.einsum('ecd,edf->ecf', selected, W1) + b1[:, None, :], approximate=False)
        out_e = jnp.einsum('ecf,efd->ecd', h, W2) + b2[:, None, :]
        weighted = vals[..., None] * out_e
        output = jnp.zeros_like(x_flat).at[idx.reshape(-1)].add(weighted.reshape(-1, Dd))
        return output.reshape(Bb, Tt, Dd)

    def _L1_attn_ref(u, Lambda_re, Lambda_im, P, B, C, D, log_step):
        import math
        import jax, jax.numpy as jnp
        import numpy as np
        H, N, L_MAX = (128, 64, 512)
        BATCH = 8

        def _s4_forward(u, Lambda_re, Lambda_im, P, B, C, D, log_step):
            L = u.shape[1]
            Lam = jnp.minimum(Lambda_re, -0.0001) + 1j * Lambda_im
            Pc = P[..., 0] + 1j * P[..., 1]
            Bc = B[..., 0] + 1j * B[..., 1]
            Cc = C[..., 0] + 1j * C[..., 1]
            step = jnp.exp(log_step)[:, None]
            Omega = jnp.exp(jnp.arange(L) * (-2j * jnp.pi / L)).astype(jnp.complex64)
            g = 2.0 / step * ((1.0 - Omega) / (1.0 + Omega))
            c_scale = 2.0 / (1.0 + Omega)
            rec = 1.0 / (g[:, :, None] - Lam[:, None, :])

            def cau(v):
                return jnp.einsum('hn,hln->hl', v, rec)
            a0, a1 = (jnp.conj(Cc), jnp.conj(Pc))
            b0, b1 = (Bc, Pc)
            k00 = cau(a0 * b0)
            k01 = cau(a0 * b1)
            k10 = cau(a1 * b0)
            k11 = cau(a1 * b1)
            at_roots = c_scale[None, :] * (k00 - k01 * k10 / (1.0 + k11))
            K = jnp.fft.ifft(at_roots, n=L, axis=1).real.astype(u.dtype)
            fft_size = 2 * L
            U = jnp.fft.rfft(u, n=fft_size, axis=1)
            Kf = jnp.fft.rfft(K, n=fft_size, axis=1)
            Y = jnp.fft.irfft(U * Kf.T[None, :, :], n=fft_size, axis=1)[:, :L, :]
            return Y.astype(u.dtype) + u * D[None, None, :]
        return _s4_forward(u, Lambda_re, Lambda_im, P, B, C, D, log_step)

    def _L1_ffn_ref(x, gate_w, thr_w, fc1_w, lora_A, lora_B, fc2_w):
        import jax, jax.numpy as jnp
        import numpy as np
        B, T, H = (8, 2048, 128)
        E, R = (4, 16)
        SCALE = 0.04
        b, t, h = x.shape
        e = gate_w.shape[0]
        xf = x.reshape(-1, h)
        gate_logits = jax.nn.softmax(xf @ gate_w.T, axis=-1)
        thresholds = jax.nn.sigmoid(xf @ thr_w.T) * (1.0 / e)
        adapted = gate_logits - thresholds
        selected = (adapted >= 0).astype(xf.dtype)
        weights = adapted * selected
        wsum = jnp.sum(weights, axis=-1, keepdims=True)
        wsum = jnp.where(wsum == 0, jnp.ones_like(wsum), wsum)
        weights = weights / wsum
        hidden = jax.nn.relu(jnp.einsum('ni,ehi->neh', xf, fc1_w))
        lo = jnp.einsum('neh,ehr->ner', hidden, lora_A)
        lo = jnp.einsum('ner,ero->neo', lo, lora_B)
        expert_out = jnp.einsum('neo,edo->ned', lo, fc2_w)
        out = jnp.einsum('ne,ned->nd', weights, expert_out)
        return out.reshape(b, t, h)
    h = _L0_tok_ref(x, L0_tok_bin_embeddings, L0_tok_w1, L0_tok_b1, L0_tok_w2, L0_tok_b2)
    h = h + _L0_attn_ref(_layernorm(h, axis=-1), L0_attn_ln1_g, L0_attn_ln1_b, L0_attn_ln2_g, L0_attn_ln2_b, L0_attn_time_decay, L0_attn_tm_q, L0_attn_tm_k, L0_attn_tm_v, L0_attn_tm_g, L0_attn_Wq, L0_attn_Wk, L0_attn_Wv, L0_attn_Wg, L0_attn_Wo, L0_attn_rms_scale, L0_attn_W1, L0_attn_W2)
    h = h + _L0_ffn_ref(_layernorm(h, axis=-1), L0_ffn_Wr, L0_ffn_W1, L0_ffn_b1, L0_ffn_W2, L0_ffn_b2)
    h = h + _L1_attn_ref(_layernorm(h, axis=-1), L1_attn_Lambda_re, L1_attn_Lambda_im, L1_attn_P, L1_attn_B, L1_attn_C, L1_attn_D, L1_attn_log_step)
    h = h + _L1_ffn_ref(_layernorm(h, axis=-1), L1_ffn_gate_w, L1_ffn_thr_w, L1_ffn_fc1_w, L1_ffn_lora_A, L1_ffn_lora_B, L1_ffn_fc2_w)
    return h

_drawn_inputs = setup_inputs


def setup_inputs(seed=0):
    import zlib

    import numpy as np

    out = dict(_drawn_inputs(seed))
    spreads = {'L0_attn_ln1_g': (1.0, 0.6),
     'L0_attn_ln1_b': (0.0, 0.8),
     'L0_attn_ln2_g': (1.0, 0.6),
     'L0_attn_ln2_b': (0.0, 2.0),
     'L0_attn_rms_scale': (1.0, 0.6),
     'L1_attn_D': (1.0, 0.6)}
    factors = {'L0_tok_b1': 8.0,
     'L0_tok_b2': 8.0,
     'L0_attn_time_decay': 8.0,
     'L0_attn_tm_q': 24.97,
     'L0_attn_tm_k': 8.0,
     'L0_attn_tm_v': 8.0,
     'L0_attn_tm_g': 8.0,
     'L0_attn_Wq': 8.0,
     'L0_attn_Wk': 8.0,
     'L0_attn_Wv': 4.448,
     'L0_attn_Wg': 8.0,
     'L0_attn_Wo': 4.55,
     'L0_ffn_Wr': 64.0,
     'L0_ffn_W1': 64.0,
     'L0_ffn_b1': 200.0,
     'L0_ffn_W2': 64.0,
     'L0_ffn_b2': 200.0,
     'L1_ffn_gate_w': 8.0,
     'L1_ffn_thr_w': 8.0,
     'L1_ffn_fc1_w': 8.0,
     'L1_ffn_lora_A': 8.0,
     'L1_ffn_lora_B': 8.0,
     'L1_ffn_fc2_w': 8.0}
    for name, (base, spread) in spreads.items():
        noise = np.random.default_rng([zlib.crc32(name.encode()), seed]).standard_normal(out[name].shape)
        drawn = base * np.exp(spread * noise) if base else spread * noise
        out[name] = jnp.asarray(drawn.astype(out[name].dtype))
    for name, factor in factors.items():
        out[name] = (out[name] * factor).astype(out[name].dtype)
    return out
```

```python
import numpy as np
import concourse.bass as bass
from concourse import mybir
from contextlib import ExitStack

F32 = mybir.dt.float32
I32 = mybir.dt.int32
U32 = mybir.dt.uint32
ALU = mybir.AluOpType
ACT = mybir.ActivationFunctionType
AX = mybir.AxisListType

P = 128
BATCH, SEQ, D = 8, 1024, 128
TILES = SEQ // P
NT = BATCH * TILES
TOK = BATCH * SEQ
HALF = 512
BINS = 51


class Steps:

    def __init__(self, eng, sem, i=0, per=0):
        self.eng, self.sem, self.base, self.per, self.n = eng, sem, i * per, per, 0

    def link(self, ins):
        ins.then_inc(self.sem, 1)
        self.n += 1
        self.eng.wait_ge(self.sem, self.base + self.n)

    def close(self):
        assert self.n == self.per, (self.n, self.per)


USED = []


class Mem:

    def __init__(self, nc, ctx, tag, banks=None):
        self.nc, self.ctx, self.tag, self.banks, self.used, self.sems = nc, ctx, tag, banks, 0, []
        ctx.callback(USED.extend, self.sems)

    def sb(self, name, shape, dt=F32):
        return self.ctx.enter_context(self.nc.sbuf_tensor(f"{self.tag}_{name}", shape, dt))

    def ps(self, shape=(P, HALF)):
        bank = self.banks[:, self.used, 0:int(np.prod(shape[1:]))]
        self.used += 1
        if len(shape) == 3:
            bank = bank.rearrange("p (a b) -> p a b", b=shape[2])
        return bank

    def sem(self, name):
        self.sems.append(self.nc.alloc_semaphore(f"{self.tag}_{name}"))
        return self.sems[-1]


def reset_used(nc):
    nc.clear_and_free_semaphores(USED)
    USED.clear()


def passes(eng, n):
    yield 0
    with eng.Fori(1, n) as i:
        yield i


def spread(ap, n):
    return ap.unsqueeze(2).broadcast_to([ap.shape[0], ap.shape[1], n])


def load_constants(nc, w, k):
    with ExitStack() as ctx:
        m = Mem(nc, ctx, "ld", k["banks"])
        s_in, s_ps, s_cp = m.sem("in"), m.sem("turned"), m.sem("copied")
        s_id = m.sem("identity")
        raw = m.sb("raw", [P, 24, P])
        rows = [m.ps((P, P)) for i in range(2)]
        jobs = [(w[f"L0_attn_{n}"], k[n][:, :]) for n in ("Wq", "Wk", "Wv", "Wg", "Wo")]
        jobs += [(w["L0_attn_W1"][P * f:P * f + P, :], k["W1T"][:, P * f:P * f + P]) for f in range(4)]
        jobs += [(w["L0_attn_W2"][:, P * f:P * f + P], k["W2T"][:, f, :]) for f in range(4)]
        jobs += [(w["L1_ffn_fc1_w"][e], k["fc1T"][:, e, :]) for e in range(4)]
        jobs += [(w["L0_tok_bin_embeddings"], k["binsT"][:, :])]
        vectors = ["L0_tok_b1", "L0_attn_ln1_g", "L0_attn_ln1_b", "L0_attn_ln2_g", "L0_attn_ln2_b",
                   "L0_attn_time_decay", "L0_attn_rms_scale"]
        tms = ["L0_attn_tm_q", "L0_attn_tm_k", "L0_attn_tm_v", "L0_attn_tm_g"]
        nvec = len(vectors) + len(tms)
        with nc.Block() as block:
            @block.sync
            def _(sp):
                for j, (src, dst) in enumerate(jobs):
                    sp.dma_start(raw[0:src.shape[0], j, 0:src.shape[1]], src).then_inc(s_in, 16)
                for j, n in enumerate(vectors):
                    sp.dma_start(raw[j:j + 1, len(jobs), :], w[n].rearrange("(a c) -> a c", a=1)).then_inc(s_in, 16)
                for j, n in enumerate(tms):
                    sp.dma_start(raw[len(vectors) + j:len(vectors) + j + 1, len(jobs), :],
                                 w[n].rearrange("a b c -> (a b) c")).then_inc(s_in, 16)
                sp.wait_ge(s_id, 3)
                sp.dma_start(k["bins"][0:BINS, 0:P], w["L0_tok_bin_embeddings"]).then_inc(s_in, 16)
                sp.dma_start(k["bins"][64:64 + BINS, P:2 * P], w["L0_tok_bin_embeddings"]).then_inc(s_in, 16)
                sp.wait_ge(s_in, 16 * (len(jobs) + nvec + 2))

            @block.gpsimd
            def _(pool):
                nc.gpsimd.memset(k["ones"][:, :], 1.0).then_inc(s_id, 1)
                nc.gpsimd.memset(k["neg_half"][:, :], -0.5).then_inc(s_id, 1)
                nc.gpsimd.memset(k["bins"][:, :], 0.0).then_inc(s_id, 1)
                pool.wait_ge(s_id, 3)
                nc.gpsimd.affine_select(out=k["ident"][:, :], in_=k["ones"][:, :], compare_op=ALU.is_equal,
                                        fill=0.0, base=0, pattern=[[-1, P]], channel_multiplier=1).then_inc(s_id, 1)

            every = jobs + [(None, k["cols"][:, 0:nvec])]

            @block.tensor
            def _(pe):
                pe.wait_ge(s_id, 4)
                pe.wait_ge(s_in, 16 * (len(jobs) + nvec + 2))
                for j, (src, dst) in enumerate(every):
                    n = src.shape[0] if src is not None else nvec
                    if j >= 2:
                        pe.wait_ge(s_cp, j - 1)
                    nc.tensor.transpose(rows[j % 2][:, 0:n], raw[0:n, j, :], k["ident"][0:n, 0:n]).then_inc(s_ps, 1)

            @block.vector
            def _(dve):
                for j, (src, dst) in enumerate(every):
                    n = src.shape[0] if src is not None else nvec
                    dve.wait_ge(s_ps, j + 1)
                    nc.vector.tensor_copy(dst, rows[j % 2][:, 0:n]).then_inc(s_cp, 1)


def embed_tokens(nc, w, k, H):
    with ExitStack() as ctx:
        m = Mem(nc, ctx, "tok", k["banks"])
        tok_i = m.sb("tok_i", [1, TOK], I32)
        tok_f = m.sb("tok_f", [1, TOK])
        til_i = m.sb("til_i", [NT, P], I32)
        til_f = m.sb("til_f", [NT, P])
        live = m.sb("live", [P, NT])
        dead = m.sb("dead", [P, NT])
        w1 = m.sb("w1", [1, P])
        w2T = m.sb("w2T", [P, P])
        w2 = m.sb("w2", [P, P])
        b2 = m.sb("b2", [P, 1])
        simw = m.sb("simw", [P, BINS])
        simb = m.sb("simb", [1, BINS])
        hT = [m.sb(f"hT{u}", [P, HALF]) for u in range(2)]
        ex = [m.sb(f"ex{u}", [P, 4, 64]) for u in range(2)]
        prob = [m.sb(f"prob{u}", [P, 4, 64]) for u in range(2)]
        pT = [m.sb(f"pT{u}", [P, 2 * P]) for u in range(2)]
        mx = [m.sb(f"mx{u}", [P, 4]) for u in range(2)]
        sm = [m.sb(f"sm{u}", [P, 4]) for u in range(2)]
        inv = [m.sb(f"inv{u}", [P, 4]) for u in range(2)]
        ph = [m.ps() for u in range(2)]
        psim = [m.ps((P, 4, 64)) for u in range(2)]
        pp = [m.ps() for u in range(2)]
        pe_ = [m.ps() for u in range(2)]
        s_in, s_f, s_w, s_wc = m.sem("in"), m.sem("float"), m.sem("weights"), m.sem("wcopied")
        s_h = [m.sem(f"h{u}") for u in range(2)]
        s_relu = [m.sem(f"relu{u}") for u in range(2)]
        s_sim = [m.sem(f"sim{u}") for u in range(2)]
        s_sub = [m.sem(f"sub{u}") for u in range(2)]
        s_exp = [m.sem(f"exp{u}") for u in range(2)]
        s_prob = [m.sem(f"prob{u}") for u in range(2)]
        s_pT = [m.sem(f"pT{u}") for u in range(2)]
        s_pTc = [m.sem(f"pTc{u}") for u in range(2)]
        s_emb = [m.sem(f"emb{u}") for u in range(2)]
        s_out = [m.sem(f"out{u}") for u in range(2)]
        s_dve = m.sem("dve")
        NG = TOK // HALF
        with nc.Block() as block:
            @block.sync
            def _(sp):
                sp.dma_start(tok_i[:, :], w["x"].rearrange("b (t c) -> (b t) c", t=1).rearrange("(a b) c -> a (b c)", a=1)).then_inc(s_in, 16)
                sp.dma_start(til_i[:, :], w["x"].rearrange("b (t c) -> (b t) c", c=P)).then_inc(s_in, 16)
                sp.dma_start(w1[:, :], w["L0_tok_w1"]).then_inc(s_in, 16)
                sp.dma_start(w2[:, :], w["L0_tok_w2"]).then_inc(s_in, 16)
                sp.dma_start(b2[:, :], w["L0_tok_b2"].rearrange("(c a) -> c a", a=1)).then_inc(s_in, 16)

            @block.tensor
            def _(pe):
                pe.wait_ge(s_f, 2)
                nc.tensor.transpose(pp[0][:, 0:NT], til_f[:, :], k["ident"][0:NT, 0:NT]).then_inc(s_w, 1)
                nc.tensor.transpose(pp[1][:, 0:P], w2[:, :], k["ident"][:, :]).then_inc(s_w, 1)
                pe.wait_ge(s_wc, 3)
                nc.tensor.matmul(ph[0][:, 0:BINS], w2T[:, :], k["binsT"][:, :], start=True, stop=True).then_inc(s_w, 1)
                nc.tensor.matmul(ph[1][0:1, 0:BINS], b2[:, :], k["binsT"][:, :], start=True, stop=True).then_inc(s_w, 1)
                pe.wait_ge(s_wc, 7)
                for i in passes(pe, NG // 2):
                    for u in range(2):
                        pe.wait_ge(s_relu[u], i)
                        nc.tensor.matmul(ph[u][:, :], w1[:, :], tok_f[0:1, bass.ds((i * 2 + u) * HALF, HALF)],
                                         start=True, stop=True).then_inc(s_h[u], 1)
                    for u in range(2):
                        pe.wait_ge(s_relu[u], i + 1)
                        pe.wait_ge(s_sub[u], i)
                        for s in range(4):
                            nc.tensor.matmul(psim[u][:, s, 0:BINS], hT[u][:, P * s:P * s + P], simw[:, :],
                                             start=(s == 0), stop=False, skip_group_check=True)
                            ins = nc.tensor.matmul(psim[u][:, s, 0:BINS], k["ones"][0:1, :], simb[:, :],
                                                   start=False, stop=(s == 3), skip_group_check=True)
                        ins.then_inc(s_sim[u], 1)
                    for u in range(2):
                        pe.wait_ge(s_prob[u], i + 1)
                        pe.wait_ge(s_pTc[u], i)
                        for s in range(2):
                            ins = nc.tensor.transpose(pp[u][:, P * s:P * s + P],
                                                      prob[u][:, 2 * s:2 * s + 2, :].rearrange("p a b -> p (a b)"), k["ident"][:, :])
                        ins.then_inc(s_pT[u], 1)
                    for u in range(2):
                        pe.wait_ge(s_pTc[u], i + 1)
                        pe.wait_ge(s_out[u], i)
                        for s in range(2):
                            ins = nc.tensor.matmul(pe_[u][:, 2 * P * s:2 * P * s + 2 * P], pT[u][:, P * s:P * s + P], k["bins"][:, :],
                                                   start=True, stop=True, skip_group_check=True)
                        ins.then_inc(s_emb[u], 1)

            @block.scalar
            def _(act):
                for i in passes(act, NG // 2):
                    for u in range(2):
                        act.wait_ge(s_h[u], i + 1)
                        act.wait_ge(s_sim[u], i)
                        nc.scalar.activation(hT[u][:, :], ph[u][:, :], ACT.Relu, bias=k["b1"]).then_inc(s_relu[u], 1)
                    for u in range(2):
                        act.wait_ge(s_sub[u], i + 1)
                        nc.scalar.activation(prob[u][:, :, 1:BINS], ex[u][:, :, 1:BINS], ACT.Exp).then_inc(s_exp[u], 1)
                    for u in range(2):
                        act.wait_ge(s_pT[u], i + 1)
                        act.wait_ge(s_emb[u], i)
                        nc.scalar.copy(pT[u][:, :], pp[u][:, 0:2 * P]).then_inc(s_pTc[u], 1)
                    for u in range(2):
                        act.wait_ge(s_emb[u], i + 1)
                        nc.scalar.copy(H[:, bass.ds((i * 2 + u) * 4, 4), :], pe_[u][:, :].rearrange("p (s d) -> p s d", s=4)).then_inc(s_out[u], 1)

            @block.vector
            def _(dve):
                for u in range(2):
                    nc.vector.memset(prob[u][:, :, :], 0.0).then_inc(s_wc, 1)
                dve.wait_ge(s_in, 80)
                nc.vector.tensor_copy(tok_f[:, :], tok_i[:, :]).then_inc(s_f, 1)
                nc.vector.tensor_copy(til_f[:, :], til_i[:, :]).then_inc(s_f, 1)
                dve.wait_ge(s_w, 2)
                nc.vector.tensor_copy(w2T[:, :], pp[1][:, 0:P]).then_inc(s_wc, 1)
                nc.vector.tensor_scalar(live[:, :], pp[0][:, 0:NT], 0.0, None, ALU.not_equal).then_inc(s_wc, 1)
                nc.vector.tensor_scalar(dead[:, :], pp[0][:, 0:NT], 0.0, None, ALU.is_equal).then_inc(s_wc, 1)
                dve.wait_ge(s_w, 4)
                nc.vector.tensor_copy(simw[:, :], ph[0][:, 0:BINS]).then_inc(s_wc, 1)
                nc.vector.tensor_copy(simb[:, :], ph[1][0:1, 0:BINS]).then_inc(s_wc, 1)
                dve.wait_ge(s_wc, 7)
                for i in passes(dve, NG // 2):
                    st = Steps(dve, s_dve, i, 8)
                    for u in range(2):
                        dve.wait_ge(s_sim[u], i + 1)
                        dve.wait_ge(s_exp[u], i)
                        st.link(nc.vector.tensor_reduce(mx[u][:, :], psim[u][:, :, 1:BINS], AX.X, ALU.max))
                        nc.vector.tensor_tensor(ex[u][:, :, 1:BINS], psim[u][:, :, 1:BINS], spread(mx[u][:, :], BINS - 1),
                                                ALU.subtract).then_inc(s_sub[u], 1)
                    for u in range(2):
                        dve.wait_ge(s_exp[u], i + 1)
                        st.link(nc.vector.tensor_reduce(sm[u][:, :], prob[u][:, :, 1:BINS], AX.X, ALU.add))
                        st.link(nc.vector.reciprocal(inv[u][:, :], sm[u][:, :]))
                        st.link(nc.vector.tensor_tensor(inv[u][:, :], inv[u][:, :], live[:, bass.ds((i * 2 + u) * 4, 4)], ALU.mult))
                        nc.vector.tensor_copy(prob[u][:, :, 0:1].rearrange("p a b -> p (a b)"), dead[:, bass.ds((i * 2 + u) * 4, 4)])
                        nc.vector.tensor_tensor(prob[u][:, :, 1:BINS], prob[u][:, :, 1:BINS], spread(inv[u][:, :], BINS - 1),
                                                ALU.mult).then_inc(s_prob[u], 1)
                    st.close()


def constants(nc, m):
    k = {n: m.sb(n, [P, P]) for n in ("ident", "ones", "Wq", "Wk", "Wv", "Wg", "Wo")}
    k["banks"] = m.ctx.enter_context(nc.psum_tensor("banks", [P, 8, HALF], F32))
    k["W1T"] = m.sb("W1T", [P, 4 * P])
    k["W2T"] = m.sb("W2T", [P, 4, P])
    k["fc1T"] = m.sb("fc1T", [P, 4, P])
    k["binsT"] = m.sb("binsT", [P, BINS])
    k["bins"] = m.sb("bins", [P, 2 * P])
    k["neg_half"] = m.sb("neg_half", [P, 16])
    k["cols"] = m.sb("cols", [P, 16])
    for j, n in enumerate(("b1", "ln1_g", "ln1_b", "ln2_g", "ln2_b", "time_decay", "rms", "tm_q", "tm_k", "tm_v", "tm_g")):
        k[n] = k["cols"][:, j:j + 1]
    return k


LEVELS = (64, 32, 16, 8, 4, 2, 1)
NL = len(LEVELS)
HEADS, DH = 4, 32


def attention_tables():
    see = np.zeros((P, NL, P // 2), np.float32)
    for l, b in enumerate(LEVELS):
        for c in range(P // 2):
            start = c // b * 2 * b
            see[start:start + b, l, c] = 1.0
    blk = np.kron(np.eye(HEADS, dtype=np.float32), np.ones((DH, DH), np.float32))
    up = np.tile(np.arange(P + 1, dtype=np.float32), (P, 1))
    return {"c_see": see.reshape(P, NL * P // 2), "c_heads": blk, "c_up": up, "c_down": up[:, ::-1].copy()}


def merge_stats(nc, st, stats, mean, sq, var):
    nc.vector.tensor_tensor(mean, stats[:, :, 1], stats[:, :, 4], ALU.add)
    nc.vector.tensor_tensor(sq, stats[:, :, 1], stats[:, :, 4], ALU.subtract)
    st.link(nc.vector.tensor_tensor(var, stats[:, :, 2], stats[:, :, 5], ALU.add))
    nc.vector.tensor_scalar(mean, mean, 0.5, None, ALU.mult)
    nc.vector.tensor_scalar(var, var, 1.0 / D, 1e-5, ALU.mult, ALU.add)
    st.link(nc.vector.tensor_tensor(sq, sq, sq, ALU.mult))
    return nc.vector.scalar_tensor_tensor(out=var, in0=sq, scalar=0.25, in1=var, op0=ALU.mult, op1=ALU.add)


def normalise_stats(nc, dve, st, src, stats, mean, sq, var):
    for t in range(TILES):
        ins = nc.vector.bn_stats(stats[:, t, :], src(t))
    st.link(ins)
    return merge_stats(nc, st, stats[:, :, :], mean[:, :], sq[:, :], var[:, :])


def attention(nc, w, k, H, X2):
    with ExitStack() as ctx:
        m = Mem(nc, ctx, "at", k["banks"])
        x, xn = m.sb("x", [P, TILES, P]), m.sb("xn", [P, TILES, P])
        hs = m.sb("hs", [P, SEQ + 1])
        diff = xn[:, :, :].rearrange("p a b -> p (a b)")
        xm = [m.sb(f"xm{j}", [P, SEQ]) for j in range(4)]
        q, kk = m.sb("q", [P, SEQ]), m.sb("k", [P, SEQ])
        sq = [m.sb(f"sq{j}", [P, SEQ]) for j in range(2)]
        qz, qk = sq
        qin, kend = xm[0], xm[1]
        z, rZ = xm[2], xm[3]
        v = m.sb("v", [P, TILES, P])
        vT, gT, dv = m.sb("vT", [P, SEQ]), m.sb("gT", [P, SEQ]), m.sb("dv", [P, SEQ])
        ktl, qtl = m.sb("ktl", [P, NL, SEQ]), m.sb("qtl", [P, NL, SEQ // 2])
        pm = [m.sb(f"pm{j}", [P, HEADS, NL * 64]) for j in range(2)]
        att = m.sb("att", [P, SEQ])
        see, heads = m.sb("see", [P, NL * 64]), m.sb("heads", [P, P])
        up, down = m.sb("up", [P, P + 1]), m.sb("down", [P, P + 1])
        pw, rpw = m.sb("pw", [P, P + 1]), m.sb("rpw", [P, P + 1])
        lnl = m.sb("lnl", [P, 2])
        state = [m.sb(f"state{j}", [P, P]) for j in range(2)]
        um = m.sb("um", [P, P])
        kendT = m.sb("kendT", [P, P])
        stats = m.sb("stats", [P, TILES, 6])
        mean, sqm = m.sb("mean", [P, TILES]), m.sb("sqm", [P, TILES])
        var, rstd = m.sb("var", [P, TILES]), m.sb("rstd", [P, TILES])
        ssv, root = m.sb("ssv", [P, 16]), m.sb("root", [P, 16])
        half = m.sb("half", [P, 16])
        PS = k["banks"]
        S = {n: m.sem(n) for n in (
            "in var rstd x var2 rstd2 xn turned hs mix proj proj_sb sq ss ssv root rms rb qn exp v vt g vsb gsb z "
            "zb rz diag dv ktl qtl qin kend kt ktsb u state inter scoreA scoreB maskA maskB av s att wo x2 dve pool lam ready").split()}
        flat = lambda t: t[:, :, :].rearrange("p a b -> p (a b)")
        with nc.Block() as block:
            @block.sync
            def _(sp):
                for dst, src in ((see, "c_see"), (heads, "c_heads"), (up, "c_up"), (down, "c_down")):
                    sp.dma_start(dst[:, :], w[src]).then_inc(S["in"], 16)
                sp.wait_ge(S["in"], 64)

            @block.gpsimd
            def _(pool):
                nc.gpsimd.memset(half[:, :], 0.5).then_inc(S["ready"], 1)
                nc.gpsimd.memset(ktl[:, :, :], 0.0).then_inc(S["ready"], 1)
                pool.wait_ge(S["ready"], 2)
                pool.wait_ge(S["lam"], 4)
                for b in passes(pool, BATCH):
                    pool.wait_ge(S["var"], b + 1)
                    nc.gpsimd.tensor_tensor(rstd[:, :], var[:, :], k["neg_half"][:, 0:TILES], ALU.pow).then_inc(S["rstd"], 1)
                    pool.wait_ge(S["var2"], b + 1)
                    nc.gpsimd.tensor_tensor(rstd[:, :], var[:, :], k["neg_half"][:, 0:TILES], ALU.pow).then_inc(S["rstd2"], 1)
                    pool.wait_ge(S["ssv"], b + 1)
                    nc.gpsimd.tensor_tensor(root[:, :], ssv[:, :], half[:, :], ALU.pow).then_inc(S["root"], 1)
                    pool.wait_ge(S["exp"], 2 * b + 2)
                    nc.gpsimd.tensor_tensor(qk[:, :], q[:, :], kk[:, :], ALU.mult).then_inc(S["diag"], 1)
                    nc.gpsimd.tensor_tensor(kend[:, :].rearrange("p (n t) -> p n t", t=P), kk[:, :].rearrange("p (n t) -> p n t", t=P),
                                            rpw[:, 1:P + 1].unsqueeze(1).broadcast_to([P, TILES, P]), ALU.mult).then_inc(S["kend"], 1)
                    for l, h in enumerate(LEVELS):
                        nb = SEQ // (2 * h)
                        left = lambda t: t.rearrange("p (n s c) -> p n s c", s=2, c=h)[:, :, 0, :]
                        nc.gpsimd.tensor_tensor(left(ktl[:, l, :]), left(kk[:, :]),
                                                rpw[:, P - h:P].unsqueeze(1).broadcast_to([P, nb, h]), ALU.mult).then_inc(S["ktl"], 1)

            @block.scalar
            def _(act):
                act.wait_ge(S["lam"], 1)
                nc.scalar.activation(lnl[:, 1:2], lnl[:, 0:1], ACT.Exp).then_inc(S["lam"], 1)
                act.wait_ge(S["lam"], 3)
                act.wait_ge(S["in"], 64)
                nc.scalar.activation(pw[:, :], up[:, :], ACT.Exp, scale=lnl[:, 0:1])
                nc.scalar.activation(rpw[:, :], down[:, :], ACT.Exp, scale=lnl[:, 0:1]).then_inc(S["lam"], 1)
                for b in passes(act, BATCH):
                    for j in range(2):
                        act.wait_ge(S["turned"], 2 * b + j + 1)
                        nc.scalar.activation(hs[:, 1 + HALF * j:1 + HALF * j + HALF], PS[:, j, :], ACT.Identity,
                                             bias=k["ln1_b"], scale=k["ln1_g"]).then_inc(S["hs"], 1)
                    for j in range(4):
                        act.wait_ge(S["proj"], 4 * b + j + 1)
                        dst = (q, kk)[j // 2][:, HALF * (j % 2):HALF * (j % 2) + HALF]
                        nc.scalar.copy(dst, PS[:, j, :]).then_inc(S["proj_sb"], 1)
                        nc.scalar.activation(sq[j // 2][:, HALF * (j % 2):HALF * (j % 2) + HALF], PS[:, j, :], ACT.Square).then_inc(S["sq"], 1)
                    for j, (a, n) in enumerate(((q, "qn"), (kk, "qn"))):
                        act.wait_ge(S["qn"], 2 * b + j + 1)
                        nc.scalar.activation(a[:, :], a[:, :], ACT.Exp, scale=k["rms"]).then_inc(S["exp"], 1)
                    act.wait_ge(S["v"], b + 1)
                    nc.scalar.copy(flat(v), PS[:, 0:2, :].rearrange("p a b -> p (a b)")).then_inc(S["vsb"], 1)
                    act.wait_ge(S["vt"], b + 1)
                    nc.scalar.copy(vT[:, :], PS[:, 2:4, :].rearrange("p a b -> p (a b)")).then_inc(S["vsb"], 1)
                    act.wait_ge(S["g"], b + 1)
                    nc.scalar.activation(gT[:, :], PS[:, 4:6, :].rearrange("p a b -> p (a b)"), ACT.Tanh, scale=0.5).then_inc(S["gsb"], 1)
                    for n in range(TILES - 1):
                        act.wait_ge(S["kt"], (TILES - 1) * b + n + 1)
                        nc.scalar.copy(kendT[:, :], PS[:, 6, 0:P]).then_inc(S["ktsb"], 1)

            @block.tensor
            def _(pe):
                for b in passes(pe, BATCH):
                    pe.wait_ge(S["xn"], b + 1)
                    pe.wait_ge(S["x2"], 2 * b)
                    for j in range(2):
                        for t in range(4):
                            ins = nc.tensor.transpose(PS[:, j, P * t:P * t + P], xn[:, 4 * j + t, :], k["ident"][:, :])
                        ins.then_inc(S["turned"], 1)
                    for j in range(4):
                        if j % 2 == 0:
                            pe.wait_ge(S["mix"], 4 * b + j // 2 + 1)
                        nc.tensor.matmul(PS[:, j, :], k[("Wq", "Wk")[j // 2]][:, :], xm[j // 2][:, HALF * (j % 2):HALF * (j % 2) + HALF],
                                         start=True, stop=True).then_inc(S["proj"], 1)
                    for j in range(2):
                        pe.wait_ge(S["sq"], 4 * b + 2 * j + 2)
                        for t in range(TILES):
                            ins = nc.tensor.matmul(PS[:, 4, 8 * j + t:8 * j + t + 1], sq[j][:, P * t:P * t + P], k["ones"][:, 0:1],
                                                   start=True, stop=True, skip_group_check=True)
                    ins.then_inc(S["ss"], 1)
                    pe.wait_ge(S["rms"], b + 1)
                    for j in range(2):
                        for t in range(TILES):
                            ins = nc.tensor.matmul(PS[:, 4 + 2 * j + t // 4, P * (t % 4):P * (t % 4) + P],
                                                   ssv[:, 8 * j + t:8 * j + t + 1].broadcast_to([P, P]), k["ident"][:, :],
                                                   start=True, stop=True, skip_group_check=True)
                        ins.then_inc(S["rb"], 1)
                    pe.wait_ge(S["mix"], 4 * b + 4)
                    for t in range(TILES):
                        ins = nc.tensor.matmul(PS[:, t // 4, P * (t % 4):P * (t % 4) + P], xm[2][:, P * t:P * t + P], k["Wv"][:, :],
                                               start=True, stop=True, skip_group_check=True)
                    ins.then_inc(S["v"], 1)
                    for j in range(2):
                        ins = nc.tensor.matmul(PS[:, 2 + j, :], k["Wv"][:, :], xm[2][:, HALF * j:HALF * j + HALF], start=True, stop=True)
                    ins.then_inc(S["vt"], 1)
                    pe.wait_ge(S["qn"], 2 * b + 2)
                    for j in range(2):
                        ins = nc.tensor.matmul(PS[:, 4 + j, :], k["Wg"][:, :], xm[3][:, HALF * j:HALF * j + HALF], start=True, stop=True)
                    ins.then_inc(S["g"], 1)
                    pe.wait_ge(S["z"], b + 1)
                    for j in range(2):
                        ins = nc.tensor.matmul(PS[:, 6 + j, :], heads[:, :], qz[:, HALF * j:HALF * j + HALF], start=True, stop=True)
                    ins.then_inc(S["zb"], 1)
                    pe.wait_ge(S["diag"], b + 1)
                    pe.wait_ge(S["vsb"], 2 * b + 2)
                    for j in range(2):
                        ins = nc.tensor.matmul(PS[:, 2 + j, :], heads[:, :], qk[:, HALF * j:HALF * j + HALF], start=True, stop=True)
                    ins.then_inc(S["s"], 1)
                    pe.wait_ge(S["rz"], b + 1)
                    pe.wait_ge(S["kend"], b + 1)
                    pe.wait_ge(S["qin"], b + 1)
                    pe.wait_ge(S["dv"], b + 1)
                    pe.wait_ge(S["ktl"], NL * b + NL)
                    pe.wait_ge(S["qtl"], NL * b + NL)
                    pe.wait_ge(S["gsb"], b + 1)

                    def scores(n, hs_, name):
                        for l in range(NL):
                            for h in hs_:
                                r = slice(DH * h, DH * h + DH)
                                ins = nc.tensor.matmul(PS[:, h, 64 * l:64 * l + 64], ktl[r, l, P * n:P * n + P],
                                                       qtl[r, l, 64 * n:64 * n + 64], start=True, stop=True, skip_group_check=True)
                        ins.then_inc(S[name], 1)

                    def values(n, name):
                        dst = PS[:, 4 + n // 4, P * (n % 4):P * (n % 4) + P]
                        for l in range(NL):
                            b_ = LEVELS[l]
                            later = dst.rearrange("p (n s c) -> p n s c", s=2, c=b_)[:, :, 1, :]
                            for h in range(HEADS):
                                r = slice(DH * h, DH * h + DH)
                                ins = nc.tensor.matmul(later[r], v[:, n, r], pm[n % 2][:, h, 64 * l:64 * l + 64],
                                                       start=False, stop=False, skip_group_check=True)
                        ins.then_inc(S[name], 1)

                    def carried(n):
                        pe.wait_ge(S["state"], TILES * b + n + 1)
                        nc.tensor.matmul(PS[:, 4 + n // 4, P * (n % 4):P * (n % 4) + P], state[n % 2][:, :], qin[:, P * n:P * n + P],
                                         start=(n % 4 == 0), stop=False, skip_group_check=True).then_inc(S["inter"], 1)
                        if n < TILES - 1:
                            if n:
                                pe.wait_ge(S["ktsb"], (TILES - 1) * b + n)
                            nc.tensor.transpose(PS[:, 6, 0:P], kend[:, P * n:P * n + P], k["ident"][:, :]).then_inc(S["kt"], 1)
                            pe.wait_ge(S["ktsb"], (TILES - 1) * b + n + 1)
                            nc.tensor.matmul(PS[:, 7, 0:P], kendT[:, :], v[:, n, :], start=True, stop=True).then_inc(S["u"], 1)

                    A, B = (0, 1), (2, 3)
                    for n in range(TILES):
                        if n:
                            pe.wait_ge(S["maskA"], TILES * b + n)
                        scores(n, A, "scoreA")
                        if n:
                            pe.wait_ge(S["maskB"], TILES * b + n)
                        scores(n, B, "scoreB")
                        carried(n)
                        if n:
                            values(n - 1, "av")
                    pe.wait_ge(S["maskB"], TILES * b + TILES)
                    values(TILES - 1, "av")
                    pe.wait_ge(S["att"], b + 1)
                    for t in range(TILES):
                        ins = nc.tensor.matmul(PS[:, t // 4, P * (t % 4):P * (t % 4) + P], att[:, P * t:P * t + P], k["Wo"][:, :],
                                               start=True, stop=True, skip_group_check=True)
                    ins.then_inc(S["wo"], 1)

            @block.vector
            def _(dve):
                nc.vector.memset(hs[:, 0:1], 0.0)
                st0 = Steps(dve, S["dve"])
                st0.link(nc.vector.tensor_scalar(lnl[:, 0:1], k["time_decay"], 80.0, None, ALU.min))
                nc.vector.tensor_copy(um[:, 0:1], lnl[:, 0:1]).then_inc(S["lam"], 1)
                dve.wait_ge(S["lam"], 2)
                nc.vector.tensor_scalar(lnl[:, 0:1], lnl[:, 1:2], -1.0, -1e4, ALU.mult, ALU.max).then_inc(S["lam"], 1)
                dve.wait_ge(S["lam"], 4)
                dve.wait_ge(S["in"], 64)
                dve.wait_ge(S["ready"], 2)
                for b in passes(dve, BATCH):
                    st = Steps(dve, S["pool"], b, PER_AT)
                    normalise_stats(nc, dve, st, lambda t: H[:, b * TILES + t, :], stats, mean, sqm, var).then_inc(S["var"], 1)
                    dve.wait_ge(S["rstd"], b + 1)
                    for t in range(TILES):
                        ins = nc.vector.tensor_scalar(x[:, t, :], H[:, b * TILES + t, :], mean[:, t:t + 1], rstd[:, t:t + 1], ALU.subtract, ALU.mult)
                    st.link(ins)
                    normalise_stats(nc, dve, st, lambda t: x[:, t, :], stats, mean, sqm, var).then_inc(S["var2"], 1)
                    dve.wait_ge(S["rstd2"], b + 1)
                    for t in range(TILES):
                        ins = nc.vector.tensor_scalar(xn[:, t, :], x[:, t, :], mean[:, t:t + 1], rstd[:, t:t + 1], ALU.subtract, ALU.mult)
                    ins.then_inc(S["xn"], 1)
                    dve.wait_ge(S["hs"], 2 * b + 2)
                    st.link(nc.vector.tensor_tensor(diff, hs[:, 1:SEQ + 1], hs[:, 0:SEQ], ALU.subtract))
                    for j, n in enumerate(("tm_q", "tm_k", "tm_v", "tm_g")):
                        nc.vector.scalar_tensor_tensor(out=xm[j][:, :], in0=diff, scalar=k[n], in1=hs[:, 0:SEQ],
                                                       op0=ALU.mult, op1=ALU.add).then_inc(S["mix"], 1)
                    dve.wait_ge(S["ss"], b + 1)
                    nc.vector.tensor_scalar(ssv[:, :], PS[:, 4, 0:16], 1.0 / D, None, ALU.mult).then_inc(S["ssv"], 1)
                    dve.wait_ge(S["root"], b + 1)
                    st.link(nc.vector.tensor_scalar(root[:, :], root[:, :], 1e-8, None, ALU.add))
                    nc.vector.reciprocal(ssv[:, :], root[:, :]).then_inc(S["rms"], 1)
                    for j, a in enumerate((q, kk)):
                        dve.wait_ge(S["proj_sb"], 4 * b + 2 * j + 2)
                        dve.wait_ge(S["rb"], 2 * b + j + 1)
                        nc.vector.tensor_tensor(a[:, :], a[:, :], PS[:, 4 + 2 * j:6 + 2 * j, :].rearrange("p a b -> p (a b)"), ALU.mult).then_inc(S["qn"], 1)
                    dve.wait_ge(S["exp"], 2 * b + 2)
                    dve.wait_ge(S["vt"], b + 1)
                    st.link(nc.vector.tensor_tensor_scan(z[:, :], pw[:, 1:2].broadcast_to([P, SEQ]), kk[:, :], 0.0, ALU.mult, ALU.add))
                    nc.vector.tensor_tensor(qz[:, :], q[:, :], z[:, :], ALU.mult).then_inc(S["z"], 1)
                    for l, h in enumerate(LEVELS):
                        nb = SEQ // (2 * h)
                        right = q[:, :].rearrange("p (n s c) -> p n s c", s=2, c=h)[:, :, 1, :]
                        nc.vector.tensor_tensor(qtl[:, l, :].rearrange("p (n c) -> p n c", c=h), right,
                                                pw[:, 0:h].unsqueeze(1).broadcast_to([P, nb, h]), ALU.mult).then_inc(S["qtl"], 1)
                    nc.vector.tensor_tensor(qin[:, :].rearrange("p (n t) -> p n t", t=P), q[:, :].rearrange("p (n t) -> p n t", t=P),
                                            pw[:, 1:P + 1].unsqueeze(1).broadcast_to([P, TILES, P]), ALU.mult).then_inc(S["qin"], 1)
                    dve.wait_ge(S["g"], b + 1)
                    dve.wait_ge(S["zb"], b + 1)
                    nc.vector.reciprocal(rZ[:, :], PS[:, 6:8, :].rearrange("p a b -> p (a b)")).then_inc(S["rz"], 1)
                    dve.wait_ge(S["s"], b + 1)
                    nc.vector.tensor_tensor(dv[:, :], vT[:, :], PS[:, 2:4, :].rearrange("p a b -> p (a b)"), ALU.mult).then_inc(S["dv"], 1)
                    dve.wait_ge(S["gsb"], b + 1)
                    st.link(nc.vector.tensor_scalar(gT[:, :], gT[:, :], 0.5, 0.5, ALU.mult, ALU.add))
                    nc.vector.memset(state[0][:, :], 0.0).then_inc(S["state"], 1)
                    for n in range(TILES):
                        for name, lo, hi in (("A", 0, 2), ("B", 2, HEADS)):
                            dve.wait_ge(S["score" + name], TILES * b + n + 1)
                            if n >= 2:
                                dve.wait_ge(S["av"], TILES * b + n - 1)
                            nc.vector.tensor_tensor(pm[n % 2][:, lo:hi, :], PS[:, lo:hi, 0:NL * 64],
                                                    see[:, :].unsqueeze(1).broadcast_to([P, hi - lo, NL * 64]), ALU.mult).then_inc(S["mask" + name], 1)
                        if n < TILES - 1:
                            dve.wait_ge(S["u"], (TILES - 1) * b + n + 1)
                            st.link(nc.vector.tensor_tensor(um[:, :], PS[:, 7, 0:P], heads[:, :], ALU.mult))
                            dve.wait_ge(S["inter"], TILES * b + n + 1)
                            nc.vector.scalar_tensor_tensor(out=state[(n + 1) % 2][:, :], in0=state[n % 2][:, :], scalar=pw[:, P:P + 1],
                                                           in1=um[:, :], op0=ALU.mult, op1=ALU.add).then_inc(S["state"], 1)
                    dve.wait_ge(S["av"], TILES * b + TILES)
                    st.link(nc.vector.tensor_tensor(dv[:, :], dv[:, :], PS[:, 4:6, :].rearrange("p a b -> p (a b)"), ALU.add))
                    st.link(nc.vector.tensor_tensor(dv[:, :], dv[:, :], rZ[:, :], ALU.mult))
                    nc.vector.tensor_tensor(att[:, :], dv[:, :], gT[:, :], ALU.mult).then_inc(S["att"], 1)
                    dve.wait_ge(S["wo"], b + 1)
                    for j in range(2):
                        nc.vector.tensor_tensor(X2[:, bass.ds(b * TILES + 4 * j, 4), :], x[:, 4 * j:4 * j + 4, :],
                                                PS[:, j, :].rearrange("p (a b) -> p a b", a=4), ALU.add).then_inc(S["x2"], 1)
                    dve.wait_ge(S["x2"], 2 * b + 2)
                    st.close()


PER_AT = 20


BF16 = mybir.dt.bfloat16
EXPERTS, FF, CAP = 8, 512, 1024
NBLK = CAP // P
ROW = P + EXPERTS


def row_stats(nc, k, src, mean, rstd, tag):
    with ExitStack() as ctx:
        m = Mem(nc, ctx, tag, k["banks"])
        stats = m.sb("stats", [P, NT, 6])
        var, sq, expo = m.sb("var", [P, NT]), m.sb("sq", [P, NT]), m.sb("expo", [P, NT])
        s_stats, s_dve, s_var, s_out = m.sem("stats"), m.sem("dve"), m.sem("var"), m.sem("rstd")
        with nc.Block() as block:
            @block.vector
            def _(dve):
                nc.vector.memset(expo[:, :], -0.5)
                with dve.Fori(0, NT // 4) as i:
                    for t in range(4):
                        ins = nc.vector.bn_stats(stats[:, i * 4 + t, :], src[:, i * 4 + t, :])
                    ins.then_inc(s_stats, 1)
                dve.wait_ge(s_stats, NT // 4)
                merge_stats(nc, Steps(dve, s_dve), stats[:, :, :], mean[:, :], sq[:, :], var[:, :]).then_inc(s_var, 1)

            @block.gpsimd
            def _(pool):
                pool.wait_ge(s_var, 1)
                nc.gpsimd.tensor_tensor(rstd[:, :], var[:, :], expo[:, :], ALU.pow).then_inc(s_out, 1)


def mlp(nc, w, k, H, X2, mean, rstd):
    with ExitStack() as ctx:
        m = Mem(nc, ctx, "mlp", k["banks"])
        xn = [m.sb(f"xn{u}", [P, 4, P]) for u in range(2)]
        hT = [m.sb(f"hT{u}", [P, HALF]) for u in range(2)]
        hid = [m.sb(f"hid{u}", [P, 4, HALF]) for u in range(2)]
        pt = [m.ps() for u in range(2)]
        pf = [m.ps() for f in range(4)]
        po = [m.ps((P, 4, P)) for u in range(2)]
        two = lambda n: [m.sem(f"{n}{u}") for u in range(2)]
        s_xn, s_turned, s_h, s_up, s_gelu, s_down, s_out = (two(n) for n in ("xn", "turned", "h", "up", "gelu", "down", "out"))
        s_dve = m.sem("dve")
        reset_used(nc)
        G = NT // 4
        with nc.Block() as block:
            @block.vector
            def _(dve):
                for i in passes(dve, G // 2):
                    st = Steps(dve, s_dve, i, 2)
                    for u in range(2):
                        dve.wait_ge(s_turned[u], i)
                        for t in range(4):
                            n = (i * 2 + u) * 4 + t
                            ins = nc.vector.tensor_scalar(xn[u][:, t, :], X2[:, n, :], mean[:, bass.ds(n, 1)], rstd[:, bass.ds(n, 1)],
                                                          ALU.subtract, ALU.mult)
                        ins.then_inc(s_xn[u], 1)
                    for u in range(2):
                        g = bass.ds((i * 2 + u) * 4, 4)
                        st.link(nc.vector.tensor_tensor(H[:, g, :], H[:, g, :], X2[:, g, :], ALU.add))
                        dve.wait_ge(s_down[u], i + 1)
                        nc.vector.tensor_tensor(H[:, g, :], H[:, g, :], po[u][:, :, :], ALU.add).then_inc(s_out[u], 1)
                    st.close()

            @block.scalar
            def _(act):
                for i in passes(act, G // 2):
                    for u in range(2):
                        act.wait_ge(s_turned[u], i + 1)
                        act.wait_ge(s_up[u], 4 * i)
                        nc.scalar.activation(hT[u][:, :], pt[u][:, :], ACT.Identity, bias=k["ln2_b"], scale=k["ln2_g"]).then_inc(s_h[u], 1)
                    for u in range(2):
                        act.wait_ge(s_down[u], i)
                        for f in range(4):
                            act.wait_ge(s_up[u], 4 * i + f + 1)
                            nc.scalar.activation(hid[u][:, f, :], pf[f][:, :], ACT.Gelu).then_inc(s_gelu[u], 1)

            @block.tensor
            def _(pe):
                for i in passes(pe, G // 2):
                    for u in range(2):
                        pe.wait_ge(s_xn[u], i + 1)
                        pe.wait_ge(s_h[u], i)
                        for t in range(4):
                            ins = nc.tensor.transpose(pt[u][:, P * t:P * t + P], xn[u][:, t, :], k["ident"][:, :])
                        ins.then_inc(s_turned[u], 1)
                    for u in range(2):
                        pe.wait_ge(s_h[u], i + 1)
                        for f in range(4):
                            pe.wait_ge(s_gelu[1 - u], 4 * i + f + 1 if u else 4 * i)
                            nc.tensor.matmul(pf[f][:, :], k["W1T"][:, P * f:P * f + P], hT[u][:, :], start=True, stop=True).then_inc(s_up[u], 1)
                    for u in range(2):
                        pe.wait_ge(s_gelu[u], 4 * i + 4)
                        pe.wait_ge(s_out[u], i)
                        for t in range(4):
                            for f in range(4):
                                ins = nc.tensor.matmul(po[u][:, t, :], hid[u][:, f, P * t:P * t + P], k["W2T"][:, f, :],
                                                       start=(f == 0), stop=(f == 3), skip_group_check=True)
                        ins.then_inc(s_down[u], 1)


def moe_tables():
    tri = np.triu(np.ones((P, P), np.float32), 1)
    nt = np.zeros((P, 2 * NT), np.float32)
    nt[:, 0:NT] = np.arange(NT)
    nt[:, NT:] = np.arange(P)[:, None]
    io = np.zeros((P, P), np.float32) + np.arange(P, dtype=np.float32)
    return {"c_before": tri, "c_ids": nt, "c_iota": io}


def moe_route(nc, w, k, H, mean, rstd, rows, acc, lists):
    with ExitStack() as ctx:
        m = Mem(nc, ctx, "rt", k["banks"])
        Wr = m.sb("Wr", [P, EXPERTS])
        before, ids, iota = m.sb("before", [P, P]), m.sb("ids", [P, 2 * NT]), m.sb("iota", [P, P])
        xn = [m.sb(f"xn{u}", [P, 4, P]) for u in range(2)]
        xT = [m.sb(f"xT{u}", [P, HALF]) for u in range(2)]
        E8 = lambda n, dt=F32: m.sb(n, [P, EXPERTS], dt)
        EN = lambda n, dt=F32: m.sb(n, [P, EXPERTS, NT], dt)
        lg, below, mask, eq, pref, tot = EN("lg"), EN("below"), EN("mask"), EN("eq"), EN("pref"), EN("tot")
        expo, prob = EN("expo"), m.sb("prob", [P, NT, EXPERTS])
        part, blk = EN("part"), EN("blk")
        posi, parti, blki = EN("posi", I32), EN("parti", I32), EN("blki", I32)
        mx, cnt, rs, need = E8("mx"), E8("cnt"), E8("rs"), E8("need")
        mx8, dg = m.sb("mx8", [EXPERTS, 1]), m.sb("dg", [EXPERTS, EXPERTS])
        thr, cand, bit, take = E8("thr", I32), E8("cand", I32), E8("bit", I32), E8("take", I32)
        onep = [m.sb(f"onep{u}", [P, 8, P], BF16) for u in range(2)]
        oneb = m.sb("oneb", [P, NT, 8])
        rhs = m.sb("rhs", [P, NT, 16], BF16)
        half_id = m.sb("half_id", [P, 16])
        idf = m.sb("idf", [P, 8])
        pt = [m.ps() for u in range(2)]
        pl = [m.ps((P, 4, EXPERTS)) for u in range(2)]
        pa, pb, pc, pd = m.ps(), m.ps(), m.ps(), m.ps()
        two = lambda n: [m.sem(f"{n}{u}") for u in range(2)]
        s_xn, s_turned, s_xT, s_lg, s_lgc, s_row = (two(n) for n in ("xn", "turned", "xT", "lg", "lgc", "row"))
        s_in, s_pe, s_dve, s_act, s_acc, s_dve2, s_cnt, s_mask, s_list, s_listc, s_dve3 = (m.sem(n) for n in (
            "in", "pe", "dve", "act", "acc", "dve2", "cnt", "mask", "list", "listc", "dve3"))
        s_dve3b, s_dve4 = m.sem("dve3b"), m.sem("dve4")
        s_onep = two("onep")
        s_oused = two("oused")
        G = NT // 4
        rows_v = rows.rearrange("(n p) c -> p n c", p=P)
        acc_v = acc.rearrange("(n p) c -> p n c", p=P)
        with nc.Block() as block:
            @block.sync
            def _(sp):
                for dst, src in ((Wr, "L0_ffn_Wr"), (before, "c_before"), (ids, "c_ids"), (iota, "c_iota")):
                    sp.dma_start(dst[:, :], w[src]).then_inc(s_in, 16)
                sp.dma_start(acc_v, H[:, :, :]).then_inc(s_acc, 16)
                for i in passes(sp, G // 2):
                    for u in range(2):
                        sp.wait_ge(s_xn[u], i + 1)
                        sp.dma_start(rows_v[:, bass.ds((i * 2 + u) * 4, 4), 0:P], xn[u][:, :, :]).then_inc(s_row[u], 16)
                for u in range(2):
                    sp.wait_ge(s_row[u], 16 * G // 2)
                sp.wait_ge(s_acc, 16)
                sp.wait_ge(s_in, 64)

            @block.vector
            def _(dve):
                for i in passes(dve, G // 2):
                    for u in range(2):
                        dve.wait_ge(s_turned[u], i)
                        dve.wait_ge(s_row[u], 16 * i)
                        for t in range(4):
                            n = (i * 2 + u) * 4 + t
                            ins = nc.vector.tensor_scalar(xn[u][:, t, :], H[:, n, :], mean[:, bass.ds(n, 1)], rstd[:, bass.ds(n, 1)],
                                                          ALU.subtract, ALU.mult)
                        ins.then_inc(s_xn[u], 1)
                    for u in range(2):
                        dve.wait_ge(s_lg[u], i + 1)
                        nc.vector.tensor_copy(lg[:, :, bass.ds((i * 2 + u) * 4, 4)], pl[u][:, :, :].rearrange("p t e -> p e t")).then_inc(s_lgc[u], 1)

            @block.scalar
            def _(act):
                for i in passes(act, G // 2):
                    for u in range(2):
                        act.wait_ge(s_turned[u], i + 1)
                        act.wait_ge(s_lg[u], i)
                        nc.scalar.copy(xT[u][:, :], pt[u][:, :]).then_inc(s_xT[u], 1)

            @block.tensor
            def _(pe):
                pe.wait_ge(s_in, 64)
                for i in passes(pe, G // 2):
                    for u in range(2):
                        pe.wait_ge(s_xn[u], i + 1)
                        pe.wait_ge(s_xT[u], i)
                        for t in range(4):
                            ins = nc.tensor.transpose(pt[u][:, P * t:P * t + P], xn[u][:, t, :], k["ident"][:, :])
                        ins.then_inc(s_turned[u], 1)
                    for u in range(2):
                        pe.wait_ge(s_xT[u], i + 1)
                        pe.wait_ge(s_lgc[u], i)
                        for t in range(4):
                            ins = nc.tensor.matmul(pl[u][:, t, :], xT[u][:, P * t:P * t + P], Wr[:, :], start=True, stop=True, skip_group_check=True)
                        ins.then_inc(s_lg[u], 1)
        flat = lambda t: t[:, :, :].rearrange("p a b -> p (a b)")
        ROUNDS = 31
        with nc.Block() as block:
            @block.tensor
            def _(pe):
                pe.wait_ge(s_dve, 1)
                nc.tensor.transpose(pa[0:EXPERTS, 0:P], mx[:, :], k["ident"][:, :]).then_inc(s_pe, 1)
                pe.wait_ge(s_dve, 3)
                nc.tensor.matmul(pb[:, 0:EXPERTS], k["ones"][0:EXPERTS, :], dg[:, :], start=True, stop=True).then_inc(s_pe, 1)
                pe.wait_ge(s_dve, 5)
                nc.tensor.matmul(pa[:, 0:EXPERTS], k["ones"][:, :], cnt[:, :], start=True, stop=True).then_inc(s_pe, 1)
                with pe.Fori(0, ROUNDS) as r:
                    pe.wait_ge(s_cnt, r + 1)
                    nc.tensor.matmul(pb[:, 0:EXPERTS], k["ones"][:, :], cnt[:, :], start=True, stop=True).then_inc(s_mask, 1)
                pe.wait_ge(s_dve2, 1)
                nc.tensor.matmul(pa[:, 0:EXPERTS], k["ones"][:, :], cnt[:, :], start=True, stop=True)
                nc.tensor.matmul(pc[:, :], before[:, :], flat(eq), start=True, stop=True)
                nc.tensor.matmul(pd[:, :], k["ones"][:, :], flat(eq), start=True, stop=True).then_inc(s_pe, 1)
                pe.wait_ge(s_dve2, 3)
                nc.tensor.matmul(pa[:, :], before[:, :], flat(mask), start=True, stop=True)
                nc.tensor.matmul(pb[:, :], k["ones"][:, :], flat(mask), start=True, stop=True).then_inc(s_pe, 1)

            @block.scalar
            def _(act):
                act.wait_ge(s_dve, 4)
                nc.scalar.activation(flat(expo), flat(below), ACT.Exp, scale=-1.0).then_inc(s_act, 1)

            @block.vector
            def _(dve):
                st = Steps(dve, s_dve)
                st.link(nc.vector.tensor_reduce(mx[:, :], lg[:, :, :], AX.X, ALU.max))
                dve.wait_ge(s_pe, 1)
                st.link(nc.vector.tensor_reduce(mx8[:, :], pa[0:EXPERTS, 0:P], AX.X, ALU.max))
                st.link(nc.vector.tensor_scalar(dg[:, :], k["ident"][0:EXPERTS, 0:EXPERTS], mx8[:, 0:1], None, ALU.mult))
                dve.wait_ge(s_pe, 2)
                nc.vector.tensor_copy(mx[:, :], pb[:, 0:EXPERTS]).then_inc(s_dve3, 1)
                dve.wait_ge(s_dve3, 1)
                st.link(nc.vector.tensor_tensor(below[:, :, :], spread(mx[:, :], NT), lg[:, :, :], ALU.subtract))
                dve.wait_ge(s_act, 1)
                st.link(nc.vector.tensor_reduce(cnt[:, :], expo[:, :, :], AX.X, ALU.add))
                dve.wait_ge(s_pe, 3)
                st.link(nc.vector.reciprocal(rs[:, :], pa[:, 0:EXPERTS]))
                st.link(nc.vector.tensor_tensor(prob[:, :, :], expo[:, :, :].rearrange("p e t -> p t e"),
                                                rs[:, :].unsqueeze(1).broadcast_to([P, NT, EXPERTS]), ALU.mult))
                nc.vector.memset(lists[:, EXPERTS, :], 0)
                nc.vector.memset(thr[:, :], 0)
                st.link(nc.vector.memset(bit[:, :], 1 << 30))
                st.link(nc.vector.tensor_tensor(cand[:, :], thr[:, :], bit[:, :], ALU.bitwise_or))
                with dve.Fori(0, ROUNDS) as r:
                    s2 = Steps(dve, s_dve3b, r, 5)
                    s2.link(nc.vector.tensor_tensor(mask[:, :, :], below[:, :, :], spread(cand[:, :].bitcast(F32), NT), ALU.is_lt))
                    nc.vector.tensor_reduce(cnt[:, :], mask[:, :, :], AX.X, ALU.add).then_inc(s_cnt, 1)
                    dve.wait_ge(s_mask, r + 1)
                    s2.link(nc.vector.scalar_tensor_tensor(out=take[:, :], in0=pb[:, 0:EXPERTS], scalar=float(CAP), in1=bit[:, :],
                                                           op0=ALU.is_lt, op1=ALU.mult))
                    s2.link(nc.vector.tensor_tensor(thr[:, :], thr[:, :], take[:, :], ALU.bitwise_or))
                    s2.link(nc.vector.tensor_scalar(bit[:, :], bit[:, :], 1, None, ALU.logical_shift_right))
                    s2.link(nc.vector.tensor_tensor(cand[:, :], thr[:, :], bit[:, :], ALU.bitwise_or))
                    s2.close()
                T = spread(thr[:, :].bitcast(F32), NT)
                nc.vector.tensor_tensor(eq[:, :, :], below[:, :, :], T, ALU.is_equal)
                st.link(nc.vector.tensor_tensor(mask[:, :, :], below[:, :, :], T, ALU.is_lt))
                nc.vector.tensor_reduce(cnt[:, :], mask[:, :, :], AX.X, ALU.add).then_inc(s_dve2, 1)
                dve.wait_ge(s_pe, 4)
                nc.vector.tensor_scalar(need[:, :], pa[:, 0:EXPERTS], -1.0, float(CAP), ALU.mult, ALU.add)

                def ahead(within, whole):
                    st.link(nc.vector.tensor_copy(flat(tot), whole))
                    for e in range(EXPERTS):
                        ins = nc.vector.tensor_tensor_scan(pref[:, e, :], k["ones"][:, 0:1].broadcast_to([P, NT]), tot[:, e, :], 0.0, ALU.mult, ALU.add)
                    st.link(ins)
                    st.link(nc.vector.tensor_tensor(flat(pref), flat(pref), flat(tot), ALU.subtract))
                    st.link(nc.vector.tensor_tensor(flat(pref), flat(pref), within, ALU.add))

                ahead(pc[:, :], pd[:, :])
                st.link(nc.vector.tensor_tensor(pref[:, :, :], pref[:, :, :], spread(need[:, :], NT), ALU.is_lt))
                st.link(nc.vector.tensor_tensor(eq[:, :, :], eq[:, :, :], pref[:, :, :], ALU.mult))
                nc.vector.tensor_copy(idf[:, :], need[:, :]).then_inc(s_dve2, 1)
                nc.vector.tensor_tensor(mask[:, :, :], mask[:, :, :], eq[:, :, :], ALU.add).then_inc(s_dve2, 1)
                dve.wait_ge(s_pe, 5)
                ahead(pa[:, :], pb[:, :])
                st.link(nc.vector.tensor_scalar(flat(eq), flat(mask), -65536.0, 65536.0, ALU.mult, ALU.add))
                st.link(nc.vector.tensor_tensor(flat(posi), flat(pref), flat(eq), ALU.add))
                nc.vector.tensor_scalar(flat(parti), flat(posi), P - 1, None, ALU.bitwise_and)
                st.link(nc.vector.tensor_scalar(flat(blki), flat(posi), 7, None, ALU.logical_shift_right))
                nc.vector.tensor_copy(flat(part), flat(parti))
                st.link(nc.vector.tensor_copy(flat(blk), flat(blki)))

            @block.sync
            def _(sp):
                sp.wait_ge(s_dve, 7)
                sp.dma_start(rows_v[:, :, P:ROW], prob[:, :, :]).then_inc(s_in, 16)
                sp.wait_ge(s_in, 80)
        with nc.Block() as block:
            @block.vector
            def _(dve):
                for e in passes(dve, EXPERTS):
                    st = Steps(dve, s_dve4, e, 4)
                    st.link(nc.vector.tensor_tensor(oneb[:, :, :], iota[:, 0:8].unsqueeze(1).broadcast_to([P, NT, 8]),
                                                    spread(blk[:, e, :], 8), ALU.is_equal))
                    dve.wait_ge(s_list, e)
                    nc.vector.tensor_tensor(rhs[:, :, 0:8], oneb[:, :, :], spread(ids[:, 0:NT], 8), ALU.mult)
                    st.link(nc.vector.tensor_tensor(rhs[:, :, 8:16], oneb[:, :, :], spread(ids[:, NT:2 * NT], 8), ALU.mult))
                    for c in range(NT // 8):
                        dve.wait_ge(s_oused[c % 2], 4 * e + c // 2)
                        nc.vector.tensor_tensor(onep[c % 2][:, :, :], iota[:, :].unsqueeze(1).broadcast_to([P, 8, P]),
                                                spread(part[:, e, bass.ds(8 * c, 8)], P), ALU.is_equal).then_inc(s_onep[c % 2], 1)
                    dve.wait_ge(s_list, e + 1)
                    st.link(nc.vector.tensor_copy(half_id[:, :], pa[:, 0:16]))
                    st.link(nc.vector.scalar_tensor_tensor(out=lists[:, e, :], in0=half_id[:, 0:8], scalar=float(P), in1=half_id[:, 8:16],
                                                           op0=ALU.mult, op1=ALU.add))
                    st.close()

            @block.tensor
            def _(pe):
                for e in passes(pe, EXPERTS):
                    pe.wait_ge(s_dve4, 4 * e + 2)
                    for c in range(NT // 8):
                        pe.wait_ge(s_onep[c % 2], 4 * e + c // 2 + 1)
                        for t in range(8):
                            n = 8 * c + t
                            ins = nc.tensor.matmul(pa[:, 0:16], onep[c % 2][:, t, :], rhs[:, n, :], start=(n == 0), stop=(n == NT - 1))
                        if c < NT // 8 - 1:
                            ins.then_inc(s_oused[c % 2], 1)
                    ins.then_inc(s_oused[(NT // 8 - 1) % 2], 1)
                    nc.tensor.matmul(pb[0:1, 0:1], rhs[:, 0, 0:1], rhs[:, 0, 0:1], start=True, stop=True).then_inc(s_list, 1)


def moe_experts(nc, w, k, rows, acc, lists):
    with ExitStack() as ctx:
        m = Mem(nc, ctx, "ex", k["banks"])
        two = lambda n: [m.sem(f"{n}{u}") for u in range(2)]
        W1 = [m.sb(f"W1{u}", [P, FF]) for u in range(2)]
        W2 = [m.sb(f"W2{u}", [P, 4, D]) for u in range(2)]
        bs = [m.sb(f"bs{u}", [P, 4]) for u in range(2)]
        b1r, b1 = m.sb("b1r", [EXPERTS * 4, P]), m.sb("b1", [P, EXPERTS * 4])
        b2 = [m.sb(f"b2{u}", [1, D]) for u in range(2)]
        idx = [m.sb(f"idx{u}", [P, NBLK], U32) for u in range(2)]
        sel = [m.sb(f"sel{u}", [P, NBLK, ROW]) for u in range(2)]
        selT = [m.sb(f"selT{u}", [P, HALF]) for u in range(2)]
        hid = [m.sb(f"hid{u}", [P, 4, HALF]) for u in range(2)]
        y = [m.sb(f"y{u}", [P, NBLK, D]) for u in range(2)]
        wt = [m.sb(f"wt{u}", [P, NBLK]) for u in range(2)]
        pt = [m.ps() for u in range(2)]
        pf = [m.ps() for f in range(4)]
        po = [m.ps((P, 4, P)) for u in range(2)]
        s_w, s_idx, s_gather, s_used, s_y, s_scatter, s_down_e = (two(n) for n in ("w", "idx", "gather", "used", "y", "scatter", "down_e"))
        s_turned, s_selT, s_up, s_gelu, s_down, s_out = (two(n) for n in ("turned", "selT", "up", "gelu", "down", "out"))
        s_wt = two("wt")
        W1_d, W2_d = w["L0_ffn_W1"], w["L0_ffn_W2"]
        s_b1 = m.sem("b1")
        with nc.Block() as block:
            @block.sync
            def _(sp):
                sp.dma_start(b1r[:, :], w["L0_ffn_b1"].rearrange("e (f p) -> (e f) p", p=P)).then_inc(s_b1, 16)

            @block.tensor
            def _(pe):
                pe.wait_ge(s_b1, 16)
                nc.tensor.transpose(pt[0][:, 0:EXPERTS * 4], b1r[:, :], k["ident"][0:EXPERTS * 4, 0:EXPERTS * 4]).then_inc(s_b1, 1)

            @block.vector
            def _(dve):
                dve.wait_ge(s_b1, 17)
                nc.vector.tensor_copy(b1[:, :], pt[0][:, 0:EXPERTS * 4]).then_inc(s_b1, 1)
        with nc.Block() as block:
            @block.sync
            def _(sp):
                for i in passes(sp, EXPERTS // 2):
                    for u in range(2):
                        e = bass.ds(i * 2 + u, 1)
                        sp.wait_ge(s_down_e[u], i)
                        sp.dma_start(W1[u][:, :], W1_d[e].rearrange("a d f -> (a d) f")).then_inc(s_w[u], 16)
                        sp.dma_start(W2[u][:, :, :], W2_d[e].rearrange("a (f p) d -> p (a f) d", p=P)).then_inc(s_w[u], 16)
                        sp.dma_start(b2[u][:, :], w["L0_ffn_b2"][e, :]).then_inc(s_w[u], 16)
                for u in range(2):
                    sp.wait_ge(s_w[u], 48 * EXPERTS // 2)

            @block.gpsimd
            def _(pool):
                def gather(u, n):
                    pool.wait_ge(s_idx[u], n + 1)
                    for c in range(NBLK):
                        nc.gpsimd.indirect_dma_start(sel[u][:, c, :], None, rows, bass.IndirectOffsetOnAxis(ap=idx[u][:, c:c + 1], axis=0)
                                                     ).then_inc(s_gather[u], 16)

                gather(0, 0)
                for i in range(EXPERTS // 2):
                    gather(1, i)
                    for u in range(2):
                        pool.wait_ge(s_y[u], i + 1)
                        if u:
                            pool.wait_ge(s_scatter[0], 16 * NBLK * (i + 1))
                        elif i:
                            pool.wait_ge(s_scatter[1], 16 * NBLK * i)
                        for c in range(NBLK):
                            nc.gpsimd.indirect_dma_start(acc, bass.IndirectOffsetOnAxis(ap=idx[u][:, c:c + 1], axis=0), y[u][:, c, :], None,
                                                         compute_op=ALU.add).then_inc(s_scatter[u], 16)
                        if u == 0 and i < EXPERTS // 2 - 1:
                            gather(0, i + 1)
                pool.wait_ge(s_scatter[1], 16 * NBLK * EXPERTS // 2)

            @block.vector
            def _(dve):
                nc.vector.tensor_copy(idx[0][:, :], lists[:, 0, :]).then_inc(s_idx[0], 1)
                for i in passes(dve, EXPERTS // 2):
                    dve.wait_ge(s_scatter[1], 16 * NBLK * i)
                    nc.vector.tensor_copy(idx[1][:, :], lists[:, i * 2 + 1, :]).then_inc(s_idx[1], 1)
                    for u in range(2):
                        dve.wait_ge(s_gather[u], 16 * NBLK * (i + 1))
                        dve.wait_ge(s_scatter[u], 16 * NBLK * i)
                        nc.vector.tensor_copy(bs[u][:, :], b1[:, bass.ds((i * 2 + u) * 4, 4)])
                        nc.vector.tensor_copy(wt[u][:, :], sel[u][:, :, bass.ds(i * 2 + (P + u), 1)].rearrange("p a b -> p (a b)")).then_inc(s_wt[u], 1)
                        dve.wait_ge(s_wt[u], i + 1)
                        for h in range(2):
                            dve.wait_ge(s_down[h], 2 * i + u + 1)
                            for t in range(4):
                                c = 4 * h + t
                                ins = nc.vector.tensor_scalar(y[u][:, c, :], po[h][:, t, :], wt[u][:, c:c + 1], None, ALU.mult)
                            ins.then_inc(s_out[h], 1)
                        dve.wait_ge(s_out[1], 2 * i + u + 1)
                        nc.vector.tensor_copy(y[u][0:1, 0, 0:1], y[u][0:1, 0, 0:1]).then_inc(s_y[u], 1)
                        if u == 0:
                            dve.wait_ge(s_scatter[0], 16 * NBLK * (i + 1))
                            nc.vector.tensor_copy(idx[0][:, :], lists[:, NEXT(i), :]).then_inc(s_idx[0], 1)

            @block.scalar
            def _(act):
                for i in passes(act, EXPERTS // 2):
                    for u in range(2):
                        for h in range(2):
                            act.wait_ge(s_turned[h], 2 * i + u + 1)
                            act.wait_ge(s_up[h], 4 * (2 * i + u))
                            nc.scalar.copy(selT[h][:, :], pt[h][:, :]).then_inc(s_selT[h], 1)
                        act.wait_ge(s_wt[u], i + 1)
                        for h in range(2):
                            act.wait_ge(s_down[h], 2 * i + u)
                            for f in range(4):
                                act.wait_ge(s_up[h], 4 * (2 * i + u) + f + 1)
                                nc.scalar.activation(hid[h][:, f, :], pf[f][:, :], ACT.Gelu, bias=bs[u][:, f:f + 1]).then_inc(s_gelu[h], 1)

            @block.tensor
            def _(pe):
                for i in passes(pe, EXPERTS // 2):
                    for u in range(2):
                        n = 2 * i + u
                        pe.wait_ge(s_gather[u], 16 * NBLK * (i + 1))
                        pe.wait_ge(s_w[u], 48 * (i + 1))
                        for h in range(2):
                            pe.wait_ge(s_selT[h], n)
                            for t in range(4):
                                ins = nc.tensor.transpose(pt[h][:, P * t:P * t + P], sel[u][:, 4 * h + t, 0:P], k["ident"][:, :])
                            ins.then_inc(s_turned[h], 1)
                        for h in range(2):
                            pe.wait_ge(s_selT[h], n + 1)
                            for f in range(4):
                                pe.wait_ge(s_gelu[1 - h], 4 * n + f + 1 if h else 4 * n)
                                nc.tensor.matmul(pf[f][:, :], W1[u][:, P * f:P * f + P], selT[h][:, :], start=True, stop=True).then_inc(s_up[h], 1)
                        for h in range(2):
                            pe.wait_ge(s_gelu[h], 4 * n + 4)
                            pe.wait_ge(s_out[h], n)
                            for t in range(4):
                                for f in range(4):
                                    nc.tensor.matmul(po[h][:, t, :], hid[h][:, f, P * t:P * t + P], W2[u][:, f, :],
                                                     start=(f == 0), stop=False, skip_group_check=True)
                                ins = nc.tensor.matmul(po[h][:, t, :], k["ones"][0:1, :], b2[u][:, :], start=False, stop=True, skip_group_check=True)
                            ins.then_inc(s_down[h], 1)
                        nc.tensor.matmul(pt[1][0:1, 0:1], k["ones"][0:1, 0:1], k["ones"][0:1, 0:1], start=True, stop=True).then_inc(s_down_e[u], 1)


def NEXT(i):
    return i * 2 + 2


def reload(nc, H, acc):
    with ExitStack() as ctx:
        m = Mem(nc, ctx, "rl")
        s = m.sem("in")
        with nc.Block() as block:
            @block.sync
            def _(sp):
                sp.dma_start(H[:, :, :], acc.rearrange("(n p) c -> p n c", p=P)).then_inc(s, 16)
                sp.wait_ge(s, 16)


TAPS, LORA, FEXP = BATCH, 16, 4


def ffn(nc, w, k, H, mean, rstd, out):
    with ExitStack() as ctx:
        m = Mem(nc, ctx, "ff", k["banks"])
        two = lambda n: [m.sem(f"{n}{u}") for u in range(2)]
        ER = FEXP * LORA
        raw = m.sb("raw", [P, 6, P])
        gw = m.sb("gw", [P, FEXP + 1])
        A = m.sb("A", [P, FEXP, LORA])
        BT, fc2T = m.sb("BT", [P, ER]), m.sb("fc2T", [P, FEXP, P])
        M = m.sb("M", [2 * ER, 2 * D])
        spreadM = [m.sb(f"BTe{e}", [P, 2 * ER]) for e in range(FEXP)]
        xn = [m.sb(f"xn{u}", [P, 4, P]) for u in range(2)]
        xT = [m.sb(f"xT{u}", [P, HALF]) for u in range(2)]
        hid = [m.sb(f"hid{u}", [P, FEXP, HALF]) for u in range(2)]
        lg = [m.sb(f"lg{u}", [P, 4, 8]) for u in range(2)]
        ex = [m.sb(f"ex{u}", [P, 4, FEXP]) for u in range(2)]
        sg = [m.sb(f"sg{u}", [P, 4]) for u in range(2)]
        t4 = [m.sb(f"t4{u}", [P, 4]) for u in range(2)]
        wl = [m.sb(f"wl{u}", [P, 4, ER]) for u in range(2)]
        wlT = [m.sb(f"wlT{u}", [P, 2 * P]) for u in range(2)]
        yo = [m.sb(f"yo{u}", [P, 4, D]) for u in range(2)]
        pt = [m.ps() for u in range(2)]
        pf = [m.ps() for e in range(2)]
        pl = [m.ps((P, 4, P)) for u in range(2)]
        po = [m.ps((P, 4, D)) for u in range(2)]
        s_in, s_t, s_tc, s_dve = m.sem("in"), m.sem("t"), m.sem("tc"), m.sem("dve")
        (s_xn, s_turned, s_xT, s_fc1, s_hid, s_low, s_lowc, s_exp, s_wl, s_wlt, s_wlT, s_o, s_y, s_store) = (two(n) for n in (
            "xn", "turned", "xT", "fc1", "hid", "low", "lowc", "exp", "wl", "wlt", "wlT", "o", "y", "store"))
        G = NT // 4
        out_v = out.rearrange("b (t p) d -> p (b t) d", p=P)
        with nc.Block() as block:
            @block.sync
            def _(sp):
                for e in range(FEXP):
                    sp.dma_start(raw[:, e, :], w["L1_ffn_fc2_w"][e]).then_inc(s_in, 16)
                sp.dma_start(raw[0:ER, 4, :], w["L1_ffn_lora_B"].rearrange("e r o -> (e r) o")).then_inc(s_in, 16)
                sp.dma_start(raw[0:FEXP, 5, :], w["L1_ffn_gate_w"]).then_inc(s_in, 16)
                sp.dma_start(raw[FEXP:FEXP + 1, 5, :], w["L1_ffn_thr_w"]).then_inc(s_in, 16)
                sp.dma_start(A[:, :, :], w["L1_ffn_lora_A"].rearrange("e h r -> h e r")).then_inc(s_in, 16)
                sp.wait_ge(s_in, 128)

            @block.tensor
            def _(pe):
                pe.wait_ge(s_in, 128)
                for e in range(FEXP):
                    nc.tensor.transpose(pt[0][:, P * e:P * e + P], raw[:, e, :], k["ident"][:, :])
                nc.tensor.transpose(pt[1][:, 0:ER], raw[0:ER, 4, :], k["ident"][0:ER, 0:ER])
                nc.tensor.transpose(pt[1][:, P:P + FEXP + 1], raw[0:FEXP + 1, 5, :], k["ident"][0:FEXP + 1, 0:FEXP + 1]).then_inc(s_t, 1)
                pe.wait_ge(s_tc, 8 + FEXP)
                for e in range(FEXP):
                    ins = nc.tensor.matmul(po[0][0:2 * ER, 0, :], spreadM[e][:, :], fc2T[:, e, :], start=(e == 0), stop=(e == FEXP - 1))
                ins.then_inc(s_t, 1)

            @block.vector
            def _(dve):
                for e in range(FEXP):
                    nc.vector.memset(spreadM[e][:, :], 0.0).then_inc(s_tc, 1)
                nc.vector.memset(M[:, :], 0.0).then_inc(s_tc, 1)
                dve.wait_ge(s_tc, FEXP + 1)
                dve.wait_ge(s_t, 1)
                nc.vector.tensor_copy(fc2T[:, :, :].rearrange("p a b -> p (a b)"), pt[0][:, :]).then_inc(s_tc, 1)
                nc.vector.tensor_copy(BT[:, :], pt[1][:, 0:ER]).then_inc(s_tc, 1)
                nc.vector.tensor_copy(gw[:, :], pt[1][:, P:P + FEXP + 1]).then_inc(s_tc, 1)
                for e in range(FEXP):
                    r = slice(LORA * e, LORA * e + LORA)
                    nc.vector.tensor_copy(spreadM[e][:, r], pt[1][:, r])
                    nc.vector.tensor_copy(spreadM[e][:, ER + LORA * e:ER + LORA * e + LORA], pt[1][:, r]).then_inc(s_tc, 1)
                dve.wait_ge(s_t, 2)
                nc.vector.tensor_copy(M[0:ER, 0:D], po[0][0:ER, 0, :])
                nc.vector.tensor_copy(M[ER:2 * ER, D:2 * D], po[0][ER:2 * ER, 0, :]).then_inc(s_tc, 1)
        with nc.Block() as block:
            @block.vector
            def _(dve):
                for i in passes(dve, G // 2):
                    st = Steps(dve, s_dve, i, 24)
                    for u in range(2):
                        dve.wait_ge(s_turned[u], i)
                        for t in range(4):
                            n = (i * 2 + u) * 4 + t
                            ins = nc.vector.tensor_scalar(xn[u][:, t, :], H[:, n, :], mean[:, bass.ds(n, 1)], rstd[:, bass.ds(n, 1)],
                                                          ALU.subtract, ALU.mult)
                        ins.then_inc(s_xn[u], 1)
                    for u in range(2):
                        dve.wait_ge(s_low[u], i + 1)
                        nc.vector.tensor_copy(wl[u][:, :, :], pl[u][:, :, 0:ER])
                        st.link(nc.vector.tensor_copy(lg[u][:, :, 0:FEXP + 1], pl[u][:, :, ER:ER + FEXP + 1]))
                        st.link(nc.vector.tensor_reduce(t4[u][:, :], lg[u][:, :, 0:FEXP], AX.X, ALU.max))
                        nc.vector.tensor_tensor(lg[u][:, :, 0:FEXP], lg[u][:, :, 0:FEXP], spread(t4[u][:, :], FEXP), ALU.subtract).then_inc(s_lowc[u], 1)
                    for u in range(2):
                        dve.wait_ge(s_exp[u], i + 1)
                        st.link(nc.vector.tensor_reduce(t4[u][:, :], ex[u][:, :, :], AX.X, ALU.add))
                        st.link(nc.vector.reciprocal(t4[u][:, :], t4[u][:, :]))
                        st.link(nc.vector.tensor_tensor(ex[u][:, :, :], ex[u][:, :, :], spread(t4[u][:, :], FEXP), ALU.mult))
                        st.link(nc.vector.tensor_scalar(sg[u][:, :], sg[u][:, :], 0.5 / FEXP, 0.5 / FEXP, ALU.mult, ALU.add))
                        st.link(nc.vector.tensor_tensor(ex[u][:, :, :], ex[u][:, :, :], spread(sg[u][:, :], FEXP), ALU.subtract))
                        st.link(nc.vector.tensor_scalar(ex[u][:, :, :], ex[u][:, :, :], 0.0, None, ALU.max))
                        st.link(nc.vector.tensor_reduce(t4[u][:, :], ex[u][:, :, :], AX.X, ALU.add))
                        st.link(nc.vector.scalar_tensor_tensor(out=t4[u][:, :], in0=t4[u][:, :], scalar=0.0, in1=t4[u][:, :],
                                                               op0=ALU.is_equal, op1=ALU.add))
                        st.link(nc.vector.reciprocal(t4[u][:, :], t4[u][:, :]))
                        st.link(nc.vector.tensor_tensor(ex[u][:, :, :], ex[u][:, :, :], spread(t4[u][:, :], FEXP), ALU.mult))
                        nc.vector.tensor_tensor(wl[u][:, :, :].rearrange("p t (e r) -> p t e r", e=FEXP), wl[u][:, :, :].rearrange("p t (e r) -> p t e r", e=FEXP),
                                                ex[u][:, :, :].unsqueeze(3).broadcast_to([P, 4, FEXP, LORA]), ALU.mult).then_inc(s_wl[u], 1)
                    for u in range(2):
                        dve.wait_ge(s_o[u], i + 1)
                        dve.wait_ge(s_store[u], 16 * i)
                        nc.vector.tensor_tensor(yo[u][:, :, :], H[:, bass.ds((i * 2 + u) * 4, 4), :], po[u][:, :, :], ALU.add).then_inc(s_y[u], 1)
                    st.close()

            @block.scalar
            def _(act):
                for i in passes(act, G // 2):
                    for u in range(2):
                        act.wait_ge(s_turned[u], i + 1)
                        act.wait_ge(s_low[u], i)
                        nc.scalar.copy(xT[u][:, :], pt[u][:, :]).then_inc(s_xT[u], 1)
                    for u in range(2):
                        for e in range(FEXP):
                            act.wait_ge(s_fc1[u], FEXP * i + e + 1)
                            nc.scalar.activation(hid[u][:, e, :], pf[e % 2][:, :], ACT.Relu).then_inc(s_hid[u], 1)
                    for u in range(2):
                        act.wait_ge(s_lowc[u], i + 1)
                        act.wait_ge(s_wl[u], i)
                        nc.scalar.activation(ex[u][:, :, :], lg[u][:, :, 0:FEXP], ACT.Exp)
                        nc.scalar.activation(sg[u][:, :], lg[u][:, :, FEXP:FEXP + 1].rearrange("p a b -> p (a b)"), ACT.Tanh, scale=0.5).then_inc(s_exp[u], 1)
                    for u in range(2):
                        act.wait_ge(s_wlt[u], i + 1)
                        nc.scalar.copy(wlT[u][:, :], pt[u][:, 0:2 * P]).then_inc(s_wlT[u], 1)

            @block.tensor
            def _(pe):
                for i in passes(pe, G // 2):
                    for u in range(2):
                        pe.wait_ge(s_xn[u], i + 1)
                        pe.wait_ge(s_wlT[u], i)
                        for t in range(4):
                            ins = nc.tensor.transpose(pt[u][:, P * t:P * t + P], xn[u][:, t, :], k["ident"][:, :])
                        ins.then_inc(s_turned[u], 1)
                    for u in range(2):
                        pe.wait_ge(s_xT[u], i + 1)
                        for e in range(FEXP):
                            if e >= 2:
                                pe.wait_ge(s_hid[u], FEXP * i + e - 1)
                            elif u:
                                pe.wait_ge(s_hid[0], FEXP * i + FEXP - 1 + e)
                            else:
                                pe.wait_ge(s_hid[1], FEXP * i)
                            nc.tensor.matmul(pf[e % 2][:, :], k["fc1T"][:, e, :], xT[u][:, :], start=True, stop=True).then_inc(s_fc1[u], 1)
                    for u in range(2):
                        pe.wait_ge(s_hid[u], FEXP * i + FEXP)
                        pe.wait_ge(s_lowc[u], i)
                        for t in range(4):
                            c = slice(P * t, P * t + P)
                            for e in range(FEXP):
                                nc.tensor.matmul(pl[u][:, t, LORA * e:LORA * e + LORA], hid[u][:, e, c], A[:, e, :],
                                                 start=True, stop=True, skip_group_check=True)
                            ins = nc.tensor.matmul(pl[u][:, t, ER:ER + FEXP + 1], xT[u][:, c], gw[:, :], start=True, stop=True, skip_group_check=True)
                        ins.then_inc(s_low[u], 1)
                    for u in range(2):
                        pe.wait_ge(s_wl[u], i + 1)
                        for t in range(2):
                            ins = nc.tensor.transpose(pt[u][:, P * t:P * t + P], wl[u][:, 2 * t:2 * t + 2, :].rearrange("p a b -> p (a b)"),
                                                      k["ident"][:, :])
                        ins.then_inc(s_wlt[u], 1)
                    for u in range(2):
                        pe.wait_ge(s_wlT[u], i + 1)
                        pe.wait_ge(s_y[u], i)
                        for t in range(2):
                            ins = nc.tensor.matmul(po[u][:, 2 * t:2 * t + 2, :].rearrange("p a b -> p (a b)"), wlT[u][:, P * t:P * t + P], M[:, :], start=True, stop=True, skip_group_check=True)
                        ins.then_inc(s_o[u], 1)

            @block.sync
            def _(sp):
                for i in passes(sp, G // 2):
                    for u in range(2):
                        sp.wait_ge(s_y[u], i + 1)
                        sp.dma_start(out_v[:, bass.ds((i * 2 + u) * 4, 4), :], yo[u][:, :, :]).then_inc(s_store[u], 16)
                for u in range(2):
                    sp.wait_ge(s_store[u], 16 * G // 2)


MODES = 64
LQ = SEQ // 2 // P
NF = 8
COMPLEX = range(2, NF)
C8 = float(np.sqrt(0.5))


def roots():
    return np.array([[2 * (P * (q % 2) + p) + q // 2 for p in range(P)] for q in range(LQ)])


def freqs():
    f = [8 * np.arange(P), 4 + 8 * np.arange(P)]
    for f1 in (1, 2, 3):
        f += [f1 + 8 * np.arange(P), f1 + 8 * np.arange(P, 2 * P)]
    return np.array(f)


def ssm_tables():
    l = roots()
    tau = np.tan(np.pi * l / SEQ)
    t = np.arange(SEQ // 2)
    ang = 2 * np.pi * ((l[:, :, None] * t) % SEQ) / SEQ
    wt = np.where(l == 0, 0.5, 1.0)[:, :, None] / SEQ
    tau_cols = np.concatenate([tau.T, (tau ** 2).T, -tau.T], 1)
    halves = np.zeros((P, 4))
    halves[0:64, 0] = halves[64:, 1] = 1
    halves[0:64, 2] = halves[64:, 3] = -1
    n = 2 * SEQ
    fwd, inv = [], []
    F = freqs()
    for c in range(NF):
        for wt_ in range(2):
            tt = np.arange(P) + P * wt_
            a = 2 * np.pi * ((tt[:, None] * F[c][None, :]) % n) / n
            C, S = np.cos(a), np.sin(a)
            mats = [C, -S] + ([-C] if c in COMPLEX else [])
            g = np.full(P, 2.0 / n)
            if c == 0:
                mats[1][:, 0] = (-1.0) ** tt
                g[0] = 1.0 / n
            fwd += mats
            IC, IS = (C * g).T, (-S * g).T
            if c == 0:
                IC, IS = (np.cos(a) * g).T, (-np.sin(a) * g).T
                IS[0, :] = (-1.0) ** tt / n
            inv += [IC, IS] + ([-IS] if c in COMPLEX else [])
    f32 = lambda a: np.ascontiguousarray(a, dtype=np.float32)
    return {"c_tau2": f32(np.tile((tau.reshape(-1) ** 2), (P, 1))), "c_tau": f32(tau_cols), "c_halves": f32(halves),
            "c_kcos": f32((np.cos(ang) * wt).transpose(1, 0, 2)), "c_ksin": f32((-np.sin(ang) * wt).transpose(1, 0, 2)),
            "c_alt": f32(((-1.0) ** np.arange(P))[None] / SEQ),
            "c_fwd": f32(np.array(fwd).transpose(1, 0, 2)), "c_inv": f32(np.array(inv).transpose(1, 0, 2))}


def matrix_at():
    at, n = {}, 0
    for c in range(NF):
        for h in range(2):
            at[c, h] = n
            n += 3 if c in COMPLEX else 2
    return at, n


def ssm_kernel(nc, w, k, Kt):
    with ExitStack() as ctx:
        m = Mem(nc, ctx, "sk", k["banks"])
        NA = 9
        rl = m.sb("rl", [64, 2, P])
        r3 = m.sb("r3", [64, 3, 2 * P])
        rs, rsT, sb_ = m.sb("rs", [2, 64]), m.sb("rsT", [64, 2]), m.sb("sbc", [64, 2, 64])
        V = m.sb("V", [P, NA, 64])
        g = lambda n: m.sb(n, [P, 64])
        lr, li, mr, mi, q2, ns = g("lr"), g("li"), g("mr"), g("mi"), g("q2"), g("ns")
        WW = m.sb("WW", [P, 4, 4, 2, 64])
        t1, t2 = m.sb("t1", [P, 4, 64]), m.sb("t2", [P, 4, 64])
        W2 = m.sb("W2", [P, 64, 2, 32])
        tau2, tau, halves = m.sb("tau2", [P, HALF]), m.sb("tau", [P, 12]), m.sb("halves", [P, 4])
        kcos, ksin = m.sb("kcos", [P, LQ, SEQ // 2]), m.sb("ksin", [P, LQ, SEQ // 2])
        alt, Drow, p512 = m.sb("alt", [1, P]), m.sb("Drow", [1, P]), m.sb("p512", [1, P])
        sqr = [m.sb(f"sqr{u}", [P, HALF]) for u in range(2)]
        R = [m.sb(f"R{u}", [P, HALF]) for u in range(2)]
        SS = m.sb("SS", [P, LQ, 64, 64])
        A, B = m.sb("A", [P, P, 8]), m.sb("B", [P, P, 8])
        KP = m.sb("KP", [P, 2, 2, 4, P])
        tmp = [m.sb(f"tmp{j}", [P, 2, P]) for j in range(8)]
        PQ = m.sb("PQ", [P, LQ, 2, P])
        odd = m.sb("odd", [P, 4 * P])
        pa, pb, pc, pd = m.ps(), m.ps(), m.ps(), m.ps()
        ps = [m.ps((P, LQ, 64)) for u in range(2)]
        s_in, s_pe, s_dve, s_act, s_k = m.sem("in"), m.sem("pe"), m.sem("dve"), m.sem("act"), m.sem("k")
        two = lambda n: [m.sem(f"{n}{u}") for u in range(2)]
        s_sqr, s_den, s_R, s_S, s_Sc = two("sqr"), two("den"), two("R"), two("S"), two("Sc")
        flat = lambda t: t[:, :, :].rearrange("p a b -> p (a b)")
        NLOAD = 15
        with nc.Block() as block:
            @block.sync
            def _(sp):
                for j, n in enumerate(("re", "im")):
                    sp.dma_start(rl[:, j, :].rearrange("p (a n) -> p a n", a=2), w[f"L1_attn_Lambda_{n}"].rearrange("(a p) n -> p a n", a=2)).then_inc(s_in, 16)
                for j, n in enumerate("PBC"):
                    sp.dma_start(r3[:, j, :].rearrange("p (a x) -> p a x", a=2), w[f"L1_attn_{n}"].rearrange("(a p) n c -> p a (n c)", a=2)).then_inc(s_in, 16)
                sp.dma_start(rs[:, :], w["L1_attn_log_step"].rearrange("(a p) -> a p", a=2)).then_inc(s_in, 16)
                sp.dma_start(Drow[:, :], w["L1_attn_D"].rearrange("(a p) -> a p", a=1)).then_inc(s_in, 16)
                for dst, src in ((tau2, "c_tau2"), (tau, "c_tau"), (halves, "c_halves"), (alt, "c_alt")):
                    sp.dma_start(dst[:, :], w[src]).then_inc(s_in, 16)
                for dst, src in ((kcos, "c_kcos"), (ksin, "c_ksin")):
                    sp.dma_start(dst[:, :, :], w[src]).then_inc(s_in, 16)
                sp.wait_ge(s_in, 16 * 13)

            @block.tensor
            def _(pe):
                pe.wait_ge(s_in, 16 * 13)
                nc.tensor.transpose(pa[0:64, 0:2], rs[:, :], k["ident"][0:2, 0:2]).then_inc(s_pe, 1)
                pe.wait_ge(s_dve, 2)
                I64 = k["ident"][0:64, 0:64]
                nc.tensor.transpose(pa[:, 64:128], sb_[:, :, :].rearrange("p a b -> p (a b)"), I64)
                for j in range(2):
                    nc.tensor.transpose(pb[:, 64 * j:64 * j + 64], rl[:, j, :], I64)
                for j in range(3):
                    for c in range(2):
                        n = 2 + 2 * j + c
                        ins = nc.tensor.transpose(pb[:, 64 * n:64 * n + 64], r3[:, j, c::2], I64)
                ins.then_inc(s_pe, 1)
                pe.wait_ge(s_k, 1)
                for a in range(2):
                    ins = nc.tensor.matmul(pa[0:1, 64 * a:64 * a + 64], halves[:, 2 + a:3 + a], WW[:, 2, 0, 0, :], start=True, stop=True, skip_group_check=True)
                ins.then_inc(s_pe, 1)
                pe.wait_ge(s_k, 3)
                for i in passes(pe, 32):
                    for u in range(2):
                        pe.wait_ge(s_R[u], i + 1)
                        pe.wait_ge(s_Sc[u], i)
                        for q in range(LQ):
                            ins = nc.tensor.matmul(ps[u][:, q, :], R[u][:, P * q:P * q + P], W2[:, i * 2 + u, :, :].rearrange("p a b -> p (a b)"),
                                                   start=True, stop=True, skip_group_check=True)
                        ins.then_inc(s_S[u], 1)
                pe.wait_ge(s_k, 4)
                for t in range(4):
                    c = slice(P * t, P * t + P)
                    for q in range(LQ):
                        dst = (pc, pd)[q // 2][:, c]
                        nc.tensor.matmul(dst, kcos[:, q, c], PQ[:, q, 0, :], start=(q % 2 == 0), stop=False, skip_group_check=True)
                        ins = nc.tensor.matmul(dst, ksin[:, q, c], PQ[:, q, 1, :], start=False, stop=(q == 3), skip_group_check=True)
                        if q == 1:
                            nc.tensor.matmul(dst, alt[:, :], p512[:, :], start=False, stop=True, skip_group_check=True)
                ins.then_inc(s_pe, 1)

            @block.scalar
            def _(act):
                act.wait_ge(s_dve, 1)
                nc.scalar.activation(rsT[:, :], rsT[:, :], ACT.Exp).then_inc(s_act, 1)
                act.wait_ge(s_k, 2)
                for i in passes(act, 32):
                    for u in range(2):
                        act.wait_ge(s_den[u], i)
                        nc.scalar.activation(sqr[u][:, :], tau2[:, :], ACT.Square, bias=mr[:, bass.ds(i * 2 + u, 1)]).then_inc(s_sqr[u], 1)
                    for u in range(2):
                        act.wait_ge(s_S[u], i + 1)
                        nc.scalar.copy(SS[:, :, i * 2 + u, :], ps[u][:, :, :]).then_inc(s_Sc[u], 1)

            @block.vector
            def _(dve):
                st = Steps(dve, s_dve)
                dve.wait_ge(s_pe, 1)
                st.link(nc.vector.tensor_copy(rsT[:, :], pa[0:64, 0:2]))
                dve.wait_ge(s_act, 1)
                st.link(nc.vector.tensor_scalar(sb_[:, :, :], spread(rsT[:, :], 64), 0.5, None, ALU.mult))
                dve.wait_ge(s_pe, 2)
                nc.vector.tensor_copy(V[:, 8, :], pa[:, 64:128])
                st.link(nc.vector.tensor_copy(V[:, 0:8, :].rearrange("p a b -> p (a b)"), pb[:, :]))
                TT, MUL = nc.vector.tensor_tensor, ALU.mult
                s = V[:, 8, :]
                Pr, Pi, Br, Bi, Cr, Ci = (V[:, j, :] for j in range(2, 8))
                nc.vector.scalar_tensor_tensor(out=lr[:, :], in0=V[:, 0, :], scalar=-1e-4, in1=s, op0=ALU.min, op1=MUL)
                nc.vector.tensor_scalar(ns[:, :], s, -1.0, None, MUL)
                st.link(TT(li[:, :], V[:, 1, :], s, MUL))
                TT(t1[:, 0, :], lr[:, :], lr[:, :], MUL)
                TT(t1[:, 1, :], li[:, :], li[:, :], MUL)
                st.link(nc.vector.scalar_tensor_tensor(out=mi[:, :], in0=lr[:, :], scalar=2.0, in1=li[:, :], op0=MUL, op1=MUL))
                TT(mr[:, :], t1[:, 0, :], t1[:, 1, :], ALU.subtract)
                st.link(TT(q2[:, :], mi[:, :], mi[:, :], MUL))
                cr, ci = WW[:, 2, :, 0, :], WW[:, 2, :, 1, :]

                def conj_product(v, ar, ai, br, bi):
                    TT(t1[:, 0, :], ar, br, MUL)
                    TT(t1[:, 1, :], ai, bi, MUL)
                    TT(t1[:, 2, :], ar, bi, MUL)
                    st.link(TT(t1[:, 3, :], ai, br, MUL))
                    TT(cr[:, v, :], t1[:, 0, :], t1[:, 1, :], ALU.add)
                    st.link(TT(ci[:, v, :], t1[:, 2, :], t1[:, 3, :], ALU.subtract))

                conj_product(0, Cr, Ci, Br, Bi)
                conj_product(1, Cr, Ci, Pr, Pi)
                conj_product(2, Pr, Pi, Br, Bi)
                conj_product(3, Pr, Pi, Pr, Pi)
                over = lambda a: a[:, :].unsqueeze(1).broadcast_to([P, 4, 64])
                TT(cr, cr, over(ns), MUL)
                st.link(TT(ci, ci, over(ns), MUL))

                def times(out, x, yr, yi, conj):
                    xr, xi, o_r, o_i = WW[:, x, :, 0, :], WW[:, x, :, 1, :], WW[:, out, :, 0, :], WW[:, out, :, 1, :]
                    TT(t1[:, :, :], xr, over(yr), MUL)
                    st.link(TT(t2[:, :, :], xi, over(yi), MUL))
                    st.link(TT(o_r, t1[:, :, :], t2[:, :, :], ALU.add if conj else ALU.subtract))
                    TT(t1[:, :, :], xi, over(yr), MUL)
                    st.link(TT(t2[:, :, :], xr, over(yi), MUL))
                    st.link(TT(o_i, t1[:, :, :], t2[:, :, :], ALU.subtract if conj else ALU.add))

                times(0, 2, lr, li, False)
                times(1, 0, mr, mi, True)
                times(3, 2, mr, mi, True)
                dve.wait_ge(s_in, 16 * 13)
                nc.vector.tensor_copy(t1[:, 0, 0:1], t2[:, 0, 0:1]).then_inc(s_k, 1)
                nc.vector.tensor_copy(t1[:, 0, 1:2], t2[:, 0, 0:1]).then_inc(s_k, 1)
                for a in range(2):
                    ins = nc.vector.tensor_scalar(W2[:, :, a, :], WW[:, :, :, :, :].rearrange("p k v c n -> p n (k v c)"), halves[:, a:a + 1], None, MUL)
                dve.wait_ge(s_pe, 3)
                nc.vector.tensor_copy(p512[:, :], pa[0:1, 0:P]).then_inc(s_k, 1)
                for i in passes(dve, 32):
                    for u in range(2):
                        dve.wait_ge(s_sqr[u], i + 1)
                        nc.vector.tensor_scalar(sqr[u][:, :], sqr[u][:, :], q2[:, bass.ds(i * 2 + u, 1)], None, ALU.add).then_inc(s_den[u], 1)
                    for u in range(2):
                        dve.wait_ge(s_den[u], i + 1)
                        dve.wait_ge(s_S[u], i)
                        nc.vector.reciprocal(R[u][:, :], sqr[u][:, :]).then_inc(s_R[u], 1)
                for u in range(2):
                    dve.wait_ge(s_Sc[u], 32)
                for q in range(LQ):
                    T, T2, NT_ = tau[:, q:q + 1], tau[:, 4 + q:5 + q], tau[:, 8 + q:9 + q]
                    sums = lambda kk: SS[:, q, :, :].rearrange("p n (a s) -> p (n a) s", a=2)[:, :, 8 * kk:8 * kk + 8]
                    STT = nc.vector.scalar_tensor_tensor
                    STT(out=A[:, :, :], in0=sums(0), scalar=T2, in1=sums(1), op0=MUL, op1=ALU.add)
                    st.link(STT(out=B[:, :, :], in0=sums(2), scalar=T2, in1=sums(3), op0=MUL, op1=ALU.add))
                    pick = lambda X, c: X[:, :, :].rearrange("p h (v c) -> p v c h", c=2)[:, :, c, :]
                    STT(out=KP[:, 0, 0], in0=pick(B, 1), scalar=NT_, in1=pick(A, 0), op0=MUL, op1=ALU.add)
                    STT(out=KP[:, 0, 1], in0=pick(B, 0), scalar=T, in1=pick(A, 1), op0=MUL, op1=ALU.add)
                    STT(out=KP[:, 1, 0], in0=pick(B, 1), scalar=T, in1=pick(A, 0), op0=MUL, op1=ALU.add)
                    st.link(STT(out=KP[:, 1, 1], in0=pick(B, 0), scalar=NT_, in1=pick(A, 1), op0=MUL, op1=ALU.add))
                    kr, ki = (lambda v: KP[:, :, 0, v, :]), (lambda v: KP[:, :, 1, v, :])
                    a0, a1, a2, a3, a4, a5, a6, a7 = (x[:, :, :] for x in tmp)
                    TT(a0, kr(1), kr(2), MUL)
                    TT(a1, ki(1), ki(2), MUL)
                    TT(a2, kr(1), ki(2), MUL)
                    TT(a3, ki(1), kr(2), MUL)
                    st.link(nc.vector.tensor_scalar(a4, kr(3), 1.0, None, ALU.add))
                    TT(a0, a0, a1, ALU.subtract)
                    TT(a2, a2, a3, ALU.add)
                    TT(a5, a4, a4, MUL)
                    st.link(TT(a6, ki(3), ki(3), MUL))
                    st.link(TT(a5, a5, a6, ALU.add))
                    nc.vector.reciprocal(a5, a5)
                    TT(a1, a0, a4, MUL)
                    TT(a3, a2, ki(3), MUL)
                    TT(a6, a2, a4, MUL)
                    st.link(TT(a7, a0, ki(3), MUL))
                    TT(a1, a1, a3, ALU.add)
                    st.link(TT(a6, a6, a7, ALU.subtract))
                    TT(a1, a1, a5, MUL)
                    st.link(TT(a6, a6, a5, MUL))
                    TT(a1, kr(0), a1, ALU.subtract)
                    st.link(TT(a6, ki(0), a6, ALU.subtract))
                    TT(a0[:, 0, :], a1[:, 0, :], a1[:, 1, :], ALU.add)
                    st.link(TT(a0[:, 1, :], a6[:, 0, :], a6[:, 1, :], ALU.subtract))
                    unpair = lambda x: x.rearrange("p (n a) -> p a n", a=2)
                    out = lambda c: PQ[:, q, c, :].rearrange("p (a n) -> p a n", a=2)
                    STT(out=out(0), in0=unpair(a0[:, 1, :]), scalar=NT_, in1=unpair(a0[:, 0, :]), op0=MUL, op1=ALU.add)
                    ins = STT(out=out(1), in0=unpair(a0[:, 0, :]), scalar=T, in1=unpair(a0[:, 1, :]), op0=MUL, op1=ALU.add)
                    if q < LQ - 1:
                        st.link(ins)
                ins.then_inc(s_k, 1)
                dve.wait_ge(s_pe, 4)
                st.link(nc.vector.tensor_copy(odd[:, :], pd[:, :]))
                TT(Kt[:, 0:4, :].rearrange("p a b -> p (a b)"), pc[:, :], odd[:, :], ALU.add)
                st.link(TT(Kt[:, 4:8, :].rearrange("p a b -> p (a b)"), pc[:, :], odd[:, :], ALU.subtract))
                st.link(TT(Kt[0:1, 0, :], Kt[0:1, 0, :], Drow[:, :], ALU.add))


def ssm_convolve(nc, w, k, H, mean, rstd, Kt):
    with ExitStack() as ctx:
        m = Mem(nc, ctx, "sc", k["banks"])
        at, NM = matrix_at()
        fwd, inv = m.sb("fwd", [P, NM, P]), m.sb("inv", [P, NM, P])
        NB = 2
        W_ = NB * P
        xu = m.sb("xu", [P, 4, 2, NB, P])
        names = "s02 d02 s13 d13 f0 f4 r1 n1 r3 n3".split()
        Y = {n: m.sb(n, [P, 2 * W_]) for n in names}
        KA, KB = m.sb("KA", [P, NF, 2, P]), m.sb("KB", [P, NF, P])
        dc = m.sb("dc", [P, 1])
        T1 = [m.sb(f"T1{u}", [P, 2, NB, P]) for u in range(2)]
        T2 = [m.sb(f"T2{u}", [P, 2, NB, P]) for u in range(2)]
        YF = m.sb("YF", [P, NF, 2, W_])
        Z = [m.sb(f"Z{j}", [P, 2 * W_]) for j in range(8)]
        pf = [m.ps() for j in range(4)]
        pz = [m.ps() for j in range(4)]
        s_in, s_f, s_kf, s_dve, s_dve2, s_kc = m.sem("in"), m.sem("f"), m.sem("kf"), m.sem("dve"), m.sem("dve2"), m.sem("kc")
        s_y, s_tile, s_used, s_z, s_zc, s_h, s_prod, s_t, s_zs, s_pool = (m.sem(n) for n in ("y", "tile", "used", "z", "zc", "h", "prod", "t", "zs", "pool"))
        TT, MUL, ADD, SUB = nc.vector.tensor_tensor, ALU.mult, ALU.add, ALU.subtract
        STT = nc.vector.scalar_tensor_tensor
        inputs = {0: ("f0", None), 1: ("f4", None), 2: ("r1", "n1"), 3: ("r1", "n1"), 4: ("d02", "d13"), 5: ("d02", "d13"),
                  6: ("r3", "n3"), 7: ("r3", "n3")}
        results = [((0,), 0), ((1,), 0), ((2, 3), 0), ((2, 3), 1), ((4, 5), 0), ((4, 5), 1), ((6, 7), 0), ((6, 7), 1)]

        def split(x, nb, st):
            y = {n: Y[n][:, 0:2 * nb * P] for n in names}
            TT(y["s02"], x(0), x(2), ADD)
            TT(y["d02"], x(0), x(2), SUB)
            TT(y["s13"], x(1), x(3), ADD)
            st.link(TT(y["d13"], x(1), x(3), SUB))
            TT(y["f0"], y["s02"], y["s13"], ADD)
            TT(y["f4"], y["s02"], y["s13"], SUB)
            STT(out=y["r1"], in0=y["d13"], scalar=C8, in1=x(0), op0=MUL, op1=ADD)
            STT(out=y["r3"], in0=y["d13"], scalar=-C8, in1=x(0), op0=MUL, op1=ADD)
            STT(out=y["n1"], in0=y["s13"], scalar=C8, in1=x(2), op0=MUL, op1=ADD)
            return STT(out=y["n3"], in0=y["s13"], scalar=C8, in1=x(2), op0=MUL, op1=SUB)

        def forward(c, dst, nb):
            a, b = inputs[c]
            terms = [(0, a), (1, b)] if b else [(0, a)]
            for part in range(2):
                n = 0
                for h in range(2):
                    for j, name in terms:
                        ins = nc.tensor.matmul(dst(part), fwd[:, at[c, h] + part + j, :], Y[name][:, h * nb * P:(h + 1) * nb * P],
                                               start=(n == 0), stop=(n == 2 * len(terms) - 1), skip_group_check=True)
                        n += 1
            return ins

        with nc.Block() as block:
            @block.sync
            def _(sp):
                sp.dma_start(fwd[:, :, :], w["c_fwd"]).then_inc(s_in, 16)
                sp.dma_start(inv[:, :, :], w["c_inv"]).then_inc(s_in, 16)
                sp.wait_ge(s_in, 32)

            @block.tensor
            def _(pe):
                pe.wait_ge(s_in, 32)
                pe.wait_ge(s_kf, 1)
                for c in range(NF):
                    ins = forward(c, lambda p_: pf[c // 2][:, P * (2 * (c % 2) + p_):P * (2 * (c % 2) + p_) + P], 1)
                ins.then_inc(s_f, 1)
                pe.wait_ge(s_kc, 1)
                for i in passes(pe, BATCH // NB):
                    pe.wait_ge(s_y, i + 1)
                    for c in range(NF):
                        if c >= 4:
                            pe.wait_ge(s_used, NF * i + c - 3)
                        forward(c, lambda p_: pf[c % 4][:, W_ * p_:W_ * p_ + W_], NB).then_inc(s_tile, 1)
                    pe.wait_ge(s_prod, NF * i + NF)
                    for j, (cs_, kind) in enumerate(results):
                        if j >= 4:
                            pe.wait_ge(s_zc, 8 * i + j - 3)
                        elif j == 0:
                            pe.wait_ge(s_zc, 8 * i)
                        for h in range(2):
                            n = 0
                            for c in cs_:
                                for src, mat in (((0, 0), (1, 1)), ((0, 2), (1, 0)))[kind]:
                                    ins = nc.tensor.matmul(pz[j % 4][:, W_ * h:W_ * h + W_], inv[:, at[c, h] + mat, :], YF[:, c, src, :],
                                                           start=(n == 0), stop=(n == 2 * len(cs_) - 1), skip_group_check=True)
                                    n += 1
                        ins.then_inc(s_z, 1)

            @block.scalar
            def _(act):
                for i in passes(act, BATCH // NB):
                    act.wait_ge(s_h, i)
                    for j in range(8):
                        act.wait_ge(s_z, 8 * i + j + 1)
                        nc.scalar.copy(Z[j][:, :], pz[j % 4][:, :]).then_inc(s_zc, 1)

            @block.gpsimd
            def _(pool):
                for i in passes(pool, BATCH // NB):
                    for c in range(NF):
                        pool.wait_ge(s_used, NF * i + c + 1)
                        u = c % 2
                        o = lambda p_: YF[:, c, p_, :].rearrange("p (b h) -> p b h", b=NB)
                        nc.gpsimd.tensor_tensor(o(0), T1[u][:, 0], T2[u][:, 1], SUB)
                        nc.gpsimd.tensor_tensor(o(1), T1[u][:, 1], T2[u][:, 0], ADD).then_inc(s_prod, 1)

            @block.vector
            def _(dve):
                st = Steps(dve, s_dve)
                st.link(nc.vector.memset(dc[:, :], 1.0))
                st.link(nc.vector.memset(dc[0:1, :], 0.0))
                split(lambda j: Kt[:, 2 * j:2 * j + 2, :].rearrange("p a b -> p (a b)"), 1, st).then_inc(s_kf, 1)
                dve.wait_ge(s_f, 1)
                for c in range(NF):
                    src = lambda p_: pf[c // 2][:, P * (2 * (c % 2) + p_):P * (2 * (c % 2) + p_) + P]
                    nc.vector.tensor_copy(KA[:, c, 0, :], src(0))
                    if c:
                        nc.vector.tensor_copy(KA[:, c, 1, :], src(0))
                        ins = nc.vector.tensor_copy(KB[:, c, :], src(1))
                    else:
                        ins = nc.vector.tensor_scalar(KB[:, c, :], src(1), dc[:, 0:1], None, MUL)
                st.link(ins)
                st.link(nc.vector.tensor_scalar(KA[:, 0, 1, :], KA[:, 0, 0, :], dc[:, 0:1], None, MUL))
                nc.vector.tensor_copy(KA[0:1, 0, 1, :], pf[0][0:1, P:2 * P]).then_inc(s_kc, 1)
                dve.wait_ge(s_kc, 1)
                for i in passes(dve, BATCH // NB):
                    s2 = Steps(dve, s_dve2, i, 5)
                    for b in range(NB):
                        for t in range(TILES):
                            n = (i * NB + b) * TILES + t
                            ins = nc.vector.tensor_scalar(xu[:, t // 2, t % 2, b, :], H[:, n, :], mean[:, bass.ds(n, 1)], rstd[:, bass.ds(n, 1)], SUB, MUL)
                    s2.link(ins)
                    dve.wait_ge(s_tile, NF * i)
                    split(lambda j: xu[:, j].rearrange("p w b h -> p (w b h)"), NB, s2).then_inc(s_y, 1)
                    for c in range(NF):
                        dve.wait_ge(s_tile, NF * i + c + 1)
                        if c >= 2:
                            dve.wait_ge(s_prod, NF * i + c - 1)
                        else:
                            dve.wait_ge(s_prod, NF * i)
                        u = c % 2
                        src = pf[c % 4][:, :].rearrange("p (c b h) -> p c b h", c=2, b=NB)
                        TT(T1[u][:, :, :, :], src, KA[:, c, :, :].unsqueeze(2).broadcast_to([P, 2, NB, P]), MUL)
                        TT(T2[u][:, :, :, :], src, KB[:, c, :].unsqueeze(1).unsqueeze(1).broadcast_to([P, 2, NB, P]), MUL).then_inc(s_used, 1)
                    dve.wait_ge(s_zc, 8 * i + 8)
                    z0, z4, r1, i1, r2, i2, r3, i3 = (z[:, :] for z in Z)
                    sA, dA, sr, dr, si, di = (Y[n][:, :] for n in ("s02", "s13", "f0", "f4", "r1", "n1"))
                    TT(sA, z0, z4, ADD)
                    TT(dA, z0, z4, SUB)
                    TT(sr, r1, r3, ADD)
                    TT(dr, r1, r3, SUB)
                    TT(si, i1, i3, ADD)
                    s2.link(TT(di, i1, i3, SUB))
                    TT(z0, sA, r2, ADD)
                    TT(z4, sA, r2, SUB)
                    TT(r1, dA, i2, SUB)
                    TT(i1, dA, i2, ADD)
                    TT(r3, dr, si, SUB)
                    s2.link(TT(i3, dr, si, ADD))
                    TT(z0, z0, sr, ADD)
                    TT(z4, z4, di, SUB)
                    STT(out=r1, in0=r3, scalar=C8, in1=r1, op0=MUL, op1=ADD)
                    s2.link(STT(out=i1, in0=i3, scalar=-C8, in1=i1, op0=MUL, op1=ADD))
                    for j, y in enumerate((z0, r1, z4, i1)):
                        for b in range(NB):
                            dst = H[:, bass.ds((i * NB + b) * TILES + 2 * j, 2), :]
                            ins = TT(dst, dst, y.rearrange("p (w b h) -> p w b h", w=2, b=NB)[:, :, b, :], ADD)
                    ins.then_inc(s_h, 1)
                    dve.wait_ge(s_h, i + 1)
                    s2.close()


def tables():
    return {**attention_tables(), **moe_tables(), **ssm_tables()}


def tower(nc, w, out):
    USED.clear()
    rows = nc.dram_tensor("rows", (TOK, ROW), F32).ap()
    acc = nc.dram_tensor("acc", (TOK, D), F32).ap()
    with ExitStack() as ctx:
        m = Mem(nc, ctx, "all")
        k = constants(nc, m)
        H = m.sb("H", [P, NT, D])
        mean, rstd = m.sb("mean", [P, NT]), m.sb("rstd", [P, NT])
        load_constants(nc, w, k)
        embed_tokens(nc, w, k, H)
        with ExitStack() as ctx2:
            X2 = Mem(nc, ctx2, "x2").sb("X2", [P, NT, D])
            attention(nc, w, k, H, X2)
            row_stats(nc, k, X2, mean, rstd, "st_mlp")
            mlp(nc, w, k, H, X2, mean, rstd)
        row_stats(nc, k, H, mean, rstd, "st_moe")
        with ExitStack() as ctx2:
            lists = Mem(nc, ctx2, "moe").sb("lists", [P, EXPERTS + 1, NBLK], I32)
            moe_route(nc, w, k, H, mean, rstd, rows, acc, lists)
            moe_experts(nc, w, k, rows, acc, lists)
        reload(nc, H, acc)
        row_stats(nc, k, H, mean, rstd, "st_ssm")
        with ExitStack() as ctx2:
            Kt = Mem(nc, ctx2, "ssm").sb("Kt", [P, TILES, P])
            ssm_kernel(nc, w, k, Kt)
            ssm_convolve(nc, w, k, H, mean, rstd, Kt)
        row_stats(nc, k, H, mean, rstd, "st_ffn")
        ffn(nc, w, k, H, mean, rstd, out)


def kernel(**inputs):
    import numpy as _np
    import concourse.bacc as _bacc
    from concourse import mybir as _mybir
    from concourse.bass_utils import run_bass_kernel_spmd as _run

    nc = _bacc.Bacc("TRN2", target_bir_lowering=False, num_devices=1)
    arrays, args = {}, {}
    for name, a in {**inputs, **tables()}.items():
        a = _np.ascontiguousarray(a)
        arrays[f"in_{name}"] = a
        args[name] = nc.dram_tensor(f"in_{name}", a.shape, _mybir.dt.from_np(a.dtype), kind="ExternalInput").ap()
    out = nc.dram_tensor("out_0", (BATCH, SEQ, D), F32, kind="ExternalOutput").ap()
    tower(nc, args, out)
    r = _run(nc, [arrays], core_ids=[0])
    return r.results[0]["out_0"]
```

```python
import numpy as np
import concourse.bass as bass
from concourse import mybir
from contextlib import ExitStack

F32 = mybir.dt.float32
I32 = mybir.dt.int32
U32 = mybir.dt.uint32
ALU = mybir.AluOpType
ACT = mybir.ActivationFunctionType
AX = mybir.AxisListType

P = 128
BATCH, SEQ, D = 8, 1024, 128
TILES = SEQ // P
NT = BATCH * TILES
TOK = BATCH * SEQ
HALF = 512
BINS = 51


class Steps:

    def __init__(self, eng, sem, i=0, per=0):
        self.eng, self.sem, self.base, self.per, self.n = eng, sem, i * per, per, 0

    def link(self, ins):
        ins.then_inc(self.sem, 1)
        self.n += 1
        self.eng.wait_ge(self.sem, self.base + self.n)

    def close(self):
        assert self.n == self.per, (self.n, self.per)


USED = []


class Mem:

    def __init__(self, nc, ctx, tag, banks=None):
        self.nc, self.ctx, self.tag, self.banks, self.used, self.sems = nc, ctx, tag, banks, 0, []
        ctx.callback(USED.extend, self.sems)

    def sb(self, name, shape, dt=F32):
        return self.ctx.enter_context(self.nc.sbuf_tensor(f"{self.tag}_{name}", shape, dt))

    def ps(self, shape=(P, HALF)):
        bank = self.banks[:, self.used, 0:int(np.prod(shape[1:]))]
        self.used += 1
        if len(shape) == 3:
            bank = bank.rearrange("p (a b) -> p a b", b=shape[2])
        return bank

    def sem(self, name):
        self.sems.append(self.nc.alloc_semaphore(f"{self.tag}_{name}"))
        return self.sems[-1]


def reset_used(nc):
    nc.clear_and_free_semaphores(USED)
    USED.clear()


def passes(eng, n):
    yield 0
    with eng.Fori(1, n) as i:
        yield i


def spread(ap, n):
    return ap.unsqueeze(2).broadcast_to([ap.shape[0], ap.shape[1], n])


def load_constants(nc, w, k):
    with ExitStack() as ctx:
        m = Mem(nc, ctx, "ld", k["banks"])
        s_in, s_ps, s_cp = m.sem("in"), m.sem("turned"), m.sem("copied")
        s_id = m.sem("identity")
        raw = m.sb("raw", [P, 24, P])
        rows = [m.ps((P, P)) for i in range(2)]
        jobs = [(w[f"L0_attn_{n}"], k[n][:, :]) for n in ("Wq", "Wk", "Wv", "Wg", "Wo")]
        jobs += [(w["L0_attn_W1"][P * f:P * f + P, :], k["W1T"][:, P * f:P * f + P]) for f in range(4)]
        jobs += [(w["L0_attn_W2"][:, P * f:P * f + P], k["W2T"][:, f, :]) for f in range(4)]
        jobs += [(w["L1_ffn_fc1_w"][e], k["fc1T"][:, e, :]) for e in range(4)]
        jobs += [(w["L0_tok_bin_embeddings"], k["binsT"][:, :])]
        vectors = ["L0_tok_b1", "L0_attn_ln1_g", "L0_attn_ln1_b", "L0_attn_ln2_g", "L0_attn_ln2_b",
                   "L0_attn_time_decay", "L0_attn_rms_scale"]
        tms = ["L0_attn_tm_q", "L0_attn_tm_k", "L0_attn_tm_v", "L0_attn_tm_g"]
        nvec = len(vectors) + len(tms)
        with nc.Block() as block:
            @block.sync
            def _(sp):
                for j, (src, dst) in enumerate(jobs):
                    sp.dma_start(raw[0:src.shape[0], j, 0:src.shape[1]], src).then_inc(s_in, 16)
                for j, n in enumerate(vectors):
                    sp.dma_start(raw[j:j + 1, len(jobs), :], w[n].rearrange("(a c) -> a c", a=1)).then_inc(s_in, 16)
                for j, n in enumerate(tms):
                    sp.dma_start(raw[len(vectors) + j:len(vectors) + j + 1, len(jobs), :],
                                 w[n].rearrange("a b c -> (a b) c")).then_inc(s_in, 16)
                sp.wait_ge(s_id, 3)
                sp.dma_start(k["bins"][0:BINS, 0:P], w["L0_tok_bin_embeddings"]).then_inc(s_in, 16)
                sp.dma_start(k["bins"][64:64 + BINS, P:2 * P], w["L0_tok_bin_embeddings"]).then_inc(s_in, 16)
                sp.wait_ge(s_in, 16 * (len(jobs) + nvec + 2))

            @block.gpsimd
            def _(pool):
                nc.gpsimd.memset(k["ones"][:, :], 1.0).then_inc(s_id, 1)
                nc.gpsimd.memset(k["neg_half"][:, :], -0.5).then_inc(s_id, 1)
                nc.gpsimd.memset(k["bins"][:, :], 0.0).then_inc(s_id, 1)
                pool.wait_ge(s_id, 3)
                nc.gpsimd.affine_select(out=k["ident"][:, :], in_=k["ones"][:, :], compare_op=ALU.is_equal,
                                        fill=0.0, base=0, pattern=[[-1, P]], channel_multiplier=1).then_inc(s_id, 1)

            every = jobs + [(None, k["cols"][:, 0:nvec])]

            @block.tensor
            def _(pe):
                pe.wait_ge(s_id, 4)
                pe.wait_ge(s_in, 16 * (len(jobs) + nvec + 2))
                for j, (src, dst) in enumerate(every):
                    n = src.shape[0] if src is not None else nvec
                    if j >= 2:
                        pe.wait_ge(s_cp, j - 1)
                    nc.tensor.transpose(rows[j % 2][:, 0:n], raw[0:n, j, :], k["ident"][0:n, 0:n]).then_inc(s_ps, 1)

            @block.vector
            def _(dve):
                for j, (src, dst) in enumerate(every):
                    n = src.shape[0] if src is not None else nvec
                    dve.wait_ge(s_ps, j + 1)
                    nc.vector.tensor_copy(dst, rows[j % 2][:, 0:n]).then_inc(s_cp, 1)


def embed_tokens(nc, w, k, H):
    with ExitStack() as ctx:
        m = Mem(nc, ctx, "tok", k["banks"])
        tok_i = m.sb("tok_i", [1, TOK], I32)
        tok_f = m.sb("tok_f", [1, TOK])
        til_i = m.sb("til_i", [NT, P], I32)
        til_f = m.sb("til_f", [NT, P])
        live = m.sb("live", [P, NT])
        dead = m.sb("dead", [P, NT])
        w1 = m.sb("w1", [1, P])
        w2T = m.sb("w2T", [P, P])
        w2 = m.sb("w2", [P, P])
        b2 = m.sb("b2", [P, 1])
        simw = m.sb("simw", [P, BINS])
        simb = m.sb("simb", [1, BINS])
        hT = [m.sb(f"hT{u}", [P, HALF]) for u in range(2)]
        ex = [m.sb(f"ex{u}", [P, 4, 64]) for u in range(2)]
        prob = [m.sb(f"prob{u}", [P, 4, 64]) for u in range(2)]
        pT = [m.sb(f"pT{u}", [P, 2 * P]) for u in range(2)]
        mx = [m.sb(f"mx{u}", [P, 4]) for u in range(2)]
        sm = [m.sb(f"sm{u}", [P, 4]) for u in range(2)]
        inv = [m.sb(f"inv{u}", [P, 4]) for u in range(2)]
        ph = [m.ps() for u in range(2)]
        psim = [m.ps((P, 4, 64)) for u in range(2)]
        pp = [m.ps() for u in range(2)]
        pe_ = [m.ps() for u in range(2)]
        s_in, s_f, s_w, s_wc = m.sem("in"), m.sem("float"), m.sem("weights"), m.sem("wcopied")
        s_h = [m.sem(f"h{u}") for u in range(2)]
        s_relu = [m.sem(f"relu{u}") for u in range(2)]
        s_sim = [m.sem(f"sim{u}") for u in range(2)]
        s_sub = [m.sem(f"sub{u}") for u in range(2)]
        s_exp = [m.sem(f"exp{u}") for u in range(2)]
        s_prob = [m.sem(f"prob{u}") for u in range(2)]
        s_pT = [m.sem(f"pT{u}") for u in range(2)]
        s_pTc = [m.sem(f"pTc{u}") for u in range(2)]
        s_emb = [m.sem(f"emb{u}") for u in range(2)]
        s_out = [m.sem(f"out{u}") for u in range(2)]
        s_dve = m.sem("dve")
        NG = TOK // HALF
        with nc.Block() as block:
            @block.sync
            def _(sp):
                sp.dma_start(tok_i[:, :], w["x"].rearrange("b (t c) -> (b t) c", t=1).rearrange("(a b) c -> a (b c)", a=1)).then_inc(s_in, 16)
                sp.dma_start(til_i[:, :], w["x"].rearrange("b (t c) -> (b t) c", c=P)).then_inc(s_in, 16)
                sp.dma_start(w1[:, :], w["L0_tok_w1"]).then_inc(s_in, 16)
                sp.dma_start(w2[:, :], w["L0_tok_w2"]).then_inc(s_in, 16)
                sp.dma_start(b2[:, :], w["L0_tok_b2"].rearrange("(c a) -> c a", a=1)).then_inc(s_in, 16)

            @block.tensor
            def _(pe):
                pe.wait_ge(s_f, 2)
                nc.tensor.transpose(pp[0][:, 0:NT], til_f[:, :], k["ident"][0:NT, 0:NT]).then_inc(s_w, 1)
                nc.tensor.transpose(pp[1][:, 0:P], w2[:, :], k["ident"][:, :]).then_inc(s_w, 1)
                pe.wait_ge(s_wc, 3)
                nc.tensor.matmul(ph[0][:, 0:BINS], w2T[:, :], k["binsT"][:, :], start=True, stop=True).then_inc(s_w, 1)
                nc.tensor.matmul(ph[1][0:1, 0:BINS], b2[:, :], k["binsT"][:, :], start=True, stop=True).then_inc(s_w, 1)
                pe.wait_ge(s_wc, 7)
                for i in passes(pe, NG // 2):
                    for u in range(2):
                        pe.wait_ge(s_relu[u], i)
                        nc.tensor.matmul(ph[u][:, :], w1[:, :], tok_f[0:1, bass.ds((i * 2 + u) * HALF, HALF)],
                                         start=True, stop=True).then_inc(s_h[u], 1)
                    for u in range(2):
                        pe.wait_ge(s_relu[u], i + 1)
                        pe.wait_ge(s_sub[u], i)
                        for s in range(4):
                            nc.tensor.matmul(psim[u][:, s, 0:BINS], hT[u][:, P * s:P * s + P], simw[:, :],
                                             start=(s == 0), stop=False, skip_group_check=True)
                            ins = nc.tensor.matmul(psim[u][:, s, 0:BINS], k["ones"][0:1, :], simb[:, :],
                                                   start=False, stop=(s == 3), skip_group_check=True)
                        ins.then_inc(s_sim[u], 1)
                    for u in range(2):
                        pe.wait_ge(s_prob[u], i + 1)
                        pe.wait_ge(s_pTc[u], i)
                        for s in range(2):
                            ins = nc.tensor.transpose(pp[u][:, P * s:P * s + P],
                                                      prob[u][:, 2 * s:2 * s + 2, :].rearrange("p a b -> p (a b)"), k["ident"][:, :])
                        ins.then_inc(s_pT[u], 1)
                    for u in range(2):
                        pe.wait_ge(s_pTc[u], i + 1)
                        pe.wait_ge(s_out[u], i)
                        for s in range(2):
                            ins = nc.tensor.matmul(pe_[u][:, 2 * P * s:2 * P * s + 2 * P], pT[u][:, P * s:P * s + P], k["bins"][:, :],
                                                   start=True, stop=True, skip_group_check=True)
                        ins.then_inc(s_emb[u], 1)

            @block.scalar
            def _(act):
                for i in passes(act, NG // 2):
                    for u in range(2):
                        act.wait_ge(s_h[u], i + 1)
                        act.wait_ge(s_sim[u], i)
                        nc.scalar.activation(hT[u][:, :], ph[u][:, :], ACT.Relu, bias=k["b1"]).then_inc(s_relu[u], 1)
                    for u in range(2):
                        act.wait_ge(s_sub[u], i + 1)
                        nc.scalar.activation(prob[u][:, :, 1:BINS], ex[u][:, :, 1:BINS], ACT.Exp).then_inc(s_exp[u], 1)
                    for u in range(2):
                        act.wait_ge(s_pT[u], i + 1)
                        act.wait_ge(s_emb[u], i)
                        nc.scalar.copy(pT[u][:, :], pp[u][:, 0:2 * P]).then_inc(s_pTc[u], 1)
                    for u in range(2):
                        act.wait_ge(s_emb[u], i + 1)
                        nc.scalar.copy(H[:, bass.ds((i * 2 + u) * 4, 4), :], pe_[u][:, :].rearrange("p (s d) -> p s d", s=4)).then_inc(s_out[u], 1)

            @block.vector
            def _(dve):
                for u in range(2):
                    nc.vector.memset(prob[u][:, :, :], 0.0).then_inc(s_wc, 1)
                dve.wait_ge(s_in, 80)
                nc.vector.tensor_copy(tok_f[:, :], tok_i[:, :]).then_inc(s_f, 1)
                nc.vector.tensor_copy(til_f[:, :], til_i[:, :]).then_inc(s_f, 1)
                dve.wait_ge(s_w, 2)
                nc.vector.tensor_copy(w2T[:, :], pp[1][:, 0:P]).then_inc(s_wc, 1)
                nc.vector.tensor_scalar(live[:, :], pp[0][:, 0:NT], 0.0, None, ALU.not_equal).then_inc(s_wc, 1)
                nc.vector.tensor_scalar(dead[:, :], pp[0][:, 0:NT], 0.0, None, ALU.is_equal).then_inc(s_wc, 1)
                dve.wait_ge(s_w, 4)
                nc.vector.tensor_copy(simw[:, :], ph[0][:, 0:BINS]).then_inc(s_wc, 1)
                nc.vector.tensor_copy(simb[:, :], ph[1][0:1, 0:BINS]).then_inc(s_wc, 1)
                dve.wait_ge(s_wc, 7)
                for i in passes(dve, NG // 2):
                    st = Steps(dve, s_dve, i, 8)
                    for u in range(2):
                        dve.wait_ge(s_sim[u], i + 1)
                        dve.wait_ge(s_exp[u], i)
                        st.link(nc.vector.tensor_reduce(mx[u][:, :], psim[u][:, :, 1:BINS], AX.X, ALU.max))
                        nc.vector.tensor_tensor(ex[u][:, :, 1:BINS], psim[u][:, :, 1:BINS], spread(mx[u][:, :], BINS - 1),
                                                ALU.subtract).then_inc(s_sub[u], 1)
                    for u in range(2):
                        dve.wait_ge(s_exp[u], i + 1)
                        st.link(nc.vector.tensor_reduce(sm[u][:, :], prob[u][:, :, 1:BINS], AX.X, ALU.add))
                        st.link(nc.vector.reciprocal(inv[u][:, :], sm[u][:, :]))
                        st.link(nc.vector.tensor_tensor(inv[u][:, :], inv[u][:, :], live[:, bass.ds((i * 2 + u) * 4, 4)], ALU.mult))
                        nc.vector.tensor_copy(prob[u][:, :, 0:1].rearrange("p a b -> p (a b)"), dead[:, bass.ds((i * 2 + u) * 4, 4)])
                        nc.vector.tensor_tensor(prob[u][:, :, 1:BINS], prob[u][:, :, 1:BINS], spread(inv[u][:, :], BINS - 1),
                                                ALU.mult).then_inc(s_prob[u], 1)
                    st.close()


def constants(nc, m):
    k = {n: m.sb(n, [P, P]) for n in ("ident", "ones", "Wq", "Wk", "Wv", "Wg", "Wo")}
    k["banks"] = m.ctx.enter_context(nc.psum_tensor("banks", [P, 8, HALF], F32))
    k["W1T"] = m.sb("W1T", [P, 4 * P])
    k["W2T"] = m.sb("W2T", [P, 4, P])
    k["fc1T"] = m.sb("fc1T", [P, 4, P])
    k["binsT"] = m.sb("binsT", [P, BINS])
    k["bins"] = m.sb("bins", [P, 2 * P])
    k["neg_half"] = m.sb("neg_half", [P, 16])
    k["cols"] = m.sb("cols", [P, 16])
    for j, n in enumerate(("b1", "ln1_g", "ln1_b", "ln2_g", "ln2_b", "time_decay", "rms", "tm_q", "tm_k", "tm_v", "tm_g")):
        k[n] = k["cols"][:, j:j + 1]
    return k


LEVELS = (64, 32, 16, 8, 4)
NL = len(LEVELS)
NEAR = LEVELS[-1]
UNIT = 2 * P
STEP = ((0, 3), (3, 5))
HEADS, DH = 4, 32


def attention_tables():
    see = np.zeros((P, NL, P), np.float32)
    for l, b in enumerate(LEVELS):
        for c in range(P):
            see[c // b * b:c // b * b + b, l, c] = 1.0
    blk = np.kron(np.eye(HEADS, dtype=np.float32), np.ones((DH, DH), np.float32))
    pick = np.tile(2 * np.kron(np.eye(HEADS, dtype=np.float32), np.ones((DH, 1), np.float32)), (1, P // HEADS))
    up = np.tile(np.arange(P + 1, dtype=np.float32), (P, 1))
    return {"c_see": see.reshape(P, NL * P), "c_heads": blk, "c_pick": pick, "c_up": up, "c_down": up[:, ::-1].copy()}


def merge_stats(nc, st, stats, mean, sq, var):
    nc.vector.tensor_tensor(mean, stats[:, :, 1], stats[:, :, 4], ALU.add)
    nc.vector.tensor_tensor(sq, stats[:, :, 1], stats[:, :, 4], ALU.subtract)
    st.link(nc.vector.tensor_tensor(var, stats[:, :, 2], stats[:, :, 5], ALU.add))
    nc.vector.tensor_scalar(mean, mean, 0.5, None, ALU.mult)
    nc.vector.tensor_scalar(var, var, 1.0 / D, 1e-5, ALU.mult, ALU.add)
    st.link(nc.vector.tensor_tensor(sq, sq, sq, ALU.mult))
    return nc.vector.scalar_tensor_tensor(out=var, in0=sq, scalar=0.25, in1=var, op0=ALU.mult, op1=ALU.add)


def double_stats(nc, k, H, mean, rstd, rstd2):
    with ExitStack() as ctx:
        m = Mem(nc, ctx, "dst", k["banks"])
        stats = m.sb("stats", [P, NT, 6])
        var, sq, expo, var2 = (m.sb(n, [P, NT]) for n in ("var", "sq", "expo", "var2"))
        s_stats, s_dve, s_var, s_out = m.sem("stats"), m.sem("dve"), m.sem("var"), m.sem("rstd")
        TT, TS = nc.vector.tensor_tensor, nc.vector.tensor_scalar
        with nc.Block() as block:
            @block.vector
            def _(dve):
                nc.vector.memset(expo[:, :], -0.5)
                with dve.Fori(0, NT // 4) as i:
                    for t in range(4):
                        ins = nc.vector.bn_stats(stats[:, i * 4 + t, :], H[:, i * 4 + t, :])
                    ins.then_inc(s_stats, 1)
                dve.wait_ge(s_stats, NT // 4)
                st = Steps(dve, s_dve)
                TT(mean[:, :], stats[:, :, 1], stats[:, :, 4], ALU.add)
                TT(sq[:, :], stats[:, :, 1], stats[:, :, 4], ALU.subtract)
                st.link(TT(var[:, :], stats[:, :, 2], stats[:, :, 5], ALU.add))
                TS(mean[:, :], mean[:, :], 0.5, None, ALU.mult)
                TS(var[:, :], var[:, :], 1.0 / D, None, ALU.mult)
                st.link(TT(sq[:, :], sq[:, :], sq[:, :], ALU.mult))
                st.link(nc.vector.scalar_tensor_tensor(out=var[:, :], in0=sq[:, :], scalar=0.25, in1=var[:, :], op0=ALU.mult, op1=ALU.add))
                TS(var2[:, :], var[:, :], 1e-5, None, ALU.add).then_inc(s_var, 1)
                dve.wait_ge(s_out, 1)
                st.link(TT(sq[:, :], rstd[:, :], rstd[:, :], ALU.mult))
                st.link(TT(sq[:, :], sq[:, :], var[:, :], ALU.mult))
                TS(var2[:, :], sq[:, :], 1e-5, None, ALU.add).then_inc(s_var, 1)
                dve.wait_ge(s_out, 2)
                TT(rstd2[:, :], rstd2[:, :], rstd[:, :], ALU.mult)

            @block.gpsimd
            def _(pool):
                for j, dst in enumerate((rstd, rstd2)):
                    pool.wait_ge(s_var, j + 1)
                    nc.gpsimd.tensor_tensor(dst[:, :], var2[:, :], expo[:, :], ALU.pow).then_inc(s_out, 1)


def attention(nc, w, k, H, X2, mean, rstd):
    with ExitStack() as ctx:
        m = Mem(nc, ctx, "at", k["banks"])
        rstd2 = m.sb("rstd2", [P, NT])
        double_stats(nc, k, H, mean, rstd, rstd2)
        xn = m.sb("xn", [P, TILES, P])
        flat = lambda t: t[:, :, :].rearrange("p a b -> p (a b)")
        hs = m.sb("hs", [P, SEQ + 1])
        diff = flat(xn)
        kend = flat(xn)
        xm = [m.sb(f"xm{j}", [P, SEQ]) for j in range(4)]
        q, kk = m.sb("q", [P, SEQ]), m.sb("k", [P, SEQ])
        sq = [m.sb(f"sq{j}", [P, SEQ]) for j in range(2)]
        z, qz = sq
        n_near = lambda d: SEQ // NEAR * (NEAR - d)
        near = [xm[0][:, :], xm[1][:, 0:n_near(1)], z[:, 0:n_near(2)], z[:, n_near(2):n_near(2) + n_near(3)]]
        tmp = hs[:, 1:1 + n_near(1)]
        v = m.sb("v", [P, TILES, P])
        xvc = m.sb("xvc", [P, NL, SEQ // 2])
        vc = m.sb("vc", [P, NL, SEQ // UNIT, P])
        vT, rg, dv = m.sb("vT", [P, SEQ]), m.sb("rg", [P, SEQ]), m.sb("dv", [P, SEQ])
        kc, qc = m.sb("kc", [P, NL, SEQ // 2]), m.sb("qc", [P, NL, SEQ // 2])
        qin = m.sb("qin", [P, SEQ])
        pm = [m.sb(f"pm{s}", [P, HEADS, (hi - lo) * P]) for s, (lo, hi) in enumerate(STEP)]
        see, heads, pick = m.sb("see", [P, NL * P]), m.sb("heads", [P, P]), m.sb("pick", [P, P])
        up, down = m.sb("up", [P, P + 1]), m.sb("down", [P, P + 1])
        pw, rpw = m.sb("pw", [P, P + 1]), m.sb("rpw", [P, P + 1])
        lnl = m.sb("lnl", [P, 2])
        state = m.sb("state", [P, TILES, P])
        kendT = m.sb("kendT", [P, TILES - 1, P])
        ssv, root = m.sb("ssv", [P, 16]), m.sb("root", [P, 16])
        rz = m.sb("rz", [P, TILES * HEADS])
        half = m.sb("half", [P, 16])
        PS = k["banks"]
        two_banks = lambda b, n=2 * HALF: PS[:, b:b + 2, :].rearrange("p a b -> p (a b)")[:, 0:n]
        S = {n: m.sem(n) for n in (
            "in lam ready xn turned hs diff mix proj projc xvc ss ssv root rms rb qn exp "
            "v vT g vc01 vc23 vc4 kt u Zs rzb nearp nearc vsb vTsb gsb vcsb ktsb qk kend kc qc qin near1 qz um state rz rg "
            "scoreA scoreB maskA maskB av att wo x2 dveM dveO dveC").split()}
        left = lambda t, h: t.rearrange("p (n s c) -> p n s c", s=2, c=h)[:, :, 0, :]
        right = lambda t, h: t.rearrange("p (n s c) -> p n s c", s=2, c=h)[:, :, 1, :]
        tiles = lambda t: t.rearrange("p (n t) -> p n t", t=P)
        blocks = lambda t: t.rearrange("p (n c) -> p n c", c=NEAR)
        UNITS, KS = SEQ // UNIT, 2 * (SEQ // UNIT)
        with nc.Block() as block:
            @block.sync
            def _(sp):
                for dst, src in ((see, "c_see"), (heads, "c_heads"), (pick, "c_pick"), (up, "c_up"), (down, "c_down")):
                    sp.dma_start(dst[:, :], w[src]).then_inc(S["in"], 16)
                sp.wait_ge(S["in"], 80)

            @block.gpsimd
            def _(pool):
                TT = nc.gpsimd.tensor_tensor

                def mix(b, first):
                    pool.wait_ge(S["hs"], 2 * b + 2)
                    TT(diff, hs[:, 1:SEQ + 1], hs[:, 0:SEQ], ALU.subtract).then_inc(S["diff"], 1)
                    pool.wait_ge(S["ssv"], b + 1)
                    TT(root[:, :], ssv[:, :], half[:, :], ALU.pow).then_inc(S["root"], 1)

                def operands(b, first):
                    pool.wait_ge(S["exp"], 2 * b + 2)
                    TT(kend.rearrange("p (n t) -> p n t", t=P), tiles(kk[:, :]), rpw[:, 1:P + 1].unsqueeze(1).broadcast_to([P, TILES, P]),
                       ALU.mult).then_inc(S["kend"], 1)
                    TT(near[0], q[:, :], kk[:, :], ALU.mult).then_inc(S["qk"], 1)
                    if not first:
                        pool.wait_ge(S["scoreB"], KS * b)
                    for l, h in enumerate(LEVELS):
                        ins = TT(kc[:, l, :].rearrange("p (n c) -> p n c", c=h), left(kk[:, :], h),
                                 rpw[:, P - h:P].unsqueeze(1).broadcast_to([P, SEQ // (2 * h), h]), ALU.mult)
                    ins.then_inc(S["kc"], 1)
                    TT(tiles(qin[:, :]), tiles(q[:, :]), pw[:, 1:P + 1].unsqueeze(1).broadcast_to([P, TILES, P]), ALU.mult).then_inc(S["qin"], 1)

                nc.gpsimd.memset(half[:, :], 0.5).then_inc(S["ready"], 1)
                pool.wait_ge(S["ready"], 1)
                pool.wait_ge(S["lam"], 4)
                mix(0, True)
                operands(0, True)
                with pool.Fori(1, BATCH) as b:
                    mix(b, False)
                    operands(b, False)

            @block.scalar
            def _(act):
                def mix(b, first):
                    for j in range(2):
                        act.wait_ge(S["turned"], 2 * b + j + 1)
                        nc.scalar.activation(hs[:, 1 + HALF * j:1 + HALF * j + HALF], PS[:, 6 + j, :], ACT.Identity,
                                             bias=k["ln1_b"], scale=k["ln1_g"]).then_inc(S["hs"], 1)
                    for j in range(4):
                        c = slice(HALF * (j % 2), HALF * (j % 2) + HALF)
                        act.wait_ge(S["proj"], 4 * b + j + 1)
                        nc.scalar.copy((q, kk)[j // 2][:, c], PS[:, 6 + j % 2, :])
                        nc.scalar.activation(sq[j // 2][:, c], PS[:, 6 + j % 2, :], ACT.Square).then_inc(S["projc"], 1)
                    act.wait_ge(S["mix"], 4 * b + 3)
                    for l, h in enumerate(LEVELS):
                        ins = nc.scalar.copy(xvc[:, l, :].rearrange("p (n c) -> p n c", c=h), left(xm[2][:, :], h))
                    ins.then_inc(S["xvc"], 1)
                    for j, a in enumerate((q, kk)):
                        act.wait_ge(S["qn"], 4 * b + 2 * j + 2)
                        nc.scalar.activation(a[:, :], a[:, :], ACT.Exp, scale=k["rms"]).then_inc(S["exp"], 1)

                def operands(b, first):
                    act.wait_ge(S["v"], b + 1)
                    nc.scalar.copy(flat(v), two_banks(2)).then_inc(S["vsb"], 1)
                    act.wait_ge(S["vT"], b + 1)
                    nc.scalar.copy(vT[:, :], two_banks(6)).then_inc(S["vTsb"], 1)
                    if not first:
                        act.wait_ge(S["att"], b)
                    act.wait_ge(S["g"], b + 1)
                    nc.scalar.activation(rg[:, :], two_banks(0), ACT.Tanh, scale=0.5).then_inc(S["gsb"], 1)
                    if not first:
                        act.wait_ge(S["av"], KS * b)
                    for n, (name, b0, lo, hi) in enumerate((("vc01", 2, 0, 2), ("vc23", 6, 2, 4), ("vc4", 0, 4, 5))):
                        act.wait_ge(S[name], b + 1)
                        nc.scalar.copy(vc[:, lo:hi, :, :].rearrange("p a b c -> p (a b c)"), two_banks(b0, HALF * (hi - lo))).then_inc(S["vcsb"], 1)
                    act.wait_ge(S["kt"], b + 1)
                    nc.scalar.copy(flat(kendT), two_banks(2, P * (TILES - 1))).then_inc(S["ktsb"], 1)

                act.wait_ge(S["lam"], 1)
                nc.scalar.activation(lnl[:, 1:2], lnl[:, 0:1], ACT.Exp).then_inc(S["lam"], 1)
                act.wait_ge(S["lam"], 3)
                act.wait_ge(S["in"], 80)
                nc.scalar.activation(pw[:, :], up[:, :], ACT.Exp, scale=lnl[:, 0:1])
                nc.scalar.activation(rpw[:, :], down[:, :], ACT.Exp, scale=lnl[:, 0:1]).then_inc(S["lam"], 1)
                mix(0, True)
                operands(0, True)
                with act.Fori(1, BATCH) as b:
                    mix(b, False)
                    operands(b, False)

            @block.tensor
            def _(pe):
                mm = nc.tensor.matmul

                def mix_part(b, k_):
                    if k_ == 1:
                        pe.wait_ge(S["xn"], b + 1)
                        for j in range(2):
                            for t in range(4):
                                ins = nc.tensor.transpose(PS[:, 6 + j, P * t:P * t + P], xn[:, 4 * j + t, :], k["ident"][:, :])
                            ins.then_inc(S["turned"], 1)
                    if k_ in (4, 5):
                        a = k_ - 4
                        pe.wait_ge(S["mix"], 4 * b + a + 1)
                        for j in range(2):
                            if a:
                                pe.wait_ge(S["projc"], 4 * b + j + 1)
                            else:
                                pe.wait_ge(S["hs"], 2 * b + j + 1)
                            mm(PS[:, 6 + j, :], k[("Wq", "Wk")[a]][:, :], xm[a][:, HALF * j:HALF * j + HALF],
                               start=True, stop=True).then_inc(S["proj"], 1)
                    if k_ == 6:
                        pe.wait_ge(S["projc"], 4 * b + 4)
                        for j in range(2):
                            for t in range(TILES):
                                n = 8 * j + t
                                ins = mm(PS[:, 6, n:n + P], sq[j][:, P * t:P * t + P], k["ones"][:, :],
                                         start=True, stop=True, skip_group_check=True)
                        ins.then_inc(S["ss"], 1)
                    if k_ == 8:
                        pe.wait_ge(S["rms"], b + 1)
                        for j in range(4):
                            for t in range(4):
                                n = 4 * j + t
                                ins = mm(PS[:, (6, 7, 0, 1)[j], P * t:P * t + P], ssv[:, n:n + 1].broadcast_to([P, P]), k["ident"][:, :],
                                         start=True, stop=True, skip_group_check=True)
                            ins.then_inc(S["rb"], 1)

                def operands(b, first):
                    if not first:
                        pe.wait_ge(S["maskB"], KS * b)
                    for t in range(TILES):
                        ins = mm(PS[:, 2 + t // 4, P * (t % 4):P * (t % 4) + P], xm[2][:, P * t:P * t + P], k["Wv"][:, :],
                                 start=True, stop=True, skip_group_check=True)
                    ins.then_inc(S["v"], 1)
                    for name, b0, Wn, x_, bank_free in (("vT", 6, "Wv", 2, 2), ("g", 0, "Wg", 3, 4)):
                        pe.wait_ge(S["qn"], 4 * b + bank_free)
                        for j in range(2):
                            ins = mm(PS[:, b0 + j, :], k[Wn][:, :], xm[x_][:, HALF * j:HALF * j + HALF], start=True, stop=True)
                        ins.then_inc(S[name], 1)
                    pe.wait_ge(S["xvc"], b + 1)
                    for name, b0, lo, hi, free in (("vc01", 2, 0, 2, "vsb"), ("vc23", 6, 2, 4, "vTsb"), ("vc4", 0, 4, 5, "gsb")):
                        pe.wait_ge(S[free], b + 1)
                        for l in range(lo, hi):
                            for g in range(UNITS):
                                ins = mm(PS[:, b0 + l - lo, P * g:P * g + P], xvc[:, l, P * g:P * g + P], k["Wv"][:, :],
                                         start=True, stop=True, skip_group_check=True)
                        ins.then_inc(S[name], 1)
                    pe.wait_ge(S["vcsb"], 3 * b + 1)
                    pe.wait_ge(S["kend"], b + 1)
                    for n in range(TILES - 1):
                        ins = nc.tensor.transpose(PS[:, 2 + n // 4, P * (n % 4):P * (n % 4) + P], kend[:, P * n:P * n + P], k["ident"][:, :])
                    ins.then_inc(S["kt"], 1)
                    pe.wait_ge(S["vcsb"], 3 * b + 2)
                    pe.wait_ge(S["qk"], b + 1)
                    for j in range(2):
                        ins = mm(PS[:, 6 + j, :], heads[:, :], near[0][:, HALF * j:HALF * j + HALF], start=True, stop=True)
                    ins.then_inc(S["nearp"], 1)
                    pe.wait_ge(S["vcsb"], 3 * b + 3)
                    pe.wait_ge(S["near1"], b + 1)
                    mm(PS[:, 0, :], heads[:, :], near[1][:, 0:HALF], start=True, stop=True)
                    mm(PS[:, 1, 0:n_near(1) - HALF], heads[:, :], near[1][:, HALF:n_near(1)], start=True, stop=True).then_inc(S["nearp"], 1)
                    pe.wait_ge(S["ktsb"], b + 1)
                    for n in range(TILES - 1):
                        ins = mm(PS[:, 2 + n // 4, P * (n % 4):P * (n % 4) + P], kendT[:, n, :], v[:, n, :], start=True, stop=True, skip_group_check=True)
                    ins.then_inc(S["u"], 1)
                    pe.wait_ge(S["nearc"], 3 * b + 1)
                    pe.wait_ge(S["qz"], b + 1)
                    mm(PS[:, 6, :], heads[:, :], near[2], start=True, stop=True)
                    mm(PS[:, 7, 0:n_near(3)], heads[:, :], near[3], start=True, stop=True).then_inc(S["nearp"], 1)
                    pe.wait_ge(S["nearc"], 3 * b + 2)
                    for t in range(TILES):
                        ins = mm(PS[:, 0, HEADS * t:HEADS * t + P], qz[:, P * t:P * t + P], pick[:, :], start=True, stop=True, skip_group_check=True)
                    ins.then_inc(S["Zs"], 1)
                    pe.wait_ge(S["rz"], b + 1)
                    pe.wait_ge(S["um"], b + 1)
                    for t in range(TILES):
                        for h in range(HEADS):
                            n = HEADS * t + h
                            ins = mm(PS[DH * h:DH * h + DH, 2 + t // 4, P * (t % 4):P * (t % 4) + P], rz[:, n:n + 1].broadcast_to([P, DH]),
                                     k["ident"][:, :], start=True, stop=True, skip_group_check=True)
                    ins.then_inc(S["rzb"], 1)

                def scores(k_, hs_, name):
                    g, (lo, hi) = k_ // 2, STEP[k_ % 2]
                    for l in range(lo, hi):
                        for h in hs_:
                            r = slice(DH * h, DH * h + DH)
                            ins = mm(PS[:, h, P * (l - lo):P * (l - lo) + P], kc[r, l, P * g:P * g + P], qc[r, l, P * g:P * g + P],
                                     start=True, stop=True, skip_group_check=True)
                    ins.then_inc(S[name], 1)

                def values(k_):
                    g, (lo, hi) = k_ // 2, STEP[k_ % 2]
                    dst = PS[:, 4 + g // 2, UNIT * (g % 2):UNIT * (g % 2) + UNIT]
                    for l in range(lo, hi):
                        later = right(dst, LEVELS[l])
                        for h in range(HEADS):
                            r = slice(DH * h, DH * h + DH)
                            ins = mm(later[r], vc[:, l, g, r], pm[k_ % 2][:, h, P * (l - lo):P * (l - lo) + P],
                                     start=False, stop=False, skip_group_check=True)
                    ins.then_inc(S["av"], 1)

                def core(b, first, last):
                    pe.wait_ge(S["kc"], b + 1)
                    pe.wait_ge(S["qc"], b + 1)
                    pe.wait_ge(S["qin"], b + 1)
                    pe.wait_ge(S["state"], b + 1)
                    if not first:
                        pe.wait_ge(S["x2"], 2 * b)
                    for k_ in range(KS):
                        for name, hs_ in (("A", (0, 1)), ("B", (2, 3))):
                            if k_:
                                pe.wait_ge(S["mask" + name], KS * b + k_)
                            elif name == "B":
                                pe.wait_ge(S["rg"], b + 1)
                            scores(k_, hs_, "score" + name)
                        if k_ % 4 == 0:
                            for n in range(k_, k_ + 4):
                                mm(PS[:, 4 + n // 4, P * (n % 4):P * (n % 4) + P], state[:, n, :], qin[:, P * n:P * n + P],
                                   start=(n % 4 == 0), stop=False, skip_group_check=True)
                        if k_:
                            values(k_ - 1)
                        if not last:
                            mix_part(b + 1, k_)
                    pe.wait_ge(S["maskB"], KS * b + KS)
                    values(KS - 1)
                    if not last:
                        mix_part(b + 1, KS)

                def gather_out(b):
                    pe.wait_ge(S["att"], b + 1)
                    for t in range(TILES):
                        ins = mm(PS[:, 4 + t // 4, P * (t % 4):P * (t % 4) + P], dv[:, P * t:P * t + P], k["Wo"][:, :],
                                 start=True, stop=True, skip_group_check=True)
                    ins.then_inc(S["wo"], 1)

                for k_ in range(KS + 1):
                    mix_part(0, k_)
                operands(0, True)
                core(0, True, False)
                gather_out(0)
                with pe.Fori(1, BATCH - 1) as b:
                    operands(b, False)
                    core(b, False, False)
                    gather_out(b)
                operands(BATCH - 1, False)
                core(BATCH - 1, False, True)
                gather_out(BATCH - 1)

            @block.vector
            def _(dve):
                TT, TS, STT = nc.vector.tensor_tensor, nc.vector.tensor_scalar, nc.vector.scalar_tensor_tensor

                def mix_part(st, b, k_):
                    if k_ == 0:
                        for t in range(TILES):
                            n = b * TILES + t
                            TS(X2[:, n, :], H[:, n, :], mean[:, bass.ds(n, 1)], rstd[:, bass.ds(n, 1)], ALU.subtract, ALU.mult)
                            ins = TS(xn[:, t, :], H[:, n, :], mean[:, bass.ds(n, 1)], rstd2[:, bass.ds(n, 1)], ALU.subtract, ALU.mult)
                        ins.then_inc(S["xn"], 1)
                    if k_ in (3, 4):
                        if k_ == 3:
                            dve.wait_ge(S["diff"], b + 1)
                        for j in range(2 * (k_ - 3), 2 * (k_ - 3) + 2):
                            STT(out=xm[j][:, :], in0=diff, scalar=(k["tm_q"], k["tm_k"], k["tm_v"], k["tm_g"])[j], in1=hs[:, 0:SEQ],
                                op0=ALU.mult, op1=ALU.add).then_inc(S["mix"], 1)
                    if k_ == 6:
                        dve.wait_ge(S["ss"], b + 1)
                        TS(ssv[:, :], PS[:, 6, 0:16], 1.0 / D, None, ALU.mult).then_inc(S["ssv"], 1)
                    if k_ == 7:
                        dve.wait_ge(S["root"], b + 1)
                        st.link(TS(root[:, :], root[:, :], 1e-8, None, ALU.add))
                        nc.vector.reciprocal(ssv[:, :], root[:, :]).then_inc(S["rms"], 1)
                    if k_ == 8:
                        for j in range(4):
                            a, c = (q, kk)[j // 2], slice(HALF * (j % 2), HALF * (j % 2) + HALF)
                            dve.wait_ge(S["rb"], 4 * b + j + 1)
                            TT(a[:, c], a[:, c], PS[:, (6, 7, 0, 1)[j], :], ALU.mult).then_inc(S["qn"], 1)

                def operands(b, first):
                    st = Steps(dve, S["dveO"], b, 10)
                    dve.wait_ge(S["exp"], 2 * b + 2)
                    st.link(nc.vector.tensor_tensor_scan(z[:, :], pw[:, 1:2].broadcast_to([P, SEQ]), kk[:, :], 0.0, ALU.mult, ALU.add))
                    pair = lambda d: STT(out=blocks_out(d), in0=blocks(q[:, :])[:, :, d:NEAR], scalar=pw[:, d:d + 1],
                                         in1=blocks(kk[:, :])[:, :, 0:NEAR - d], op0=ALU.mult, op1=ALU.mult)
                    blocks_out = lambda d: near[d].rearrange("p (n c) -> p n c", c=NEAR - d)
                    pair(1).then_inc(S["near1"], 1)
                    st.link(TT(qz[:, :], q[:, :], z[:, :], ALU.mult))
                    pair(2)
                    pair(3).then_inc(S["qz"], 1)
                    for l, h in enumerate(LEVELS):
                        ins = TT(qc[:, l, :].rearrange("p (n c) -> p n c", c=h), right(q[:, :], h),
                                 pw[:, 0:h].unsqueeze(1).broadcast_to([P, SEQ // (2 * h), h]), ALU.mult)
                    ins.then_inc(S["qc"], 1)
                    dve.wait_ge(S["nearp"], 3 * b + 1)
                    dve.wait_ge(S["vTsb"], b + 1)
                    TT(dv[:, :], vT[:, :], two_banks(6), ALU.mult).then_inc(S["nearc"], 1)
                    later = lambda d, t: blocks(t)[:, :, d:NEAR]
                    earlier = lambda d: blocks(vT[:, :])[:, :, 0:NEAR - d]
                    cut = lambda d, t: t.rearrange("p (n c) -> p n c", c=NEAR - d)
                    dve.wait_ge(S["nearp"], 3 * b + 2)
                    TT(cut(1, tmp), cut(1, two_banks(0, n_near(1))), earlier(1), ALU.mult).then_inc(S["nearc"], 1)
                    dve.wait_ge(S["nearc"], 3 * b + 2)
                    st.link(TT(later(1, dv[:, :]), later(1, dv[:, :]), cut(1, tmp), ALU.add))
                    dve.wait_ge(S["u"], b + 1)
                    TT(state[:, 1:TILES, :], two_banks(2, P * (TILES - 1)).rearrange("p (n c) -> p n c", c=P),
                       heads[:, :].unsqueeze(1).broadcast_to([P, TILES - 1, P]), ALU.mult).then_inc(S["um"], 1)
                    dve.wait_ge(S["um"], b + 1)
                    for n in range(1, TILES - 1):
                        ins = STT(out=state[:, n + 1, :], in0=state[:, n, :], scalar=pw[:, P:P + 1], in1=state[:, n + 1, :], op0=ALU.mult, op1=ALU.add)
                        if n < TILES - 2:
                            st.link(ins)
                        else:
                            ins.then_inc(S["state"], 1)
                    dve.wait_ge(S["Zs"], b + 1)
                    nc.vector.reciprocal(rz[:, :], PS[:, 0, 0:TILES * HEADS]).then_inc(S["rz"], 1)
                    dve.wait_ge(S["nearp"], 3 * b + 3)
                    tmp2, tmp3 = tmp[:, 0:n_near(2)], tmp[:, n_near(2):n_near(1)]
                    TT(cut(2, tmp2), cut(2, PS[:, 6, :]), earlier(2), ALU.mult)
                    TT(cut(3, tmp3), cut(3, PS[:, 7, 0:n_near(3)]), earlier(3), ALU.mult).then_inc(S["nearc"], 1)
                    dve.wait_ge(S["nearc"], 3 * b + 3)
                    st.link(TT(later(2, dv[:, :]), later(2, dv[:, :]), cut(2, tmp2), ALU.add))
                    st.link(TT(later(3, dv[:, :]), later(3, dv[:, :]), cut(3, tmp3), ALU.add))
                    dve.wait_ge(S["rzb"], b + 1)
                    dve.wait_ge(S["gsb"], b + 1)
                    STT(out=rg[:, :], in0=rg[:, :], scalar=1.0, in1=two_banks(2), op0=ALU.add, op1=ALU.mult).then_inc(S["rg"], 1)
                    st.close()

                def core(b, last):
                    st = Steps(dve, S["dveC"], b, 1)
                    stm = Steps(dve, S["dveM"], b + 1, 1)
                    for k_ in range(KS):
                        lo, hi = STEP[k_ % 2]
                        for name, h0, h1 in (("A", 0, 2), ("B", 2, HEADS)):
                            dve.wait_ge(S["score" + name], KS * b + k_ + 1)
                            if k_ >= 2:
                                dve.wait_ge(S["av"], KS * b + k_ - 1)
                            TT(pm[k_ % 2][:, h0:h1, :], PS[:, h0:h1, 0:(hi - lo) * P],
                               see[:, P * lo:P * hi].unsqueeze(1).broadcast_to([P, h1 - h0, (hi - lo) * P]), ALU.mult).then_inc(S["mask" + name], 1)
                        if not last:
                            mix_part(stm, b + 1, k_)
                    if not last:
                        mix_part(stm, b + 1, KS)
                    dve.wait_ge(S["av"], KS * b + KS)
                    dve.wait_ge(S["rg"], b + 1)
                    st.link(TT(dv[:, :], dv[:, :], two_banks(4), ALU.add))
                    TT(dv[:, :], dv[:, :], rg[:, :], ALU.mult).then_inc(S["att"], 1)

                def add_out(b):
                    dve.wait_ge(S["wo"], b + 1)
                    for j in range(2):
                        n = bass.ds(b * TILES + 4 * j, 4)
                        TT(X2[:, n, :], X2[:, n, :], PS[:, 4 + j, :].rearrange("p (a b) -> p a b", a=4), ALU.add).then_inc(S["x2"], 1)

                nc.vector.memset(hs[:, 0:1], 0.0)
                nc.vector.memset(state[:, 0, :], 0.0)
                TS(lnl[:, 0:1], k["time_decay"], 80.0, None, ALU.min).then_inc(S["lam"], 1)
                dve.wait_ge(S["lam"], 2)
                TS(lnl[:, 0:1], lnl[:, 1:2], -1.0, -1e4, ALU.mult, ALU.max).then_inc(S["lam"], 1)
                dve.wait_ge(S["lam"], 4)
                dve.wait_ge(S["in"], 80)
                st0 = Steps(dve, S["dveM"], 0, 1)
                for k_ in range(KS + 1):
                    mix_part(st0, 0, k_)
                operands(0, True)
                core(0, False)
                with dve.Fori(1, BATCH - 1) as b:
                    add_out(b - 1)
                    operands(b, False)
                    core(b, False)
                add_out(BATCH - 2)
                operands(BATCH - 1, False)
                core(BATCH - 1, True)
                add_out(BATCH - 1)


BF16 = mybir.dt.bfloat16
EXPERTS, FF, CAP = 8, 512, 1024
NBLK = CAP // P
ROW = P + EXPERTS


def row_stats(nc, k, src, mean, rstd, tag):
    with ExitStack() as ctx:
        m = Mem(nc, ctx, tag, k["banks"])
        stats = m.sb("stats", [P, NT, 6])
        var, sq, expo = m.sb("var", [P, NT]), m.sb("sq", [P, NT]), m.sb("expo", [P, NT])
        s_stats, s_dve, s_var, s_out = m.sem("stats"), m.sem("dve"), m.sem("var"), m.sem("rstd")
        with nc.Block() as block:
            @block.vector
            def _(dve):
                nc.vector.memset(expo[:, :], -0.5)
                with dve.Fori(0, NT // 4) as i:
                    for t in range(4):
                        ins = nc.vector.bn_stats(stats[:, i * 4 + t, :], src[:, i * 4 + t, :])
                    ins.then_inc(s_stats, 1)
                dve.wait_ge(s_stats, NT // 4)
                merge_stats(nc, Steps(dve, s_dve), stats[:, :, :], mean[:, :], sq[:, :], var[:, :]).then_inc(s_var, 1)

            @block.gpsimd
            def _(pool):
                pool.wait_ge(s_var, 1)
                nc.gpsimd.tensor_tensor(rstd[:, :], var[:, :], expo[:, :], ALU.pow).then_inc(s_out, 1)


def mlp(nc, w, k, H, X2, mean, rstd):
    with ExitStack() as ctx:
        m = Mem(nc, ctx, "mlp", k["banks"])
        xn = [m.sb(f"xn{u}", [P, 4, P]) for u in range(2)]
        hT = [m.sb(f"hT{u}", [P, HALF]) for u in range(2)]
        hid = [m.sb(f"hid{u}", [P, 4, HALF]) for u in range(2)]
        pt = [m.ps() for u in range(2)]
        pf = [m.ps() for f in range(4)]
        po = [m.ps((P, 4, P)) for u in range(2)]
        two = lambda n: [m.sem(f"{n}{u}") for u in range(2)]
        s_xn, s_turned, s_h, s_up, s_gelu, s_down, s_out = (two(n) for n in ("xn", "turned", "h", "up", "gelu", "down", "out"))
        s_dve = m.sem("dve")
        reset_used(nc)
        G = NT // 4
        with nc.Block() as block:
            @block.vector
            def _(dve):
                for i in passes(dve, G // 2):
                    st = Steps(dve, s_dve, i, 2)
                    for u in range(2):
                        dve.wait_ge(s_turned[u], i)
                        for t in range(4):
                            n = (i * 2 + u) * 4 + t
                            ins = nc.vector.tensor_scalar(xn[u][:, t, :], X2[:, n, :], mean[:, bass.ds(n, 1)], rstd[:, bass.ds(n, 1)],
                                                          ALU.subtract, ALU.mult)
                        ins.then_inc(s_xn[u], 1)
                    for u in range(2):
                        g = bass.ds((i * 2 + u) * 4, 4)
                        st.link(nc.vector.tensor_tensor(H[:, g, :], H[:, g, :], X2[:, g, :], ALU.add))
                        dve.wait_ge(s_down[u], i + 1)
                        nc.vector.tensor_tensor(H[:, g, :], H[:, g, :], po[u][:, :, :], ALU.add).then_inc(s_out[u], 1)
                    st.close()

            @block.scalar
            def _(act):
                for i in passes(act, G // 2):
                    for u in range(2):
                        act.wait_ge(s_turned[u], i + 1)
                        act.wait_ge(s_up[u], 4 * i)
                        nc.scalar.activation(hT[u][:, :], pt[u][:, :], ACT.Identity, bias=k["ln2_b"], scale=k["ln2_g"]).then_inc(s_h[u], 1)
                    for u in range(2):
                        act.wait_ge(s_down[u], i)
                        for f in range(4):
                            act.wait_ge(s_up[u], 4 * i + f + 1)
                            nc.scalar.activation(hid[u][:, f, :], pf[f][:, :], ACT.Gelu).then_inc(s_gelu[u], 1)

            @block.tensor
            def _(pe):
                for i in passes(pe, G // 2):
                    for u in range(2):
                        pe.wait_ge(s_xn[u], i + 1)
                        pe.wait_ge(s_h[u], i)
                        for t in range(4):
                            ins = nc.tensor.transpose(pt[u][:, P * t:P * t + P], xn[u][:, t, :], k["ident"][:, :])
                        ins.then_inc(s_turned[u], 1)
                    for u in range(2):
                        pe.wait_ge(s_h[u], i + 1)
                        for f in range(4):
                            pe.wait_ge(s_gelu[1 - u], 4 * i + f + 1 if u else 4 * i)
                            nc.tensor.matmul(pf[f][:, :], k["W1T"][:, P * f:P * f + P], hT[u][:, :], start=True, stop=True).then_inc(s_up[u], 1)
                    for u in range(2):
                        pe.wait_ge(s_gelu[u], 4 * i + 4)
                        pe.wait_ge(s_out[u], i)
                        for t in range(4):
                            for f in range(4):
                                ins = nc.tensor.matmul(po[u][:, t, :], hid[u][:, f, P * t:P * t + P], k["W2T"][:, f, :],
                                                       start=(f == 0), stop=(f == 3), skip_group_check=True)
                        ins.then_inc(s_down[u], 1)


def moe_tables():
    tri = np.triu(np.ones((P, P), np.float32), 1)
    nt = np.zeros((P, 2 * NT), np.float32)
    nt[:, 0:NT] = np.arange(NT)
    nt[:, NT:] = np.arange(P)[:, None]
    io = np.zeros((P, P), np.float32) + np.arange(P, dtype=np.float32)
    return {"c_before": tri, "c_ids": nt, "c_iota": io}


def moe_route(nc, w, k, H, mean, rstd, rows, acc, lists):
    with ExitStack() as ctx:
        m = Mem(nc, ctx, "rt", k["banks"])
        Wr = m.sb("Wr", [P, EXPERTS])
        before, ids, iota = m.sb("before", [P, P]), m.sb("ids", [P, 2 * NT]), m.sb("iota", [P, P])
        xn = [m.sb(f"xn{u}", [P, 4, P]) for u in range(2)]
        xT = [m.sb(f"xT{u}", [P, HALF]) for u in range(2)]
        E8 = lambda n, dt=F32: m.sb(n, [P, EXPERTS], dt)
        EN = lambda n, dt=F32: m.sb(n, [P, EXPERTS, NT], dt)
        lg, below, mask, eq, pref, tot = EN("lg"), EN("below"), EN("mask"), EN("eq"), EN("pref"), EN("tot")
        expo, prob = EN("expo"), m.sb("prob", [P, NT, EXPERTS])
        part, blk = EN("part"), EN("blk")
        posi, parti, blki = EN("posi", I32), EN("parti", I32), EN("blki", I32)
        mx, cnt, rs, need = E8("mx"), E8("cnt"), E8("rs"), E8("need")
        mx8, dg = m.sb("mx8", [EXPERTS, 1]), m.sb("dg", [EXPERTS, EXPERTS])
        thr, cand, bit, take = E8("thr", I32), E8("cand", I32), E8("bit", I32), E8("take", I32)
        onep = [m.sb(f"onep{u}", [P, 8, P], BF16) for u in range(2)]
        oneb = m.sb("oneb", [P, NT, 8])
        rhs = m.sb("rhs", [P, NT, 16], BF16)
        half_id = m.sb("half_id", [P, 16])
        idf = m.sb("idf", [P, 8])
        pt = [m.ps() for u in range(2)]
        pl = [m.ps((P, 4, EXPERTS)) for u in range(2)]
        pa, pb, pc, pd = m.ps(), m.ps(), m.ps(), m.ps()
        two = lambda n: [m.sem(f"{n}{u}") for u in range(2)]
        s_xn, s_turned, s_xT, s_lg, s_lgc, s_row = (two(n) for n in ("xn", "turned", "xT", "lg", "lgc", "row"))
        s_in, s_pe, s_dve, s_act, s_acc, s_dve2, s_cnt, s_mask, s_list, s_listc, s_dve3 = (m.sem(n) for n in (
            "in", "pe", "dve", "act", "acc", "dve2", "cnt", "mask", "list", "listc", "dve3"))
        s_dve3b, s_dve4 = m.sem("dve3b"), m.sem("dve4")
        s_onep = two("onep")
        s_oused = two("oused")
        G = NT // 4
        rows_v = rows.rearrange("(n p) c -> p n c", p=P)
        acc_v = acc.rearrange("(n p) c -> p n c", p=P)
        with nc.Block() as block:
            @block.sync
            def _(sp):
                for dst, src in ((Wr, "L0_ffn_Wr"), (before, "c_before"), (ids, "c_ids"), (iota, "c_iota")):
                    sp.dma_start(dst[:, :], w[src]).then_inc(s_in, 16)
                sp.dma_start(acc_v, H[:, :, :]).then_inc(s_acc, 16)
                for i in passes(sp, G // 2):
                    for u in range(2):
                        sp.wait_ge(s_xn[u], i + 1)
                        sp.dma_start(rows_v[:, bass.ds((i * 2 + u) * 4, 4), 0:P], xn[u][:, :, :]).then_inc(s_row[u], 16)
                for u in range(2):
                    sp.wait_ge(s_row[u], 16 * G // 2)
                sp.wait_ge(s_acc, 16)
                sp.wait_ge(s_in, 64)

            @block.vector
            def _(dve):
                for i in passes(dve, G // 2):
                    for u in range(2):
                        dve.wait_ge(s_turned[u], i)
                        dve.wait_ge(s_row[u], 16 * i)
                        for t in range(4):
                            n = (i * 2 + u) * 4 + t
                            ins = nc.vector.tensor_scalar(xn[u][:, t, :], H[:, n, :], mean[:, bass.ds(n, 1)], rstd[:, bass.ds(n, 1)],
                                                          ALU.subtract, ALU.mult)
                        ins.then_inc(s_xn[u], 1)
                    for u in range(2):
                        dve.wait_ge(s_lg[u], i + 1)
                        nc.vector.tensor_copy(lg[:, :, bass.ds((i * 2 + u) * 4, 4)], pl[u][:, :, :].rearrange("p t e -> p e t")).then_inc(s_lgc[u], 1)

            @block.scalar
            def _(act):
                for i in passes(act, G // 2):
                    for u in range(2):
                        act.wait_ge(s_turned[u], i + 1)
                        act.wait_ge(s_lg[u], i)
                        nc.scalar.copy(xT[u][:, :], pt[u][:, :]).then_inc(s_xT[u], 1)

            @block.tensor
            def _(pe):
                pe.wait_ge(s_in, 64)
                for i in passes(pe, G // 2):
                    for u in range(2):
                        pe.wait_ge(s_xn[u], i + 1)
                        pe.wait_ge(s_xT[u], i)
                        for t in range(4):
                            ins = nc.tensor.transpose(pt[u][:, P * t:P * t + P], xn[u][:, t, :], k["ident"][:, :])
                        ins.then_inc(s_turned[u], 1)
                    for u in range(2):
                        pe.wait_ge(s_xT[u], i + 1)
                        pe.wait_ge(s_lgc[u], i)
                        for t in range(4):
                            ins = nc.tensor.matmul(pl[u][:, t, :], xT[u][:, P * t:P * t + P], Wr[:, :], start=True, stop=True, skip_group_check=True)
                        ins.then_inc(s_lg[u], 1)
        flat = lambda t: t[:, :, :].rearrange("p a b -> p (a b)")
        ROUNDS = 31
        with nc.Block() as block:
            @block.tensor
            def _(pe):
                pe.wait_ge(s_dve, 1)
                nc.tensor.transpose(pa[0:EXPERTS, 0:P], mx[:, :], k["ident"][:, :]).then_inc(s_pe, 1)
                pe.wait_ge(s_dve, 3)
                nc.tensor.matmul(pb[:, 0:EXPERTS], k["ones"][0:EXPERTS, :], dg[:, :], start=True, stop=True).then_inc(s_pe, 1)
                pe.wait_ge(s_dve, 5)
                nc.tensor.matmul(pa[:, 0:EXPERTS], k["ones"][:, :], cnt[:, :], start=True, stop=True).then_inc(s_pe, 1)
                with pe.Fori(0, ROUNDS) as r:
                    pe.wait_ge(s_cnt, r + 1)
                    nc.tensor.matmul(pb[:, 0:EXPERTS], k["ones"][:, :], cnt[:, :], start=True, stop=True).then_inc(s_mask, 1)
                pe.wait_ge(s_dve2, 1)
                nc.tensor.matmul(pa[:, 0:EXPERTS], k["ones"][:, :], cnt[:, :], start=True, stop=True)
                nc.tensor.matmul(pc[:, :], before[:, :], flat(eq), start=True, stop=True)
                nc.tensor.matmul(pd[:, :], k["ones"][:, :], flat(eq), start=True, stop=True).then_inc(s_pe, 1)
                pe.wait_ge(s_dve2, 3)
                nc.tensor.matmul(pa[:, :], before[:, :], flat(mask), start=True, stop=True)
                nc.tensor.matmul(pb[:, :], k["ones"][:, :], flat(mask), start=True, stop=True).then_inc(s_pe, 1)

            @block.scalar
            def _(act):
                act.wait_ge(s_dve, 4)
                nc.scalar.activation(flat(expo), flat(below), ACT.Exp, scale=-1.0).then_inc(s_act, 1)

            @block.vector
            def _(dve):
                st = Steps(dve, s_dve)
                st.link(nc.vector.tensor_reduce(mx[:, :], lg[:, :, :], AX.X, ALU.max))
                dve.wait_ge(s_pe, 1)
                st.link(nc.vector.tensor_reduce(mx8[:, :], pa[0:EXPERTS, 0:P], AX.X, ALU.max))
                st.link(nc.vector.tensor_scalar(dg[:, :], k["ident"][0:EXPERTS, 0:EXPERTS], mx8[:, 0:1], None, ALU.mult))
                dve.wait_ge(s_pe, 2)
                nc.vector.tensor_copy(mx[:, :], pb[:, 0:EXPERTS]).then_inc(s_dve3, 1)
                dve.wait_ge(s_dve3, 1)
                st.link(nc.vector.tensor_tensor(below[:, :, :], spread(mx[:, :], NT), lg[:, :, :], ALU.subtract))
                dve.wait_ge(s_act, 1)
                st.link(nc.vector.tensor_reduce(cnt[:, :], expo[:, :, :], AX.X, ALU.add))
                dve.wait_ge(s_pe, 3)
                st.link(nc.vector.reciprocal(rs[:, :], pa[:, 0:EXPERTS]))
                st.link(nc.vector.tensor_tensor(prob[:, :, :], expo[:, :, :].rearrange("p e t -> p t e"),
                                                rs[:, :].unsqueeze(1).broadcast_to([P, NT, EXPERTS]), ALU.mult))
                nc.vector.memset(lists[:, EXPERTS, :], 0)
                nc.vector.memset(thr[:, :], 0)
                st.link(nc.vector.memset(bit[:, :], 1 << 30))
                st.link(nc.vector.tensor_tensor(cand[:, :], thr[:, :], bit[:, :], ALU.bitwise_or))
                with dve.Fori(0, ROUNDS) as r:
                    s2 = Steps(dve, s_dve3b, r, 5)
                    s2.link(nc.vector.tensor_tensor(mask[:, :, :], below[:, :, :], spread(cand[:, :].bitcast(F32), NT), ALU.is_lt))
                    nc.vector.tensor_reduce(cnt[:, :], mask[:, :, :], AX.X, ALU.add).then_inc(s_cnt, 1)
                    dve.wait_ge(s_mask, r + 1)
                    s2.link(nc.vector.scalar_tensor_tensor(out=take[:, :], in0=pb[:, 0:EXPERTS], scalar=float(CAP), in1=bit[:, :],
                                                           op0=ALU.is_lt, op1=ALU.mult))
                    s2.link(nc.vector.tensor_tensor(thr[:, :], thr[:, :], take[:, :], ALU.bitwise_or))
                    s2.link(nc.vector.tensor_scalar(bit[:, :], bit[:, :], 1, None, ALU.logical_shift_right))
                    s2.link(nc.vector.tensor_tensor(cand[:, :], thr[:, :], bit[:, :], ALU.bitwise_or))
                    s2.close()
                T = spread(thr[:, :].bitcast(F32), NT)
                nc.vector.tensor_tensor(eq[:, :, :], below[:, :, :], T, ALU.is_equal)
                st.link(nc.vector.tensor_tensor(mask[:, :, :], below[:, :, :], T, ALU.is_lt))
                nc.vector.tensor_reduce(cnt[:, :], mask[:, :, :], AX.X, ALU.add).then_inc(s_dve2, 1)
                dve.wait_ge(s_pe, 4)
                nc.vector.tensor_scalar(need[:, :], pa[:, 0:EXPERTS], -1.0, float(CAP), ALU.mult, ALU.add)

                def ahead(within, whole):
                    st.link(nc.vector.tensor_copy(flat(tot), whole))
                    for e in range(EXPERTS):
                        ins = nc.vector.tensor_tensor_scan(pref[:, e, :], k["ones"][:, 0:1].broadcast_to([P, NT]), tot[:, e, :], 0.0, ALU.mult, ALU.add)
                    st.link(ins)
                    st.link(nc.vector.tensor_tensor(flat(pref), flat(pref), flat(tot), ALU.subtract))
                    st.link(nc.vector.tensor_tensor(flat(pref), flat(pref), within, ALU.add))

                ahead(pc[:, :], pd[:, :])
                st.link(nc.vector.tensor_tensor(pref[:, :, :], pref[:, :, :], spread(need[:, :], NT), ALU.is_lt))
                st.link(nc.vector.tensor_tensor(eq[:, :, :], eq[:, :, :], pref[:, :, :], ALU.mult))
                nc.vector.tensor_copy(idf[:, :], need[:, :]).then_inc(s_dve2, 1)
                nc.vector.tensor_tensor(mask[:, :, :], mask[:, :, :], eq[:, :, :], ALU.add).then_inc(s_dve2, 1)
                dve.wait_ge(s_pe, 5)
                ahead(pa[:, :], pb[:, :])
                st.link(nc.vector.tensor_scalar(flat(eq), flat(mask), -65536.0, 65536.0, ALU.mult, ALU.add))
                st.link(nc.vector.tensor_tensor(flat(posi), flat(pref), flat(eq), ALU.add))
                nc.vector.tensor_scalar(flat(parti), flat(posi), P - 1, None, ALU.bitwise_and)
                st.link(nc.vector.tensor_scalar(flat(blki), flat(posi), 7, None, ALU.logical_shift_right))
                nc.vector.tensor_copy(flat(part), flat(parti))
                st.link(nc.vector.tensor_copy(flat(blk), flat(blki)))

            @block.sync
            def _(sp):
                sp.wait_ge(s_dve, 7)
                sp.dma_start(rows_v[:, :, P:ROW], prob[:, :, :]).then_inc(s_in, 16)
                sp.wait_ge(s_in, 80)
        with nc.Block() as block:
            @block.vector
            def _(dve):
                for e in passes(dve, EXPERTS):
                    st = Steps(dve, s_dve4, e, 4)
                    st.link(nc.vector.tensor_tensor(oneb[:, :, :], iota[:, 0:8].unsqueeze(1).broadcast_to([P, NT, 8]),
                                                    spread(blk[:, e, :], 8), ALU.is_equal))
                    dve.wait_ge(s_list, e)
                    nc.vector.tensor_tensor(rhs[:, :, 0:8], oneb[:, :, :], spread(ids[:, 0:NT], 8), ALU.mult)
                    st.link(nc.vector.tensor_tensor(rhs[:, :, 8:16], oneb[:, :, :], spread(ids[:, NT:2 * NT], 8), ALU.mult))
                    for c in range(NT // 8):
                        dve.wait_ge(s_oused[c % 2], 4 * e + c // 2)
                        nc.vector.tensor_tensor(onep[c % 2][:, :, :], iota[:, :].unsqueeze(1).broadcast_to([P, 8, P]),
                                                spread(part[:, e, bass.ds(8 * c, 8)], P), ALU.is_equal).then_inc(s_onep[c % 2], 1)
                    dve.wait_ge(s_list, e + 1)
                    st.link(nc.vector.tensor_copy(half_id[:, :], pa[:, 0:16]))
                    st.link(nc.vector.scalar_tensor_tensor(out=lists[:, e, :], in0=half_id[:, 0:8], scalar=float(P), in1=half_id[:, 8:16],
                                                           op0=ALU.mult, op1=ALU.add))
                    st.close()

            @block.tensor
            def _(pe):
                for e in passes(pe, EXPERTS):
                    pe.wait_ge(s_dve4, 4 * e + 2)
                    for c in range(NT // 8):
                        pe.wait_ge(s_onep[c % 2], 4 * e + c // 2 + 1)
                        for t in range(8):
                            n = 8 * c + t
                            ins = nc.tensor.matmul(pa[:, 0:16], onep[c % 2][:, t, :], rhs[:, n, :], start=(n == 0), stop=(n == NT - 1))
                        if c < NT // 8 - 1:
                            ins.then_inc(s_oused[c % 2], 1)
                    ins.then_inc(s_oused[(NT // 8 - 1) % 2], 1)
                    nc.tensor.matmul(pb[0:1, 0:1], rhs[:, 0, 0:1], rhs[:, 0, 0:1], start=True, stop=True).then_inc(s_list, 1)


def moe_experts(nc, w, k, rows, acc, lists):
    with ExitStack() as ctx:
        m = Mem(nc, ctx, "ex", k["banks"])
        two = lambda n: [m.sem(f"{n}{u}") for u in range(2)]
        W1 = [m.sb(f"W1{u}", [P, FF]) for u in range(2)]
        W2 = [m.sb(f"W2{u}", [P, 4, D]) for u in range(2)]
        bs = [m.sb(f"bs{u}", [P, 4]) for u in range(2)]
        b1r, b1 = m.sb("b1r", [EXPERTS * 4, P]), m.sb("b1", [P, EXPERTS * 4])
        b2 = [m.sb(f"b2{u}", [1, D]) for u in range(2)]
        idx = [m.sb(f"idx{u}", [P, NBLK], U32) for u in range(2)]
        sel = [m.sb(f"sel{u}", [P, NBLK, ROW]) for u in range(2)]
        selT = [m.sb(f"selT{u}", [P, HALF]) for u in range(2)]
        hid = [m.sb(f"hid{u}", [P, 4, HALF]) for u in range(2)]
        y = [m.sb(f"y{u}", [P, NBLK, D]) for u in range(2)]
        wt = [m.sb(f"wt{u}", [P, NBLK]) for u in range(2)]
        pt = [m.ps() for u in range(2)]
        pf = [m.ps() for f in range(4)]
        po = [m.ps((P, 4, P)) for u in range(2)]
        s_w, s_idx, s_gather, s_used, s_y, s_scatter, s_down_e = (two(n) for n in ("w", "idx", "gather", "used", "y", "scatter", "down_e"))
        s_turned, s_selT, s_up, s_gelu, s_down, s_out = (two(n) for n in ("turned", "selT", "up", "gelu", "down", "out"))
        s_wt = two("wt")
        W1_d, W2_d = w["L0_ffn_W1"], w["L0_ffn_W2"]
        s_b1 = m.sem("b1")
        with nc.Block() as block:
            @block.sync
            def _(sp):
                sp.dma_start(b1r[:, :], w["L0_ffn_b1"].rearrange("e (f p) -> (e f) p", p=P)).then_inc(s_b1, 16)

            @block.tensor
            def _(pe):
                pe.wait_ge(s_b1, 16)
                nc.tensor.transpose(pt[0][:, 0:EXPERTS * 4], b1r[:, :], k["ident"][0:EXPERTS * 4, 0:EXPERTS * 4]).then_inc(s_b1, 1)

            @block.vector
            def _(dve):
                dve.wait_ge(s_b1, 17)
                nc.vector.tensor_copy(b1[:, :], pt[0][:, 0:EXPERTS * 4]).then_inc(s_b1, 1)
        with nc.Block() as block:
            @block.sync
            def _(sp):
                for i in passes(sp, EXPERTS // 2):
                    for u in range(2):
                        e = bass.ds(i * 2 + u, 1)
                        sp.wait_ge(s_down_e[u], i)
                        sp.dma_start(W1[u][:, :], W1_d[e].rearrange("a d f -> (a d) f")).then_inc(s_w[u], 16)
                        sp.dma_start(W2[u][:, :, :], W2_d[e].rearrange("a (f p) d -> p (a f) d", p=P)).then_inc(s_w[u], 16)
                        sp.dma_start(b2[u][:, :], w["L0_ffn_b2"][e, :]).then_inc(s_w[u], 16)
                for u in range(2):
                    sp.wait_ge(s_w[u], 48 * EXPERTS // 2)

            @block.gpsimd
            def _(pool):
                def gather(u, n):
                    pool.wait_ge(s_idx[u], n + 1)
                    for c in range(NBLK):
                        nc.gpsimd.indirect_dma_start(sel[u][:, c, :], None, rows, bass.IndirectOffsetOnAxis(ap=idx[u][:, c:c + 1], axis=0)
                                                     ).then_inc(s_gather[u], 16)

                gather(0, 0)
                for i in range(EXPERTS // 2):
                    gather(1, i)
                    for u in range(2):
                        pool.wait_ge(s_y[u], i + 1)
                        if u:
                            pool.wait_ge(s_scatter[0], 16 * NBLK * (i + 1))
                        elif i:
                            pool.wait_ge(s_scatter[1], 16 * NBLK * i)
                        for c in range(NBLK):
                            nc.gpsimd.indirect_dma_start(acc, bass.IndirectOffsetOnAxis(ap=idx[u][:, c:c + 1], axis=0), y[u][:, c, :], None,
                                                         compute_op=ALU.add).then_inc(s_scatter[u], 16)
                        if u == 0 and i < EXPERTS // 2 - 1:
                            gather(0, i + 1)
                pool.wait_ge(s_scatter[1], 16 * NBLK * EXPERTS // 2)

            @block.vector
            def _(dve):
                nc.vector.tensor_copy(idx[0][:, :], lists[:, 0, :]).then_inc(s_idx[0], 1)
                for i in passes(dve, EXPERTS // 2):
                    dve.wait_ge(s_scatter[1], 16 * NBLK * i)
                    nc.vector.tensor_copy(idx[1][:, :], lists[:, i * 2 + 1, :]).then_inc(s_idx[1], 1)
                    for u in range(2):
                        dve.wait_ge(s_gather[u], 16 * NBLK * (i + 1))
                        dve.wait_ge(s_scatter[u], 16 * NBLK * i)
                        nc.vector.tensor_copy(bs[u][:, :], b1[:, bass.ds((i * 2 + u) * 4, 4)])
                        nc.vector.tensor_copy(wt[u][:, :], sel[u][:, :, bass.ds(i * 2 + (P + u), 1)].rearrange("p a b -> p (a b)")).then_inc(s_wt[u], 1)
                        dve.wait_ge(s_wt[u], i + 1)
                        for h in range(2):
                            dve.wait_ge(s_down[h], 2 * i + u + 1)
                            for t in range(4):
                                c = 4 * h + t
                                ins = nc.vector.tensor_scalar(y[u][:, c, :], po[h][:, t, :], wt[u][:, c:c + 1], None, ALU.mult)
                            ins.then_inc(s_out[h], 1)
                        dve.wait_ge(s_out[1], 2 * i + u + 1)
                        nc.vector.tensor_copy(y[u][0:1, 0, 0:1], y[u][0:1, 0, 0:1]).then_inc(s_y[u], 1)
                        if u == 0:
                            dve.wait_ge(s_scatter[0], 16 * NBLK * (i + 1))
                            nc.vector.tensor_copy(idx[0][:, :], lists[:, NEXT(i), :]).then_inc(s_idx[0], 1)

            @block.scalar
            def _(act):
                for i in passes(act, EXPERTS // 2):
                    for u in range(2):
                        for h in range(2):
                            act.wait_ge(s_turned[h], 2 * i + u + 1)
                            act.wait_ge(s_up[h], 4 * (2 * i + u))
                            nc.scalar.copy(selT[h][:, :], pt[h][:, :]).then_inc(s_selT[h], 1)
                        act.wait_ge(s_wt[u], i + 1)
                        for h in range(2):
                            act.wait_ge(s_down[h], 2 * i + u)
                            for f in range(4):
                                act.wait_ge(s_up[h], 4 * (2 * i + u) + f + 1)
                                nc.scalar.activation(hid[h][:, f, :], pf[f][:, :], ACT.Gelu, bias=bs[u][:, f:f + 1]).then_inc(s_gelu[h], 1)

            @block.tensor
            def _(pe):
                for i in passes(pe, EXPERTS // 2):
                    for u in range(2):
                        n = 2 * i + u
                        pe.wait_ge(s_gather[u], 16 * NBLK * (i + 1))
                        pe.wait_ge(s_w[u], 48 * (i + 1))
                        for h in range(2):
                            pe.wait_ge(s_selT[h], n)
                            for t in range(4):
                                ins = nc.tensor.transpose(pt[h][:, P * t:P * t + P], sel[u][:, 4 * h + t, 0:P], k["ident"][:, :])
                            ins.then_inc(s_turned[h], 1)
                        for h in range(2):
                            pe.wait_ge(s_selT[h], n + 1)
                            for f in range(4):
                                pe.wait_ge(s_gelu[1 - h], 4 * n + f + 1 if h else 4 * n)
                                nc.tensor.matmul(pf[f][:, :], W1[u][:, P * f:P * f + P], selT[h][:, :], start=True, stop=True).then_inc(s_up[h], 1)
                        for h in range(2):
                            pe.wait_ge(s_gelu[h], 4 * n + 4)
                            pe.wait_ge(s_out[h], n)
                            for t in range(4):
                                for f in range(4):
                                    nc.tensor.matmul(po[h][:, t, :], hid[h][:, f, P * t:P * t + P], W2[u][:, f, :],
                                                     start=(f == 0), stop=False, skip_group_check=True)
                                ins = nc.tensor.matmul(po[h][:, t, :], k["ones"][0:1, :], b2[u][:, :], start=False, stop=True, skip_group_check=True)
                            ins.then_inc(s_down[h], 1)
                        nc.tensor.matmul(pt[1][0:1, 0:1], k["ones"][0:1, 0:1], k["ones"][0:1, 0:1], start=True, stop=True).then_inc(s_down_e[u], 1)


def NEXT(i):
    return i * 2 + 2


def reload(nc, H, acc):
    with ExitStack() as ctx:
        m = Mem(nc, ctx, "rl")
        s = m.sem("in")
        with nc.Block() as block:
            @block.sync
            def _(sp):
                sp.dma_start(H[:, :, :], acc.rearrange("(n p) c -> p n c", p=P)).then_inc(s, 16)
                sp.wait_ge(s, 16)


TAPS, LORA, FEXP = BATCH, 16, 4


def ffn(nc, w, k, H, mean, rstd, out):
    with ExitStack() as ctx:
        m = Mem(nc, ctx, "ff", k["banks"])
        two = lambda n: [m.sem(f"{n}{u}") for u in range(2)]
        ER = FEXP * LORA
        raw = m.sb("raw", [P, 6, P])
        gw = m.sb("gw", [P, FEXP + 1])
        A = m.sb("A", [P, FEXP, LORA])
        BT, fc2T = m.sb("BT", [P, ER]), m.sb("fc2T", [P, FEXP, P])
        M = m.sb("M", [2 * ER, 2 * D])
        spreadM = [m.sb(f"BTe{e}", [P, 2 * ER]) for e in range(FEXP)]
        xn = [m.sb(f"xn{u}", [P, 4, P]) for u in range(2)]
        xT = [m.sb(f"xT{u}", [P, HALF]) for u in range(2)]
        hid = [m.sb(f"hid{u}", [P, FEXP, HALF]) for u in range(2)]
        lg = [m.sb(f"lg{u}", [P, 4, 8]) for u in range(2)]
        ex = [m.sb(f"ex{u}", [P, 4, FEXP]) for u in range(2)]
        sg = [m.sb(f"sg{u}", [P, 4]) for u in range(2)]
        t4 = [m.sb(f"t4{u}", [P, 4]) for u in range(2)]
        wl = [m.sb(f"wl{u}", [P, 4, ER]) for u in range(2)]
        wlT = [m.sb(f"wlT{u}", [P, 2 * P]) for u in range(2)]
        yo = [m.sb(f"yo{u}", [P, 4, D]) for u in range(2)]
        pt = [m.ps() for u in range(2)]
        pf = [m.ps() for e in range(2)]
        pl = [m.ps((P, 4, P)) for u in range(2)]
        po = [m.ps((P, 4, D)) for u in range(2)]
        s_in, s_t, s_tc, s_dve = m.sem("in"), m.sem("t"), m.sem("tc"), m.sem("dve")
        (s_xn, s_turned, s_xT, s_fc1, s_hid, s_low, s_lowc, s_exp, s_wl, s_wlt, s_wlT, s_o, s_y, s_store) = (two(n) for n in (
            "xn", "turned", "xT", "fc1", "hid", "low", "lowc", "exp", "wl", "wlt", "wlT", "o", "y", "store"))
        G = NT // 4
        out_v = out.rearrange("b (t p) d -> p (b t) d", p=P)
        with nc.Block() as block:
            @block.sync
            def _(sp):
                for e in range(FEXP):
                    sp.dma_start(raw[:, e, :], w["L1_ffn_fc2_w"][e]).then_inc(s_in, 16)
                sp.dma_start(raw[0:ER, 4, :], w["L1_ffn_lora_B"].rearrange("e r o -> (e r) o")).then_inc(s_in, 16)
                sp.dma_start(raw[0:FEXP, 5, :], w["L1_ffn_gate_w"]).then_inc(s_in, 16)
                sp.dma_start(raw[FEXP:FEXP + 1, 5, :], w["L1_ffn_thr_w"]).then_inc(s_in, 16)
                sp.dma_start(A[:, :, :], w["L1_ffn_lora_A"].rearrange("e h r -> h e r")).then_inc(s_in, 16)
                sp.wait_ge(s_in, 128)

            @block.tensor
            def _(pe):
                pe.wait_ge(s_in, 128)
                for e in range(FEXP):
                    nc.tensor.transpose(pt[0][:, P * e:P * e + P], raw[:, e, :], k["ident"][:, :])
                nc.tensor.transpose(pt[1][:, 0:ER], raw[0:ER, 4, :], k["ident"][0:ER, 0:ER])
                nc.tensor.transpose(pt[1][:, P:P + FEXP + 1], raw[0:FEXP + 1, 5, :], k["ident"][0:FEXP + 1, 0:FEXP + 1]).then_inc(s_t, 1)
                pe.wait_ge(s_tc, 8 + FEXP)
                for e in range(FEXP):
                    ins = nc.tensor.matmul(po[0][0:2 * ER, 0, :], spreadM[e][:, :], fc2T[:, e, :], start=(e == 0), stop=(e == FEXP - 1))
                ins.then_inc(s_t, 1)

            @block.vector
            def _(dve):
                for e in range(FEXP):
                    nc.vector.memset(spreadM[e][:, :], 0.0).then_inc(s_tc, 1)
                nc.vector.memset(M[:, :], 0.0).then_inc(s_tc, 1)
                dve.wait_ge(s_tc, FEXP + 1)
                dve.wait_ge(s_t, 1)
                nc.vector.tensor_copy(fc2T[:, :, :].rearrange("p a b -> p (a b)"), pt[0][:, :]).then_inc(s_tc, 1)
                nc.vector.tensor_copy(BT[:, :], pt[1][:, 0:ER]).then_inc(s_tc, 1)
                nc.vector.tensor_copy(gw[:, :], pt[1][:, P:P + FEXP + 1]).then_inc(s_tc, 1)
                for e in range(FEXP):
                    r = slice(LORA * e, LORA * e + LORA)
                    nc.vector.tensor_copy(spreadM[e][:, r], pt[1][:, r])
                    nc.vector.tensor_copy(spreadM[e][:, ER + LORA * e:ER + LORA * e + LORA], pt[1][:, r]).then_inc(s_tc, 1)
                dve.wait_ge(s_t, 2)
                nc.vector.tensor_copy(M[0:ER, 0:D], po[0][0:ER, 0, :])
                nc.vector.tensor_copy(M[ER:2 * ER, D:2 * D], po[0][ER:2 * ER, 0, :]).then_inc(s_tc, 1)
        with nc.Block() as block:
            @block.vector
            def _(dve):
                for i in passes(dve, G // 2):
                    st = Steps(dve, s_dve, i, 24)
                    for u in range(2):
                        dve.wait_ge(s_turned[u], i)
                        for t in range(4):
                            n = (i * 2 + u) * 4 + t
                            ins = nc.vector.tensor_scalar(xn[u][:, t, :], H[:, n, :], mean[:, bass.ds(n, 1)], rstd[:, bass.ds(n, 1)],
                                                          ALU.subtract, ALU.mult)
                        ins.then_inc(s_xn[u], 1)
                    for u in range(2):
                        dve.wait_ge(s_low[u], i + 1)
                        nc.vector.tensor_copy(wl[u][:, :, :], pl[u][:, :, 0:ER])
                        st.link(nc.vector.tensor_copy(lg[u][:, :, 0:FEXP + 1], pl[u][:, :, ER:ER + FEXP + 1]))
                        st.link(nc.vector.tensor_reduce(t4[u][:, :], lg[u][:, :, 0:FEXP], AX.X, ALU.max))
                        nc.vector.tensor_tensor(lg[u][:, :, 0:FEXP], lg[u][:, :, 0:FEXP], spread(t4[u][:, :], FEXP), ALU.subtract).then_inc(s_lowc[u], 1)
                    for u in range(2):
                        dve.wait_ge(s_exp[u], i + 1)
                        st.link(nc.vector.tensor_reduce(t4[u][:, :], ex[u][:, :, :], AX.X, ALU.add))
                        st.link(nc.vector.reciprocal(t4[u][:, :], t4[u][:, :]))
                        st.link(nc.vector.tensor_tensor(ex[u][:, :, :], ex[u][:, :, :], spread(t4[u][:, :], FEXP), ALU.mult))
                        st.link(nc.vector.tensor_scalar(sg[u][:, :], sg[u][:, :], 0.5 / FEXP, 0.5 / FEXP, ALU.mult, ALU.add))
                        st.link(nc.vector.tensor_tensor(ex[u][:, :, :], ex[u][:, :, :], spread(sg[u][:, :], FEXP), ALU.subtract))
                        st.link(nc.vector.tensor_scalar(ex[u][:, :, :], ex[u][:, :, :], 0.0, None, ALU.max))
                        st.link(nc.vector.tensor_reduce(t4[u][:, :], ex[u][:, :, :], AX.X, ALU.add))
                        st.link(nc.vector.scalar_tensor_tensor(out=t4[u][:, :], in0=t4[u][:, :], scalar=0.0, in1=t4[u][:, :],
                                                               op0=ALU.is_equal, op1=ALU.add))
                        st.link(nc.vector.reciprocal(t4[u][:, :], t4[u][:, :]))
                        st.link(nc.vector.tensor_tensor(ex[u][:, :, :], ex[u][:, :, :], spread(t4[u][:, :], FEXP), ALU.mult))
                        nc.vector.tensor_tensor(wl[u][:, :, :].rearrange("p t (e r) -> p t e r", e=FEXP), wl[u][:, :, :].rearrange("p t (e r) -> p t e r", e=FEXP),
                                                ex[u][:, :, :].unsqueeze(3).broadcast_to([P, 4, FEXP, LORA]), ALU.mult).then_inc(s_wl[u], 1)
                    for u in range(2):
                        dve.wait_ge(s_o[u], i + 1)
                        dve.wait_ge(s_store[u], 16 * i)
                        nc.vector.tensor_tensor(yo[u][:, :, :], H[:, bass.ds((i * 2 + u) * 4, 4), :], po[u][:, :, :], ALU.add).then_inc(s_y[u], 1)
                    st.close()

            @block.scalar
            def _(act):
                for i in passes(act, G // 2):
                    for u in range(2):
                        act.wait_ge(s_turned[u], i + 1)
                        act.wait_ge(s_low[u], i)
                        nc.scalar.copy(xT[u][:, :], pt[u][:, :]).then_inc(s_xT[u], 1)
                    for u in range(2):
                        for e in range(FEXP):
                            act.wait_ge(s_fc1[u], FEXP * i + e + 1)
                            nc.scalar.activation(hid[u][:, e, :], pf[e % 2][:, :], ACT.Relu).then_inc(s_hid[u], 1)
                    for u in range(2):
                        act.wait_ge(s_lowc[u], i + 1)
                        act.wait_ge(s_wl[u], i)
                        nc.scalar.activation(ex[u][:, :, :], lg[u][:, :, 0:FEXP], ACT.Exp)
                        nc.scalar.activation(sg[u][:, :], lg[u][:, :, FEXP:FEXP + 1].rearrange("p a b -> p (a b)"), ACT.Tanh, scale=0.5).then_inc(s_exp[u], 1)
                    for u in range(2):
                        act.wait_ge(s_wlt[u], i + 1)
                        nc.scalar.copy(wlT[u][:, :], pt[u][:, 0:2 * P]).then_inc(s_wlT[u], 1)

            @block.tensor
            def _(pe):
                for i in passes(pe, G // 2):
                    for u in range(2):
                        pe.wait_ge(s_xn[u], i + 1)
                        pe.wait_ge(s_wlT[u], i)
                        for t in range(4):
                            ins = nc.tensor.transpose(pt[u][:, P * t:P * t + P], xn[u][:, t, :], k["ident"][:, :])
                        ins.then_inc(s_turned[u], 1)
                    for u in range(2):
                        pe.wait_ge(s_xT[u], i + 1)
                        for e in range(FEXP):
                            if e >= 2:
                                pe.wait_ge(s_hid[u], FEXP * i + e - 1)
                            elif u:
                                pe.wait_ge(s_hid[0], FEXP * i + FEXP - 1 + e)
                            else:
                                pe.wait_ge(s_hid[1], FEXP * i)
                            nc.tensor.matmul(pf[e % 2][:, :], k["fc1T"][:, e, :], xT[u][:, :], start=True, stop=True).then_inc(s_fc1[u], 1)
                    for u in range(2):
                        pe.wait_ge(s_hid[u], FEXP * i + FEXP)
                        pe.wait_ge(s_lowc[u], i)
                        for t in range(4):
                            c = slice(P * t, P * t + P)
                            for e in range(FEXP):
                                nc.tensor.matmul(pl[u][:, t, LORA * e:LORA * e + LORA], hid[u][:, e, c], A[:, e, :],
                                                 start=True, stop=True, skip_group_check=True)
                            ins = nc.tensor.matmul(pl[u][:, t, ER:ER + FEXP + 1], xT[u][:, c], gw[:, :], start=True, stop=True, skip_group_check=True)
                        ins.then_inc(s_low[u], 1)
                    for u in range(2):
                        pe.wait_ge(s_wl[u], i + 1)
                        for t in range(2):
                            ins = nc.tensor.transpose(pt[u][:, P * t:P * t + P], wl[u][:, 2 * t:2 * t + 2, :].rearrange("p a b -> p (a b)"),
                                                      k["ident"][:, :])
                        ins.then_inc(s_wlt[u], 1)
                    for u in range(2):
                        pe.wait_ge(s_wlT[u], i + 1)
                        pe.wait_ge(s_y[u], i)
                        for t in range(2):
                            ins = nc.tensor.matmul(po[u][:, 2 * t:2 * t + 2, :].rearrange("p a b -> p (a b)"), wlT[u][:, P * t:P * t + P], M[:, :], start=True, stop=True, skip_group_check=True)
                        ins.then_inc(s_o[u], 1)

            @block.sync
            def _(sp):
                for i in passes(sp, G // 2):
                    for u in range(2):
                        sp.wait_ge(s_y[u], i + 1)
                        sp.dma_start(out_v[:, bass.ds((i * 2 + u) * 4, 4), :], yo[u][:, :, :]).then_inc(s_store[u], 16)
                for u in range(2):
                    sp.wait_ge(s_store[u], 16 * G // 2)


MODES = 64
LQ = SEQ // 2 // P
NF = 8
COMPLEX = range(2, NF)
C8 = float(np.sqrt(0.5))


def roots():
    return np.array([[2 * (P * (q % 2) + p) + q // 2 for p in range(P)] for q in range(LQ)])


def freqs():
    f = [8 * np.arange(P), 4 + 8 * np.arange(P)]
    for f1 in (1, 2, 3):
        f += [f1 + 8 * np.arange(P), f1 + 8 * np.arange(P, 2 * P)]
    return np.array(f)


def ssm_tables():
    l = roots()
    tau = np.tan(np.pi * l / SEQ)
    t = np.arange(SEQ // 2)
    ang = 2 * np.pi * ((l[:, :, None] * t) % SEQ) / SEQ
    wt = np.where(l == 0, 0.5, 1.0)[:, :, None] / SEQ
    tau_cols = np.concatenate([tau.T, (tau ** 2).T, -tau.T], 1)
    halves = np.zeros((P, 4))
    halves[0:64, 0] = halves[64:, 1] = 1
    halves[0:64, 2] = halves[64:, 3] = -1
    n = 2 * SEQ
    fwd, inv = [], []
    F = freqs()
    for c in range(NF):
        for wt_ in range(2):
            tt = np.arange(P) + P * wt_
            a = 2 * np.pi * ((tt[:, None] * F[c][None, :]) % n) / n
            C, S = np.cos(a), np.sin(a)
            mats = [C, -S] + ([-C] if c in COMPLEX else [])
            g = np.full(P, 2.0 / n)
            if c == 0:
                mats[1][:, 0] = (-1.0) ** tt
                g[0] = 1.0 / n
            fwd += mats
            IC, IS = (C * g).T, (-S * g).T
            if c == 0:
                IC, IS = (np.cos(a) * g).T, (-np.sin(a) * g).T
                IS[0, :] = (-1.0) ** tt / n
            inv += [IC, IS] + ([-IS] if c in COMPLEX else [])
    f32 = lambda a: np.ascontiguousarray(a, dtype=np.float32)
    return {"c_tau2": f32(np.tile((tau.reshape(-1) ** 2), (P, 1))), "c_tau": f32(tau_cols), "c_halves": f32(halves),
            "c_kcos": f32((np.cos(ang) * wt).transpose(1, 0, 2)), "c_ksin": f32((-np.sin(ang) * wt).transpose(1, 0, 2)),
            "c_alt": f32(((-1.0) ** np.arange(P))[None] / SEQ),
            "c_fwd": f32(np.array(fwd).transpose(1, 0, 2)), "c_inv": f32(np.array(inv).transpose(1, 0, 2))}


def matrix_at():
    at, n = {}, 0
    for c in range(NF):
        for h in range(2):
            at[c, h] = n
            n += 3 if c in COMPLEX else 2
    return at, n


def ssm_kernel(nc, w, k, Kt):
    with ExitStack() as ctx:
        m = Mem(nc, ctx, "sk", k["banks"])
        NA = 9
        rl = m.sb("rl", [64, 2, P])
        r3 = m.sb("r3", [64, 3, 2 * P])
        rs, rsT, sb_ = m.sb("rs", [2, 64]), m.sb("rsT", [64, 2]), m.sb("sbc", [64, 2, 64])
        V = m.sb("V", [P, NA, 64])
        g = lambda n: m.sb(n, [P, 64])
        lr, li, mr, mi, q2, ns = g("lr"), g("li"), g("mr"), g("mi"), g("q2"), g("ns")
        WW = m.sb("WW", [P, 4, 4, 2, 64])
        t1, t2 = m.sb("t1", [P, 4, 64]), m.sb("t2", [P, 4, 64])
        W2 = m.sb("W2", [P, 64, 2, 32])
        tau2, tau, halves = m.sb("tau2", [P, HALF]), m.sb("tau", [P, 12]), m.sb("halves", [P, 4])
        kcos, ksin = m.sb("kcos", [P, LQ, SEQ // 2]), m.sb("ksin", [P, LQ, SEQ // 2])
        alt, Drow, p512 = m.sb("alt", [1, P]), m.sb("Drow", [1, P]), m.sb("p512", [1, P])
        sqr = [m.sb(f"sqr{u}", [P, HALF]) for u in range(2)]
        R = [m.sb(f"R{u}", [P, HALF]) for u in range(2)]
        SS = m.sb("SS", [P, LQ, 64, 64])
        A, B = m.sb("A", [P, P, 8]), m.sb("B", [P, P, 8])
        KP = m.sb("KP", [P, 2, 2, 4, P])
        tmp = [m.sb(f"tmp{j}", [P, 2, P]) for j in range(8)]
        PQ = m.sb("PQ", [P, LQ, 2, P])
        odd = m.sb("odd", [P, 4 * P])
        pa, pb, pc, pd = m.ps(), m.ps(), m.ps(), m.ps()
        ps = [m.ps((P, LQ, 64)) for u in range(2)]
        s_in, s_pe, s_dve, s_act, s_k = m.sem("in"), m.sem("pe"), m.sem("dve"), m.sem("act"), m.sem("k")
        two = lambda n: [m.sem(f"{n}{u}") for u in range(2)]
        s_sqr, s_den, s_R, s_S, s_Sc = two("sqr"), two("den"), two("R"), two("S"), two("Sc")
        flat = lambda t: t[:, :, :].rearrange("p a b -> p (a b)")
        NLOAD = 15
        with nc.Block() as block:
            @block.sync
            def _(sp):
                for j, n in enumerate(("re", "im")):
                    sp.dma_start(rl[:, j, :].rearrange("p (a n) -> p a n", a=2), w[f"L1_attn_Lambda_{n}"].rearrange("(a p) n -> p a n", a=2)).then_inc(s_in, 16)
                for j, n in enumerate("PBC"):
                    sp.dma_start(r3[:, j, :].rearrange("p (a x) -> p a x", a=2), w[f"L1_attn_{n}"].rearrange("(a p) n c -> p a (n c)", a=2)).then_inc(s_in, 16)
                sp.dma_start(rs[:, :], w["L1_attn_log_step"].rearrange("(a p) -> a p", a=2)).then_inc(s_in, 16)
                sp.dma_start(Drow[:, :], w["L1_attn_D"].rearrange("(a p) -> a p", a=1)).then_inc(s_in, 16)
                for dst, src in ((tau2, "c_tau2"), (tau, "c_tau"), (halves, "c_halves"), (alt, "c_alt")):
                    sp.dma_start(dst[:, :], w[src]).then_inc(s_in, 16)
                for dst, src in ((kcos, "c_kcos"), (ksin, "c_ksin")):
                    sp.dma_start(dst[:, :, :], w[src]).then_inc(s_in, 16)
                sp.wait_ge(s_in, 16 * 13)

            @block.tensor
            def _(pe):
                pe.wait_ge(s_in, 16 * 13)
                nc.tensor.transpose(pa[0:64, 0:2], rs[:, :], k["ident"][0:2, 0:2]).then_inc(s_pe, 1)
                pe.wait_ge(s_dve, 2)
                I64 = k["ident"][0:64, 0:64]
                nc.tensor.transpose(pa[:, 64:128], sb_[:, :, :].rearrange("p a b -> p (a b)"), I64)
                for j in range(2):
                    nc.tensor.transpose(pb[:, 64 * j:64 * j + 64], rl[:, j, :], I64)
                for j in range(3):
                    for c in range(2):
                        n = 2 + 2 * j + c
                        ins = nc.tensor.transpose(pb[:, 64 * n:64 * n + 64], r3[:, j, c::2], I64)
                ins.then_inc(s_pe, 1)
                pe.wait_ge(s_k, 1)
                for a in range(2):
                    ins = nc.tensor.matmul(pa[0:1, 64 * a:64 * a + 64], halves[:, 2 + a:3 + a], WW[:, 2, 0, 0, :], start=True, stop=True, skip_group_check=True)
                ins.then_inc(s_pe, 1)
                pe.wait_ge(s_k, 3)
                for i in passes(pe, 32):
                    for u in range(2):
                        pe.wait_ge(s_R[u], i + 1)
                        pe.wait_ge(s_Sc[u], i)
                        for q in range(LQ):
                            ins = nc.tensor.matmul(ps[u][:, q, :], R[u][:, P * q:P * q + P], W2[:, i * 2 + u, :, :].rearrange("p a b -> p (a b)"),
                                                   start=True, stop=True, skip_group_check=True)
                        ins.then_inc(s_S[u], 1)
                pe.wait_ge(s_k, 4)
                for t in range(4):
                    c = slice(P * t, P * t + P)
                    for q in range(LQ):
                        dst = (pc, pd)[q // 2][:, c]
                        nc.tensor.matmul(dst, kcos[:, q, c], PQ[:, q, 0, :], start=(q % 2 == 0), stop=False, skip_group_check=True)
                        ins = nc.tensor.matmul(dst, ksin[:, q, c], PQ[:, q, 1, :], start=False, stop=(q == 3), skip_group_check=True)
                        if q == 1:
                            nc.tensor.matmul(dst, alt[:, :], p512[:, :], start=False, stop=True, skip_group_check=True)
                ins.then_inc(s_pe, 1)

            @block.scalar
            def _(act):
                act.wait_ge(s_dve, 1)
                nc.scalar.activation(rsT[:, :], rsT[:, :], ACT.Exp).then_inc(s_act, 1)
                act.wait_ge(s_k, 2)
                for i in passes(act, 32):
                    for u in range(2):
                        act.wait_ge(s_den[u], i)
                        nc.scalar.activation(sqr[u][:, :], tau2[:, :], ACT.Square, bias=mr[:, bass.ds(i * 2 + u, 1)]).then_inc(s_sqr[u], 1)
                    for u in range(2):
                        act.wait_ge(s_S[u], i + 1)
                        nc.scalar.copy(SS[:, :, i * 2 + u, :], ps[u][:, :, :]).then_inc(s_Sc[u], 1)

            @block.vector
            def _(dve):
                st = Steps(dve, s_dve)
                dve.wait_ge(s_pe, 1)
                st.link(nc.vector.tensor_copy(rsT[:, :], pa[0:64, 0:2]))
                dve.wait_ge(s_act, 1)
                st.link(nc.vector.tensor_scalar(sb_[:, :, :], spread(rsT[:, :], 64), 0.5, None, ALU.mult))
                dve.wait_ge(s_pe, 2)
                nc.vector.tensor_copy(V[:, 8, :], pa[:, 64:128])
                st.link(nc.vector.tensor_copy(V[:, 0:8, :].rearrange("p a b -> p (a b)"), pb[:, :]))
                TT, MUL = nc.vector.tensor_tensor, ALU.mult
                s = V[:, 8, :]
                Pr, Pi, Br, Bi, Cr, Ci = (V[:, j, :] for j in range(2, 8))
                nc.vector.scalar_tensor_tensor(out=lr[:, :], in0=V[:, 0, :], scalar=-1e-4, in1=s, op0=ALU.min, op1=MUL)
                nc.vector.tensor_scalar(ns[:, :], s, -1.0, None, MUL)
                st.link(TT(li[:, :], V[:, 1, :], s, MUL))
                TT(t1[:, 0, :], lr[:, :], lr[:, :], MUL)
                TT(t1[:, 1, :], li[:, :], li[:, :], MUL)
                st.link(nc.vector.scalar_tensor_tensor(out=mi[:, :], in0=lr[:, :], scalar=2.0, in1=li[:, :], op0=MUL, op1=MUL))
                TT(mr[:, :], t1[:, 0, :], t1[:, 1, :], ALU.subtract)
                st.link(TT(q2[:, :], mi[:, :], mi[:, :], MUL))
                cr, ci = WW[:, 2, :, 0, :], WW[:, 2, :, 1, :]

                def conj_product(v, ar, ai, br, bi):
                    TT(t1[:, 0, :], ar, br, MUL)
                    TT(t1[:, 1, :], ai, bi, MUL)
                    TT(t1[:, 2, :], ar, bi, MUL)
                    st.link(TT(t1[:, 3, :], ai, br, MUL))
                    TT(cr[:, v, :], t1[:, 0, :], t1[:, 1, :], ALU.add)
                    st.link(TT(ci[:, v, :], t1[:, 2, :], t1[:, 3, :], ALU.subtract))

                conj_product(0, Cr, Ci, Br, Bi)
                conj_product(1, Cr, Ci, Pr, Pi)
                conj_product(2, Pr, Pi, Br, Bi)
                conj_product(3, Pr, Pi, Pr, Pi)
                over = lambda a: a[:, :].unsqueeze(1).broadcast_to([P, 4, 64])
                TT(cr, cr, over(ns), MUL)
                st.link(TT(ci, ci, over(ns), MUL))

                def times(out, x, yr, yi, conj):
                    xr, xi, o_r, o_i = WW[:, x, :, 0, :], WW[:, x, :, 1, :], WW[:, out, :, 0, :], WW[:, out, :, 1, :]
                    TT(t1[:, :, :], xr, over(yr), MUL)
                    st.link(TT(t2[:, :, :], xi, over(yi), MUL))
                    st.link(TT(o_r, t1[:, :, :], t2[:, :, :], ALU.add if conj else ALU.subtract))
                    TT(t1[:, :, :], xi, over(yr), MUL)
                    st.link(TT(t2[:, :, :], xr, over(yi), MUL))
                    st.link(TT(o_i, t1[:, :, :], t2[:, :, :], ALU.subtract if conj else ALU.add))

                times(0, 2, lr, li, False)
                times(1, 0, mr, mi, True)
                times(3, 2, mr, mi, True)
                dve.wait_ge(s_in, 16 * 13)
                nc.vector.tensor_copy(t1[:, 0, 0:1], t2[:, 0, 0:1]).then_inc(s_k, 1)
                nc.vector.tensor_copy(t1[:, 0, 1:2], t2[:, 0, 0:1]).then_inc(s_k, 1)
                for a in range(2):
                    ins = nc.vector.tensor_scalar(W2[:, :, a, :], WW[:, :, :, :, :].rearrange("p k v c n -> p n (k v c)"), halves[:, a:a + 1], None, MUL)
                dve.wait_ge(s_pe, 3)
                nc.vector.tensor_copy(p512[:, :], pa[0:1, 0:P]).then_inc(s_k, 1)
                for i in passes(dve, 32):
                    for u in range(2):
                        dve.wait_ge(s_sqr[u], i + 1)
                        nc.vector.tensor_scalar(sqr[u][:, :], sqr[u][:, :], q2[:, bass.ds(i * 2 + u, 1)], None, ALU.add).then_inc(s_den[u], 1)
                    for u in range(2):
                        dve.wait_ge(s_den[u], i + 1)
                        dve.wait_ge(s_S[u], i)
                        nc.vector.reciprocal(R[u][:, :], sqr[u][:, :]).then_inc(s_R[u], 1)
                for u in range(2):
                    dve.wait_ge(s_Sc[u], 32)
                for q in range(LQ):
                    T, T2, NT_ = tau[:, q:q + 1], tau[:, 4 + q:5 + q], tau[:, 8 + q:9 + q]
                    sums = lambda kk: SS[:, q, :, :].rearrange("p n (a s) -> p (n a) s", a=2)[:, :, 8 * kk:8 * kk + 8]
                    STT = nc.vector.scalar_tensor_tensor
                    STT(out=A[:, :, :], in0=sums(0), scalar=T2, in1=sums(1), op0=MUL, op1=ALU.add)
                    st.link(STT(out=B[:, :, :], in0=sums(2), scalar=T2, in1=sums(3), op0=MUL, op1=ALU.add))
                    pick = lambda X, c: X[:, :, :].rearrange("p h (v c) -> p v c h", c=2)[:, :, c, :]
                    STT(out=KP[:, 0, 0], in0=pick(B, 1), scalar=NT_, in1=pick(A, 0), op0=MUL, op1=ALU.add)
                    STT(out=KP[:, 0, 1], in0=pick(B, 0), scalar=T, in1=pick(A, 1), op0=MUL, op1=ALU.add)
                    STT(out=KP[:, 1, 0], in0=pick(B, 1), scalar=T, in1=pick(A, 0), op0=MUL, op1=ALU.add)
                    st.link(STT(out=KP[:, 1, 1], in0=pick(B, 0), scalar=NT_, in1=pick(A, 1), op0=MUL, op1=ALU.add))
                    kr, ki = (lambda v: KP[:, :, 0, v, :]), (lambda v: KP[:, :, 1, v, :])
                    a0, a1, a2, a3, a4, a5, a6, a7 = (x[:, :, :] for x in tmp)
                    TT(a0, kr(1), kr(2), MUL)
                    TT(a1, ki(1), ki(2), MUL)
                    TT(a2, kr(1), ki(2), MUL)
                    TT(a3, ki(1), kr(2), MUL)
                    st.link(nc.vector.tensor_scalar(a4, kr(3), 1.0, None, ALU.add))
                    TT(a0, a0, a1, ALU.subtract)
                    TT(a2, a2, a3, ALU.add)
                    TT(a5, a4, a4, MUL)
                    st.link(TT(a6, ki(3), ki(3), MUL))
                    st.link(TT(a5, a5, a6, ALU.add))
                    nc.vector.reciprocal(a5, a5)
                    TT(a1, a0, a4, MUL)
                    TT(a3, a2, ki(3), MUL)
                    TT(a6, a2, a4, MUL)
                    st.link(TT(a7, a0, ki(3), MUL))
                    TT(a1, a1, a3, ALU.add)
                    st.link(TT(a6, a6, a7, ALU.subtract))
                    TT(a1, a1, a5, MUL)
                    st.link(TT(a6, a6, a5, MUL))
                    TT(a1, kr(0), a1, ALU.subtract)
                    st.link(TT(a6, ki(0), a6, ALU.subtract))
                    TT(a0[:, 0, :], a1[:, 0, :], a1[:, 1, :], ALU.add)
                    st.link(TT(a0[:, 1, :], a6[:, 0, :], a6[:, 1, :], ALU.subtract))
                    unpair = lambda x: x.rearrange("p (n a) -> p a n", a=2)
                    out = lambda c: PQ[:, q, c, :].rearrange("p (a n) -> p a n", a=2)
                    STT(out=out(0), in0=unpair(a0[:, 1, :]), scalar=NT_, in1=unpair(a0[:, 0, :]), op0=MUL, op1=ALU.add)
                    ins = STT(out=out(1), in0=unpair(a0[:, 0, :]), scalar=T, in1=unpair(a0[:, 1, :]), op0=MUL, op1=ALU.add)
                    if q < LQ - 1:
                        st.link(ins)
                ins.then_inc(s_k, 1)
                dve.wait_ge(s_pe, 4)
                st.link(nc.vector.tensor_copy(odd[:, :], pd[:, :]))
                TT(Kt[:, 0:4, :].rearrange("p a b -> p (a b)"), pc[:, :], odd[:, :], ALU.add)
                st.link(TT(Kt[:, 4:8, :].rearrange("p a b -> p (a b)"), pc[:, :], odd[:, :], ALU.subtract))
                st.link(TT(Kt[0:1, 0, :], Kt[0:1, 0, :], Drow[:, :], ALU.add))


def ssm_convolve(nc, w, k, H, mean, rstd, Kt):
    with ExitStack() as ctx:
        m = Mem(nc, ctx, "sc", k["banks"])
        at, NM = matrix_at()
        fwd, inv = m.sb("fwd", [P, NM, P]), m.sb("inv", [P, NM, P])
        NB = 2
        W_ = NB * P
        xu = m.sb("xu", [P, 4, 2, NB, P])
        names = "s02 d02 s13 d13 f0 f4 r1 n1 r3 n3".split()
        Y = {n: m.sb(n, [P, 2 * W_]) for n in names}
        KA, KB = m.sb("KA", [P, NF, 2, P]), m.sb("KB", [P, NF, P])
        dc = m.sb("dc", [P, 1])
        T1 = [m.sb(f"T1{u}", [P, 2, NB, P]) for u in range(2)]
        T2 = [m.sb(f"T2{u}", [P, 2, NB, P]) for u in range(2)]
        YF = m.sb("YF", [P, NF, 2, W_])
        Z = [m.sb(f"Z{j}", [P, 2 * W_]) for j in range(8)]
        pf = [m.ps() for j in range(4)]
        pz = [m.ps() for j in range(4)]
        s_in, s_f, s_kf, s_dve, s_dve2, s_kc = m.sem("in"), m.sem("f"), m.sem("kf"), m.sem("dve"), m.sem("dve2"), m.sem("kc")
        s_y, s_tile, s_used, s_z, s_zc, s_h, s_prod, s_t, s_zs, s_pool = (m.sem(n) for n in ("y", "tile", "used", "z", "zc", "h", "prod", "t", "zs", "pool"))
        TT, MUL, ADD, SUB = nc.vector.tensor_tensor, ALU.mult, ALU.add, ALU.subtract
        STT = nc.vector.scalar_tensor_tensor
        inputs = {0: ("f0", None), 1: ("f4", None), 2: ("r1", "n1"), 3: ("r1", "n1"), 4: ("d02", "d13"), 5: ("d02", "d13"),
                  6: ("r3", "n3"), 7: ("r3", "n3")}
        results = [((0,), 0), ((1,), 0), ((2, 3), 0), ((2, 3), 1), ((4, 5), 0), ((4, 5), 1), ((6, 7), 0), ((6, 7), 1)]

        def split(x, nb, st):
            y = {n: Y[n][:, 0:2 * nb * P] for n in names}
            TT(y["s02"], x(0), x(2), ADD)
            TT(y["d02"], x(0), x(2), SUB)
            TT(y["s13"], x(1), x(3), ADD)
            st.link(TT(y["d13"], x(1), x(3), SUB))
            TT(y["f0"], y["s02"], y["s13"], ADD)
            TT(y["f4"], y["s02"], y["s13"], SUB)
            STT(out=y["r1"], in0=y["d13"], scalar=C8, in1=x(0), op0=MUL, op1=ADD)
            STT(out=y["r3"], in0=y["d13"], scalar=-C8, in1=x(0), op0=MUL, op1=ADD)
            STT(out=y["n1"], in0=y["s13"], scalar=C8, in1=x(2), op0=MUL, op1=ADD)
            return STT(out=y["n3"], in0=y["s13"], scalar=C8, in1=x(2), op0=MUL, op1=SUB)

        def forward(c, dst, nb):
            a, b = inputs[c]
            terms = [(0, a), (1, b)] if b else [(0, a)]
            for part in range(2):
                n = 0
                for h in range(2):
                    for j, name in terms:
                        ins = nc.tensor.matmul(dst(part), fwd[:, at[c, h] + part + j, :], Y[name][:, h * nb * P:(h + 1) * nb * P],
                                               start=(n == 0), stop=(n == 2 * len(terms) - 1), skip_group_check=True)
                        n += 1
            return ins

        with nc.Block() as block:
            @block.sync
            def _(sp):
                sp.dma_start(fwd[:, :, :], w["c_fwd"]).then_inc(s_in, 16)
                sp.dma_start(inv[:, :, :], w["c_inv"]).then_inc(s_in, 16)
                sp.wait_ge(s_in, 32)

            @block.tensor
            def _(pe):
                pe.wait_ge(s_in, 32)
                pe.wait_ge(s_kf, 1)
                for c in range(NF):
                    ins = forward(c, lambda p_: pf[c // 2][:, P * (2 * (c % 2) + p_):P * (2 * (c % 2) + p_) + P], 1)
                ins.then_inc(s_f, 1)
                pe.wait_ge(s_kc, 1)
                for i in passes(pe, BATCH // NB):
                    pe.wait_ge(s_y, i + 1)
                    for c in range(NF):
                        if c >= 4:
                            pe.wait_ge(s_used, NF * i + c - 3)
                        forward(c, lambda p_: pf[c % 4][:, W_ * p_:W_ * p_ + W_], NB).then_inc(s_tile, 1)
                    pe.wait_ge(s_prod, NF * i + NF)
                    for j, (cs_, kind) in enumerate(results):
                        if j >= 4:
                            pe.wait_ge(s_zc, 8 * i + j - 3)
                        elif j == 0:
                            pe.wait_ge(s_zc, 8 * i)
                        for h in range(2):
                            n = 0
                            for c in cs_:
                                for src, mat in (((0, 0), (1, 1)), ((0, 2), (1, 0)))[kind]:
                                    ins = nc.tensor.matmul(pz[j % 4][:, W_ * h:W_ * h + W_], inv[:, at[c, h] + mat, :], YF[:, c, src, :],
                                                           start=(n == 0), stop=(n == 2 * len(cs_) - 1), skip_group_check=True)
                                    n += 1
                        ins.then_inc(s_z, 1)

            @block.scalar
            def _(act):
                for i in passes(act, BATCH // NB):
                    act.wait_ge(s_h, i)
                    for j in range(8):
                        act.wait_ge(s_z, 8 * i + j + 1)
                        nc.scalar.copy(Z[j][:, :], pz[j % 4][:, :]).then_inc(s_zc, 1)

            @block.gpsimd
            def _(pool):
                for i in passes(pool, BATCH // NB):
                    for c in range(NF):
                        pool.wait_ge(s_used, NF * i + c + 1)
                        u = c % 2
                        o = lambda p_: YF[:, c, p_, :].rearrange("p (b h) -> p b h", b=NB)
                        nc.gpsimd.tensor_tensor(o(0), T1[u][:, 0], T2[u][:, 1], SUB)
                        nc.gpsimd.tensor_tensor(o(1), T1[u][:, 1], T2[u][:, 0], ADD).then_inc(s_prod, 1)

            @block.vector
            def _(dve):
                st = Steps(dve, s_dve)
                st.link(nc.vector.memset(dc[:, :], 1.0))
                st.link(nc.vector.memset(dc[0:1, :], 0.0))
                split(lambda j: Kt[:, 2 * j:2 * j + 2, :].rearrange("p a b -> p (a b)"), 1, st).then_inc(s_kf, 1)
                dve.wait_ge(s_f, 1)
                for c in range(NF):
                    src = lambda p_: pf[c // 2][:, P * (2 * (c % 2) + p_):P * (2 * (c % 2) + p_) + P]
                    nc.vector.tensor_copy(KA[:, c, 0, :], src(0))
                    if c:
                        nc.vector.tensor_copy(KA[:, c, 1, :], src(0))
                        ins = nc.vector.tensor_copy(KB[:, c, :], src(1))
                    else:
                        ins = nc.vector.tensor_scalar(KB[:, c, :], src(1), dc[:, 0:1], None, MUL)
                st.link(ins)
                st.link(nc.vector.tensor_scalar(KA[:, 0, 1, :], KA[:, 0, 0, :], dc[:, 0:1], None, MUL))
                nc.vector.tensor_copy(KA[0:1, 0, 1, :], pf[0][0:1, P:2 * P]).then_inc(s_kc, 1)
                dve.wait_ge(s_kc, 1)
                for i in passes(dve, BATCH // NB):
                    s2 = Steps(dve, s_dve2, i, 5)
                    for b in range(NB):
                        for t in range(TILES):
                            n = (i * NB + b) * TILES + t
                            ins = nc.vector.tensor_scalar(xu[:, t // 2, t % 2, b, :], H[:, n, :], mean[:, bass.ds(n, 1)], rstd[:, bass.ds(n, 1)], SUB, MUL)
                    s2.link(ins)
                    dve.wait_ge(s_tile, NF * i)
                    split(lambda j: xu[:, j].rearrange("p w b h -> p (w b h)"), NB, s2).then_inc(s_y, 1)
                    for c in range(NF):
                        dve.wait_ge(s_tile, NF * i + c + 1)
                        if c >= 2:
                            dve.wait_ge(s_prod, NF * i + c - 1)
                        else:
                            dve.wait_ge(s_prod, NF * i)
                        u = c % 2
                        src = pf[c % 4][:, :].rearrange("p (c b h) -> p c b h", c=2, b=NB)
                        TT(T1[u][:, :, :, :], src, KA[:, c, :, :].unsqueeze(2).broadcast_to([P, 2, NB, P]), MUL)
                        TT(T2[u][:, :, :, :], src, KB[:, c, :].unsqueeze(1).unsqueeze(1).broadcast_to([P, 2, NB, P]), MUL).then_inc(s_used, 1)
                    dve.wait_ge(s_zc, 8 * i + 8)
                    z0, z4, r1, i1, r2, i2, r3, i3 = (z[:, :] for z in Z)
                    sA, dA, sr, dr, si, di = (Y[n][:, :] for n in ("s02", "s13", "f0", "f4", "r1", "n1"))
                    TT(sA, z0, z4, ADD)
                    TT(dA, z0, z4, SUB)
                    TT(sr, r1, r3, ADD)
                    TT(dr, r1, r3, SUB)
                    TT(si, i1, i3, ADD)
                    s2.link(TT(di, i1, i3, SUB))
                    TT(z0, sA, r2, ADD)
                    TT(z4, sA, r2, SUB)
                    TT(r1, dA, i2, SUB)
                    TT(i1, dA, i2, ADD)
                    TT(r3, dr, si, SUB)
                    s2.link(TT(i3, dr, si, ADD))
                    TT(z0, z0, sr, ADD)
                    TT(z4, z4, di, SUB)
                    STT(out=r1, in0=r3, scalar=C8, in1=r1, op0=MUL, op1=ADD)
                    s2.link(STT(out=i1, in0=i3, scalar=-C8, in1=i1, op0=MUL, op1=ADD))
                    for j, y in enumerate((z0, r1, z4, i1)):
                        for b in range(NB):
                            dst = H[:, bass.ds((i * NB + b) * TILES + 2 * j, 2), :]
                            ins = TT(dst, dst, y.rearrange("p (w b h) -> p w b h", w=2, b=NB)[:, :, b, :], ADD)
                    ins.then_inc(s_h, 1)
                    dve.wait_ge(s_h, i + 1)
                    s2.close()


def tables():
    return {**attention_tables(), **moe_tables(), **ssm_tables()}


def tower(nc, w, out):
    USED.clear()
    rows = nc.dram_tensor("rows", (TOK, ROW), F32).ap()
    acc = nc.dram_tensor("acc", (TOK, D), F32).ap()
    with ExitStack() as ctx:
        m = Mem(nc, ctx, "all")
        k = constants(nc, m)
        H = m.sb("H", [P, NT, D])
        mean, rstd = m.sb("mean", [P, NT]), m.sb("rstd", [P, NT])
        load_constants(nc, w, k)
        embed_tokens(nc, w, k, H)
        with ExitStack() as ctx2:
            X2 = Mem(nc, ctx2, "x2").sb("X2", [P, NT, D])
            attention(nc, w, k, H, X2, mean, rstd)
            row_stats(nc, k, X2, mean, rstd, "st_mlp")
            mlp(nc, w, k, H, X2, mean, rstd)
        row_stats(nc, k, H, mean, rstd, "st_moe")
        with ExitStack() as ctx2:
            lists = Mem(nc, ctx2, "moe").sb("lists", [P, EXPERTS + 1, NBLK], I32)
            moe_route(nc, w, k, H, mean, rstd, rows, acc, lists)
            moe_experts(nc, w, k, rows, acc, lists)
        reload(nc, H, acc)
        row_stats(nc, k, H, mean, rstd, "st_ssm")
        with ExitStack() as ctx2:
            Kt = Mem(nc, ctx2, "ssm").sb("Kt", [P, TILES, P])
            ssm_kernel(nc, w, k, Kt)
            ssm_convolve(nc, w, k, H, mean, rstd, Kt)
        row_stats(nc, k, H, mean, rstd, "st_ffn")
        ffn(nc, w, k, H, mean, rstd, out)


def kernel(**inputs):
    import numpy as _np
    import concourse.bacc as _bacc
    from concourse import mybir as _mybir
    from concourse.bass_utils import run_bass_kernel_spmd as _run

    nc = _bacc.Bacc("TRN2", target_bir_lowering=False, num_devices=1)
    arrays, args = {}, {}
    for name, a in {**inputs, **tables()}.items():
        a = _np.ascontiguousarray(a)
        arrays[f"in_{name}"] = a
        args[name] = nc.dram_tensor(f"in_{name}", a.shape, _mybir.dt.from_np(a.dtype), kind="ExternalInput").ap()
    out = nc.dram_tensor("out_0", (BATCH, SEQ, D), F32, kind="ExternalOutput").ap()
    tower(nc, args, out)
    r = _run(nc, [arrays], core_ids=[0])
    return r.results[0]["out_0"]
```

```python
import numpy as np
import concourse.bass as bass
from concourse import mybir
from contextlib import ExitStack

F32 = mybir.dt.float32
I32 = mybir.dt.int32
U32 = mybir.dt.uint32
ALU = mybir.AluOpType
ACT = mybir.ActivationFunctionType
AX = mybir.AxisListType

P = 128
BATCH, SEQ, D = 8, 1024, 128
TILES = SEQ // P
NT = BATCH * TILES
TOK = BATCH * SEQ
HALF = 512
BINS = 51


class Steps:

    def __init__(self, eng, sem, i=0, per=0):
        self.eng, self.sem, self.base, self.per, self.n = eng, sem, i * per, per, 0

    def link(self, ins):
        ins.then_inc(self.sem, 1)
        self.n += 1
        self.eng.wait_ge(self.sem, self.base + self.n)

    def close(self):
        assert self.n == self.per, (self.n, self.per)


USED = []


class Mem:

    def __init__(self, nc, ctx, tag, banks=None):
        self.nc, self.ctx, self.tag, self.banks, self.used, self.sems = nc, ctx, tag, banks, 0, []
        ctx.callback(USED.extend, self.sems)

    def sb(self, name, shape, dt=F32):
        return self.ctx.enter_context(self.nc.sbuf_tensor(f"{self.tag}_{name}", shape, dt))

    def ps(self, shape=(P, HALF)):
        bank = self.banks[:, self.used, 0:int(np.prod(shape[1:]))]
        self.used += 1
        if len(shape) == 3:
            bank = bank.rearrange("p (a b) -> p a b", b=shape[2])
        return bank

    def sem(self, name):
        self.sems.append(self.nc.alloc_semaphore(f"{self.tag}_{name}"))
        return self.sems[-1]


def reset_used(nc):
    nc.clear_and_free_semaphores(USED)
    USED.clear()


def passes(eng, n):
    yield 0
    with eng.Fori(1, n) as i:
        yield i


def pairs(eng, n):
    def both(i, first, last):
        for u in range(2):
            yield i * 2 + u, u, first and u == 0, last and u == 1, first
    yield from both(0, True, False)
    yield from both(1, False, False)
    with eng.Fori(2, n // 2 - 1) as i:
        yield from both(i, False, False)
    yield from both(n // 2 - 1, False, True)


def after(eng, sem, n):
    if not (isinstance(n, int) and n <= 0):
        eng.wait_ge(sem, n)


def spread(ap, n):
    return ap.unsqueeze(2).broadcast_to([ap.shape[0], ap.shape[1], n])


def guess_root(nc, act, dst, var, s_out, s_act, n):
    nc.scalar.activation(dst[:, :], var[:, :], ACT.Ln).then_inc(s_act, 1)
    act.wait_ge(s_act, n + 1)
    nc.scalar.activation(dst[:, :], dst[:, :], ACT.Exp, scale=-0.5).then_inc(s_out, 1)


def refine_root(nc, st, r, var, tmp):
    TT = nc.vector.tensor_tensor
    st.link(TT(tmp[:, :], r[:, :], r[:, :], ALU.mult))
    st.link(TT(tmp[:, :], tmp[:, :], var[:, :], ALU.mult))
    st.link(nc.vector.tensor_scalar(tmp[:, :], tmp[:, :], -0.5, 1.5, ALU.mult, ALU.add))
    st.link(TT(r[:, :], r[:, :], tmp[:, :], ALU.mult))


def merge_stats(nc, st, stats, mean, sq, var):
    nc.vector.tensor_tensor(mean, stats[:, :, 1], stats[:, :, 4], ALU.add)
    nc.vector.tensor_tensor(sq, stats[:, :, 1], stats[:, :, 4], ALU.subtract)
    st.link(nc.vector.tensor_tensor(var, stats[:, :, 2], stats[:, :, 5], ALU.add))
    nc.vector.tensor_scalar(mean, mean, 0.5, None, ALU.mult)
    nc.vector.tensor_scalar(var, var, 1.0 / D, 1e-5, ALU.mult, ALU.add)
    st.link(nc.vector.tensor_tensor(sq, sq, sq, ALU.mult))
    return nc.vector.scalar_tensor_tensor(out=var, in0=sq, scalar=0.25, in1=var, op0=ALU.mult, op1=ALU.add)


def row_stats(nc, k, stats, mean, rstd, tag):
    with ExitStack() as ctx:
        m = Mem(nc, ctx, tag, k["banks"])
        var, sq = m.sb("var", [P, NT]), m.sb("sq", [P, NT])
        s_dve, s_var, s_guess, s_act = m.sem("dve"), m.sem("var"), m.sem("guess"), m.sem("act")
        with nc.Block() as block:
            @block.vector
            def _(dve):
                st = Steps(dve, s_dve)
                merge_stats(nc, st, stats[:, :, :], mean[:, :], sq[:, :], var[:, :]).then_inc(s_var, 1)
                dve.wait_ge(s_guess, 1)
                refine_root(nc, st, rstd, var, sq)

            @block.scalar
            def _(act):
                nc.scalar.preload_act_table_set("natural_log_exp_and_others")
                act.wait_ge(s_var, 1)
                guess_root(nc, act, rstd, var, s_guess, s_act, 0)


def load_constants(nc, w, k):
    with ExitStack() as ctx:
        m = Mem(nc, ctx, "ld", k["banks"])
        s_in, s_ps, s_cp = m.sem("in"), m.sem("turned"), m.sem("copied")
        s_id = m.sem("identity")
        raw = m.sb("raw", [P, 24, P])
        rows = [m.ps((P, P)) for i in range(2)]
        jobs = [(P, k[n][:, :]) for n in ("Wq", "Wk", "Wv", "Wg", "Wo")]
        loads = [(w[f"L0_attn_{n}"].unsqueeze(1), 1) for n in ("Wq", "Wk", "Wv", "Wg", "Wo")]
        jobs += [(P, k["W1T"][:, P * f:P * f + P]) for f in range(4)]
        loads += [(w["L0_attn_W1"].rearrange("(f p) c -> p f c", p=P), 4)]
        jobs += [(P, k["W2T"][:, f, :]) for f in range(4)]
        loads += [(w["L0_attn_W2"].rearrange("p (f c) -> p f c", f=4), 4)]
        jobs += [(P, k["fc1T"][:, e, :]) for e in range(4)]
        loads += [(w["L1_ffn_fc1_w"].rearrange("e o i -> o e i"), 4)]
        jobs += [(BINS, k["binsT"][:, :])]
        loads += [(w["L0_tok_bin_embeddings"].unsqueeze(1), 1)]
        vectors = ["L0_tok_b1", "L0_attn_ln1_g", "L0_attn_ln1_b", "L0_attn_ln2_g", "L0_attn_ln2_b",
                   "L0_attn_time_decay", "L0_attn_rms_scale"]
        tms = ["L0_attn_tm_q", "L0_attn_tm_k", "L0_attn_tm_v", "L0_attn_tm_g"]
        nvec = len(vectors) + len(tms)
        with nc.Block() as block:
            @block.sync
            def _(sp):
                j = 0
                for src, n in loads:
                    sp.dma_start(raw[0:src.shape[0], j:j + n, :], src).then_inc(s_in, 16)
                    j += n
                sp.wait_ge(s_id, 4)
                sp.dma_start(k["bins"][0:BINS, 0:P], w["L0_tok_bin_embeddings"]).then_inc(s_in, 16)
                sp.dma_start(k["bins"][64:64 + BINS, P:2 * P], w["L0_tok_bin_embeddings"]).then_inc(s_in, 16)
                sp.wait_ge(s_in, 16 * (len(loads) + nvec + 2))

            @block.scalar
            def _(act):
                for j, n in enumerate(vectors):
                    nc.scalar.dma_start(raw[j:j + 1, len(jobs), :], w[n].rearrange("(a c) -> a c", a=1)).then_inc(s_in, 16)
                for j, n in enumerate(tms):
                    nc.scalar.dma_start(raw[len(vectors) + j:len(vectors) + j + 1, len(jobs), :],
                                        w[n].rearrange("a b c -> (a b) c")).then_inc(s_in, 16)

            @block.gpsimd
            def _(pool):
                nc.gpsimd.memset(k["ones"][:, :], 1.0).then_inc(s_id, 1)
                nc.gpsimd.memset(k["neg_half"][:, :], -0.5).then_inc(s_id, 1)
                nc.gpsimd.memset(k["bins"][:, :], 0.0).then_inc(s_id, 1)
                nc.gpsimd.memset(k["row0"][:, :], 0.0).then_inc(s_id, 1)
                pool.wait_ge(s_id, 4)
                nc.gpsimd.memset(k["row0"][0:1, :], 1.0)
                nc.gpsimd.affine_select(out=k["ident"][:, :], in_=k["ones"][:, :], compare_op=ALU.is_equal,
                                        fill=0.0, base=0, pattern=[[-1, P]], channel_multiplier=1).then_inc(s_id, 1)

            every = jobs + [(nvec, k["cols"][:, 0:nvec])]

            @block.tensor
            def _(pe):
                pe.wait_ge(s_id, 5)
                pe.wait_ge(s_in, 16 * (len(loads) + nvec + 2))
                for j, (n, dst) in enumerate(every):
                    if j >= 2:
                        pe.wait_ge(s_cp, j - 1)
                    nc.tensor.transpose(rows[j % 2][:, 0:n], raw[0:n, j, :], k["ident"][0:n, 0:n]).then_inc(s_ps, 1)

            @block.vector
            def _(dve):
                for j, (n, dst) in enumerate(every):
                    dve.wait_ge(s_ps, j + 1)
                    nc.vector.tensor_copy(dst, rows[j % 2][:, 0:n]).then_inc(s_cp, 1)


def embed_tokens(nc, w, k, H, stats):
    with ExitStack() as ctx:
        m = Mem(nc, ctx, "tok", k["banks"])
        tok = m.sb("tok", [P, TOK], I32)
        til_i = m.sb("til_i", [NT, P], I32)
        til_f = m.sb("til_f", [NT, P])
        live = m.sb("live", [P, NT])
        dead = m.sb("dead", [P, NT])
        w1 = m.sb("w1", [P, 1])
        w2T = m.sb("w2T", [P, P])
        w2 = m.sb("w2", [P, P])
        b2 = m.sb("b2", [P, 1])
        simw = m.sb("simw", [P, P])
        simb = m.sb("simb", [P, 64])
        hT = [m.sb(f"hT{u}", [P, HALF]) for u in range(2)]
        ex = [m.sb(f"ex{u}", [P, 4, 64]) for u in range(2)]
        prob = [m.sb(f"prob{u}", [P, 4, 64]) for u in range(2)]
        pT = [m.sb(f"pT{u}", [P, 2 * P]) for u in range(2)]
        mx = [m.sb(f"mx{u}", [P, 4]) for u in range(2)]
        sm = [m.sb(f"sm{u}", [P, 4]) for u in range(2)]
        inv = [m.sb(f"inv{u}", [P, 4]) for u in range(2)]
        pa = m.ps()
        psim = [m.ps((P, 4, P)) for u in range(2)]
        pp = [m.ps() for u in range(2)]
        pe_ = [m.ps() for u in range(2)]
        s_in, s_f, s_w, s_wc = m.sem("in"), m.sem("float"), m.sem("weights"), m.sem("wcopied")
        s_tok = [m.sem(f"tok{c}") for c in range(4)]
        (s_relu, s_sim, s_sub, s_exp, s_prob, s_pT, s_pTc, s_emb, s_out) = (m.sem(n) for n in (
            "relu", "sim", "sub", "exp", "prob", "pT", "pTc", "emb", "out"))
        s_dve, s_dve2 = m.sem("dve"), m.sem("dve2")
        NG = TOK // HALF
        with nc.Block() as block:
            @block.sync
            def _(sp):
                sp.dma_start(til_i[:, :], w["x"].rearrange("b (t c) -> (b t) c", c=P)).then_inc(s_in, 16)
                sp.dma_start(w1[:, :], w["L0_tok_w1"].rearrange("a c -> c a")).then_inc(s_in, 16)
                sp.dma_start(w2[:, :], w["L0_tok_w2"]).then_inc(s_in, 16)
                sp.dma_start(b2[:, :], w["L0_tok_b2"].rearrange("(c a) -> c a", a=1)).then_inc(s_in, 16)
                x = w["x"].rearrange("b (t c) -> (b t) c", t=1).rearrange("(a b) c -> a (b c)", a=1)
                for c in range(4):
                    part = slice(TOK // 4 * c, TOK // 4 * c + TOK // 4)
                    sp.dma_start(tok[:, part], x[:, part].broadcast_to([P, TOK // 4])).then_inc(s_tok[c], 16)

            @block.tensor
            def _(pe):
                pe.wait_ge(s_f, 1)
                nc.tensor.transpose(pp[0][:, 0:NT], til_f[:, :], k["ident"][0:NT, 0:NT]).then_inc(s_w, 1)
                nc.tensor.transpose(pp[1][:, 0:P], w2[:, :], k["ident"][:, :]).then_inc(s_w, 1)
                pe.wait_ge(s_wc, 4)
                nc.tensor.matmul(pa[:, 0:BINS], w2T[:, :], k["binsT"][:, :], start=True, stop=True).then_inc(s_w, 1)
                nc.tensor.matmul(pa[:, P:P + BINS], b2[:, 0:1].broadcast_to([P, P]), k["binsT"][:, :], start=True, stop=True).then_inc(s_w, 1)
                pe.wait_ge(s_wc, 8)

                def similarity(g, u):
                    pe.wait_ge(s_relu, g + 1)
                    after(pe, s_sub, g - 1)
                    for s in range(4):
                        ins = nc.tensor.matmul(psim[u][:, s, :], hT[u][:, P * s:P * s + P], simw[:, :], start=True, stop=True, skip_group_check=True)
                    ins.then_inc(s_sim, 1)

                def turn(g, u):
                    pe.wait_ge(s_prob, g + 1)
                    after(pe, s_pTc, g - 1)
                    for s in range(2):
                        ins = nc.tensor.transpose(pp[u][:, P * s:P * s + P],
                                                  prob[u][:, 2 * s:2 * s + 2, :].rearrange("p a b -> p (a b)"), k["ident"][:, :])
                    ins.then_inc(s_pT, 1)

                def embed(g, u):
                    pe.wait_ge(s_pTc, g + 1)
                    after(pe, s_out, g - 1)
                    for s in range(2):
                        ins = nc.tensor.matmul(pe_[u][:, 2 * P * s:2 * P * s + 2 * P], pT[u][:, P * s:P * s + P], k["bins"][:, :],
                                               start=True, stop=True, skip_group_check=True)
                    ins.then_inc(s_emb, 1)

                for g, u, first, last, lead in pairs(pe, NG):
                    similarity(g, u)
                    if not first:
                        turn(g - 1, 1 - u)
                    if not lead:
                        embed(g - 2, u)
                turn(NG - 1, 1)
                embed(NG - 2, 0)
                embed(NG - 1, 1)

            @block.scalar
            def _(act):
                def relu(g, u):
                    after(act, s_sim, g - 1)
                    nc.scalar.activation(hT[u][:, :], tok[:, bass.ds(g * HALF, HALF)], ACT.Relu, bias=k["b1"], scale=w1[:, 0:1]).then_inc(s_relu, 1)

                def exponent(g, u):
                    act.wait_ge(s_sub, g + 1)
                    nc.scalar.activation(prob[u][:, :, 1:BINS], ex[u][:, :, 1:BINS], ACT.Exp).then_inc(s_exp, 1)

                def keep_turned(g, u):
                    act.wait_ge(s_pT, g + 1)
                    nc.scalar.copy(pT[u][:, :], pp[u][:, 0:2 * P]).then_inc(s_pTc, 1)

                def keep(g, u):
                    act.wait_ge(s_emb, g + 1)
                    nc.scalar.copy(H[:, bass.ds(g * 4, 4), :], pe_[u][:, :].rearrange("p (s d) -> p s d", s=4)).then_inc(s_out, 1)

                act.wait_ge(s_in, 64)
                act.wait_ge(s_tok[0], 16)
                relu(0, 0)
                for g, u, first, last, lead in pairs(act, NG):
                    if isinstance(g, int) and g == NG // 4 - 1:
                        for c in range(1, 4):
                            act.wait_ge(s_tok[c], 16)
                    if not last:
                        relu(g + 1, 1 - u)
                    exponent(g, u)
                    if not first:
                        keep_turned(g - 1, 1 - u)
                    if not lead:
                        keep(g - 2, u)
                keep_turned(NG - 1, 1)
                keep(NG - 2, 0)
                keep(NG - 1, 1)

            @block.vector
            def _(dve):
                for u in range(2):
                    nc.vector.memset(prob[u][:, :, :], 0.0).then_inc(s_wc, 1)
                nc.vector.memset(simw[:, :], 0.0).then_inc(s_wc, 1)
                dve.wait_ge(s_in, 64)
                nc.vector.tensor_copy(til_f[:, :], til_i[:, :]).then_inc(s_f, 1)
                dve.wait_ge(s_w, 2)
                nc.vector.tensor_copy(w2T[:, :], pp[1][:, 0:P]).then_inc(s_wc, 1)
                nc.vector.tensor_scalar(live[:, :], pp[0][:, 0:NT], 0.0, None, ALU.not_equal).then_inc(s_wc, 1)
                nc.vector.tensor_scalar(dead[:, :], pp[0][:, 0:NT], 0.0, None, ALU.is_equal).then_inc(s_wc, 1)
                dve.wait_ge(s_w, 4)
                nc.vector.tensor_copy(simw[:, 0:BINS], pa[:, 0:BINS]).then_inc(s_wc, 1)
                nc.vector.tensor_copy(simb[:, 0:BINS], pa[:, P:P + BINS]).then_inc(s_wc, 1)
                dve.wait_ge(s_wc, 8)

                def shift(g, u):
                    st = Steps(dve, s_dve, g, 2)
                    dve.wait_ge(s_sim, g + 1)
                    st.link(nc.vector.tensor_tensor(ex[u][:, :, 1:BINS], psim[u][:, :, 1:BINS],
                                                    simb[:, 1:BINS].unsqueeze(1).broadcast_to([P, 4, BINS - 1]), ALU.add))
                    st.link(nc.vector.tensor_reduce(mx[u][:, :], ex[u][:, :, 1:BINS], AX.X, ALU.max))
                    nc.vector.tensor_tensor(ex[u][:, :, 1:BINS], ex[u][:, :, 1:BINS], spread(mx[u][:, :], BINS - 1),
                                            ALU.subtract).then_inc(s_sub, 1)
                    st.close()

                def weigh(g, u):
                    st = Steps(dve, s_dve2, g, 3)
                    dve.wait_ge(s_exp, g + 1)
                    st.link(nc.vector.tensor_reduce(sm[u][:, :], prob[u][:, :, 1:BINS], AX.X, ALU.add))
                    st.link(nc.vector.reciprocal(inv[u][:, :], sm[u][:, :]))
                    st.link(nc.vector.tensor_tensor(inv[u][:, :], inv[u][:, :], live[:, bass.ds(g * 4, 4)], ALU.mult))
                    nc.vector.tensor_copy(prob[u][:, :, 0:1].rearrange("p a b -> p (a b)"), dead[:, bass.ds(g * 4, 4)])
                    nc.vector.tensor_tensor(prob[u][:, :, 1:BINS], prob[u][:, :, 1:BINS], spread(inv[u][:, :], BINS - 1),
                                            ALU.mult).then_inc(s_prob, 1)
                    st.close()

                def take_stats(g):
                    dve.wait_ge(s_out, g + 1)
                    for t in range(4):
                        nc.vector.bn_stats(stats[:, g * 4 + t, :], H[:, g * 4 + t, :])

                for g, u, first, last, lead in pairs(dve, NG):
                    if not first:
                        weigh(g - 1, 1 - u)
                    shift(g, u)
                    if not isinstance(g, int) or g >= 4:
                        take_stats(g - 4)
                weigh(NG - 1, 1)
                for g in range(NG - 4, NG):
                    take_stats(g)


def constants(nc, m):
    k = {n: m.sb(n, [P, P]) for n in ("ident", "ones", "row0", "Wq", "Wk", "Wv", "Wg", "Wo")}
    k["banks"] = m.ctx.enter_context(nc.psum_tensor("banks", [P, 8, HALF], F32))
    k["W1T"] = m.sb("W1T", [P, 4 * P])
    k["W2T"] = m.sb("W2T", [P, 4, P])
    k["fc1T"] = m.sb("fc1T", [P, 4, P])
    k["binsT"] = m.sb("binsT", [P, BINS])
    k["bins"] = m.sb("bins", [P, 2 * P])
    k["neg_half"] = m.sb("neg_half", [P, 16])
    k["cols"] = m.sb("cols", [P, 16])
    for j, n in enumerate(("b1", "ln1_g", "ln1_b", "ln2_g", "ln2_b", "time_decay", "rms", "tm_q", "tm_k", "tm_v", "tm_g")):
        k[n] = k["cols"][:, j:j + 1]
    return k


LEVELS = (64, 32, 16, 8, 4)
NL = len(LEVELS)
NEAR = LEVELS[-1]
UNIT = 2 * P
STEP = ((0, 3), (3, 5))
HEADS, DH = 4, 32


def attention_tables():
    see = np.zeros((P, NL, P), np.float32)
    for l, b in enumerate(LEVELS):
        for c in range(P):
            see[c // b * b:c // b * b + b, l, c] = 1.0
    blk = np.kron(np.eye(HEADS, dtype=np.float32), np.ones((DH, DH), np.float32))
    pick = np.tile(2 * np.kron(np.eye(HEADS, dtype=np.float32), np.ones((DH, 1), np.float32)), (1, P // HEADS))
    up = np.tile(np.arange(P + 1, dtype=np.float32), (P, 1))
    return {"c_see": see.reshape(P, NL * P), "c_heads": blk, "c_pick": pick, "c_up": up, "c_down": up[:, ::-1].copy()}


def double_stats(nc, k, stats, mean, rstd, rstd2):
    with ExitStack() as ctx:
        m = Mem(nc, ctx, "dst", k["banks"])
        var, sq, var2 = (m.sb(n, [P, NT]) for n in ("var", "sq", "var2"))
        s_dve, s_var, s_out = m.sem("dve"), m.sem("var"), m.sem("guess")
        s_act = m.sem("act")
        TT, TS = nc.vector.tensor_tensor, nc.vector.tensor_scalar
        with nc.Block() as block:
            @block.vector
            def _(dve):
                st = Steps(dve, s_dve)
                TT(mean[:, :], stats[:, :, 1], stats[:, :, 4], ALU.add)
                TT(sq[:, :], stats[:, :, 1], stats[:, :, 4], ALU.subtract)
                st.link(TT(var[:, :], stats[:, :, 2], stats[:, :, 5], ALU.add))
                TS(mean[:, :], mean[:, :], 0.5, None, ALU.mult)
                TS(var[:, :], var[:, :], 1.0 / D, None, ALU.mult)
                st.link(TT(sq[:, :], sq[:, :], sq[:, :], ALU.mult))
                st.link(nc.vector.scalar_tensor_tensor(out=var[:, :], in0=sq[:, :], scalar=0.25, in1=var[:, :], op0=ALU.mult, op1=ALU.add))
                TS(var2[:, :], var[:, :], 1e-5, None, ALU.add).then_inc(s_var, 1)
                dve.wait_ge(s_out, 1)
                refine_root(nc, st, rstd, var2, sq)
                st.link(TT(sq[:, :], rstd[:, :], rstd[:, :], ALU.mult))
                st.link(TT(sq[:, :], sq[:, :], var[:, :], ALU.mult))
                TS(var2[:, :], sq[:, :], 1e-5, None, ALU.add).then_inc(s_var, 1)
                dve.wait_ge(s_out, 2)
                refine_root(nc, st, rstd2, var2, sq)
                TT(rstd2[:, :], rstd2[:, :], rstd[:, :], ALU.mult)

            @block.scalar
            def _(act):
                for j, dst in enumerate((rstd, rstd2)):
                    act.wait_ge(s_var, j + 1)
                    guess_root(nc, act, dst, var2, s_out, s_act, j)


def attention(nc, w, k, H, X2, mean, rstd, stats):
    with ExitStack() as ctx:
        m = Mem(nc, ctx, "at", k["banks"])
        rstd2 = m.sb("rstd2", [P, NT])
        double_stats(nc, k, stats, mean, rstd, rstd2)
        xn = m.sb("xn", [P, TILES, P])
        flat = lambda t: t[:, :, :].rearrange("p a b -> p (a b)")
        hs = m.sb("hs", [P, SEQ + 1])
        diff = flat(xn)
        kend = flat(xn)
        xm = [m.sb(f"xm{j}", [P, SEQ]) for j in range(4)]
        q, kk = m.sb("q", [P, SEQ]), m.sb("k", [P, SEQ])
        sq = [m.sb(f"sq{j}", [P, SEQ]) for j in range(2)]
        z, qz = sq
        n_near = lambda d: SEQ // NEAR * (NEAR - d)
        near = [xm[0][:, :], xm[1][:, 0:n_near(1)], z[:, 0:n_near(2)], z[:, n_near(2):n_near(2) + n_near(3)]]
        tmp = hs[:, 1:1 + n_near(1)]
        v = m.sb("v", [P, TILES, P])
        xvc = m.sb("xvc", [P, NL, SEQ // 2])
        vc = m.sb("vc", [P, NL, SEQ // UNIT, P])
        vT, rg, dv = m.sb("vT", [P, SEQ]), m.sb("rg", [P, SEQ]), m.sb("dv", [P, SEQ])
        kc, qc = m.sb("kc", [P, NL, SEQ // 2]), m.sb("qc", [P, NL, SEQ // 2])
        qin = m.sb("qin", [P, SEQ])
        pm = [m.sb(f"pm{s}", [P, HEADS, (hi - lo) * P]) for s, (lo, hi) in enumerate(STEP)]
        see, heads, pick = m.sb("see", [P, NL * P]), m.sb("heads", [P, P]), m.sb("pick", [P, P])
        up, down = m.sb("up", [P, P + 1]), m.sb("down", [P, P + 1])
        pw, rpw = m.sb("pw", [P, P + 1]), m.sb("rpw", [P, P + 1])
        lnl = m.sb("lnl", [P, 2])
        state = m.sb("state", [P, TILES, P])
        kendT = m.sb("kendT", [P, TILES - 1, P])
        ssv, root = m.sb("ssv", [P, 16]), m.sb("root", [P, 16])
        rz = m.sb("rz", [P, TILES * HEADS])
        half = m.sb("half", [P, 16])
        PS = k["banks"]
        two_banks = lambda b, n=2 * HALF: PS[:, b:b + 2, :].rearrange("p a b -> p (a b)")[:, 0:n]
        S = {n: m.sem(n) for n in (
            "in lam ready xn turned hs diff mix proj projc xvc ss ssv root rms rb qn exp "
            "v vT g vc01 vc23 vc4 kt u Zs rzb nearp nearc vsb vTsb gsb vcsb ktsb qk kend kc qc qin near1 qz um state rz rg "
            "scoreA scoreB maskA maskB av att wo x2 dveM dveO dveC").split()}
        left = lambda t, h: t.rearrange("p (n s c) -> p n s c", s=2, c=h)[:, :, 0, :]
        right = lambda t, h: t.rearrange("p (n s c) -> p n s c", s=2, c=h)[:, :, 1, :]
        tiles = lambda t: t.rearrange("p (n t) -> p n t", t=P)
        blocks = lambda t: t.rearrange("p (n c) -> p n c", c=NEAR)
        UNITS, KS = SEQ // UNIT, 2 * (SEQ // UNIT)
        with nc.Block() as block:
            @block.sync
            def _(sp):
                for dst, src in ((see, "c_see"), (heads, "c_heads"), (pick, "c_pick"), (up, "c_up"), (down, "c_down")):
                    sp.dma_start(dst[:, :], w[src]).then_inc(S["in"], 16)
                sp.wait_ge(S["in"], 80)

            @block.gpsimd
            def _(pool):
                TT = nc.gpsimd.tensor_tensor

                def mix(b, first):
                    pool.wait_ge(S["hs"], 2 * b + 2)
                    TT(diff, hs[:, 1:SEQ + 1], hs[:, 0:SEQ], ALU.subtract).then_inc(S["diff"], 1)
                    pool.wait_ge(S["ssv"], b + 1)
                    TT(root[:, :], ssv[:, :], half[:, :], ALU.pow).then_inc(S["root"], 1)

                def operands(b, first):
                    pool.wait_ge(S["exp"], 2 * b + 2)
                    TT(kend.rearrange("p (n t) -> p n t", t=P), tiles(kk[:, :]), rpw[:, 1:P + 1].unsqueeze(1).broadcast_to([P, TILES, P]),
                       ALU.mult).then_inc(S["kend"], 1)
                    TT(near[0], q[:, :], kk[:, :], ALU.mult).then_inc(S["qk"], 1)
                    if not first:
                        pool.wait_ge(S["scoreB"], KS * b)
                    for l, h in enumerate(LEVELS):
                        ins = TT(kc[:, l, :].rearrange("p (n c) -> p n c", c=h), left(kk[:, :], h),
                                 rpw[:, P - h:P].unsqueeze(1).broadcast_to([P, SEQ // (2 * h), h]), ALU.mult)
                    ins.then_inc(S["kc"], 1)
                    TT(tiles(qin[:, :]), tiles(q[:, :]), pw[:, 1:P + 1].unsqueeze(1).broadcast_to([P, TILES, P]), ALU.mult).then_inc(S["qin"], 1)

                nc.gpsimd.memset(half[:, :], 0.5).then_inc(S["ready"], 1)
                pool.wait_ge(S["ready"], 1)
                pool.wait_ge(S["lam"], 4)
                mix(0, True)
                operands(0, True)
                with pool.Fori(1, BATCH) as b:
                    mix(b, False)
                    operands(b, False)

            @block.scalar
            def _(act):
                def mix(b, first):
                    for j in range(2):
                        act.wait_ge(S["turned"], 2 * b + j + 1)
                        nc.scalar.activation(hs[:, 1 + HALF * j:1 + HALF * j + HALF], PS[:, 6 + j, :], ACT.Identity,
                                             bias=k["ln1_b"], scale=k["ln1_g"]).then_inc(S["hs"], 1)
                    for j in range(4):
                        c = slice(HALF * (j % 2), HALF * (j % 2) + HALF)
                        act.wait_ge(S["proj"], 4 * b + j + 1)
                        nc.scalar.copy((q, kk)[j // 2][:, c], PS[:, 6 + j % 2, :])
                        nc.scalar.activation(sq[j // 2][:, c], PS[:, 6 + j % 2, :], ACT.Square).then_inc(S["projc"], 1)
                    act.wait_ge(S["mix"], 4 * b + 3)
                    for l, h in enumerate(LEVELS):
                        ins = nc.scalar.copy(xvc[:, l, :].rearrange("p (n c) -> p n c", c=h), left(xm[2][:, :], h))
                    ins.then_inc(S["xvc"], 1)
                    for j, a in enumerate((q, kk)):
                        act.wait_ge(S["qn"], 4 * b + 2 * j + 2)
                        nc.scalar.activation(a[:, :], a[:, :], ACT.Exp, scale=k["rms"]).then_inc(S["exp"], 1)

                def operands(b, first):
                    act.wait_ge(S["v"], b + 1)
                    nc.scalar.copy(flat(v), two_banks(2)).then_inc(S["vsb"], 1)
                    act.wait_ge(S["vT"], b + 1)
                    nc.scalar.copy(vT[:, :], two_banks(6)).then_inc(S["vTsb"], 1)
                    if not first:
                        act.wait_ge(S["att"], b)
                    act.wait_ge(S["g"], b + 1)
                    nc.scalar.activation(rg[:, :], two_banks(0), ACT.Tanh, scale=0.5).then_inc(S["gsb"], 1)
                    if not first:
                        act.wait_ge(S["av"], KS * b)
                    for n, (name, b0, lo, hi) in enumerate((("vc01", 2, 0, 2), ("vc23", 6, 2, 4), ("vc4", 0, 4, 5))):
                        act.wait_ge(S[name], b + 1)
                        nc.scalar.copy(vc[:, lo:hi, :, :].rearrange("p a b c -> p (a b c)"), two_banks(b0, HALF * (hi - lo))).then_inc(S["vcsb"], 1)
                    act.wait_ge(S["kt"], b + 1)
                    nc.scalar.copy(flat(kendT), two_banks(2, P * (TILES - 1))).then_inc(S["ktsb"], 1)

                act.wait_ge(S["lam"], 1)
                nc.scalar.activation(lnl[:, 1:2], lnl[:, 0:1], ACT.Exp).then_inc(S["lam"], 1)
                act.wait_ge(S["lam"], 3)
                act.wait_ge(S["in"], 80)
                nc.scalar.activation(pw[:, :], up[:, :], ACT.Exp, scale=lnl[:, 0:1])
                nc.scalar.activation(rpw[:, :], down[:, :], ACT.Exp, scale=lnl[:, 0:1]).then_inc(S["lam"], 1)
                mix(0, True)
                operands(0, True)
                with act.Fori(1, BATCH) as b:
                    mix(b, False)
                    operands(b, False)

            @block.tensor
            def _(pe):
                mm = nc.tensor.matmul

                def mix_part(b, k_):
                    if k_ == 1:
                        pe.wait_ge(S["xn"], b + 1)
                        for j in range(2):
                            for t in range(4):
                                ins = nc.tensor.transpose(PS[:, 6 + j, P * t:P * t + P], xn[:, 4 * j + t, :], k["ident"][:, :])
                            ins.then_inc(S["turned"], 1)
                    if k_ in (4, 5):
                        a = k_ - 4
                        pe.wait_ge(S["mix"], 4 * b + a + 1)
                        for j in range(2):
                            if a:
                                pe.wait_ge(S["projc"], 4 * b + j + 1)
                            else:
                                pe.wait_ge(S["hs"], 2 * b + j + 1)
                            mm(PS[:, 6 + j, :], k[("Wq", "Wk")[a]][:, :], xm[a][:, HALF * j:HALF * j + HALF],
                               start=True, stop=True).then_inc(S["proj"], 1)
                    if k_ == 6:
                        pe.wait_ge(S["projc"], 4 * b + 4)
                        for j in range(2):
                            for t in range(TILES):
                                n = 8 * j + t
                                ins = mm(PS[:, 6, n:n + P], sq[j][:, P * t:P * t + P], k["ones"][:, :],
                                         start=True, stop=True, skip_group_check=True)
                        ins.then_inc(S["ss"], 1)
                    if k_ == 8:
                        pe.wait_ge(S["rms"], b + 1)
                        for j in range(4):
                            for t in range(4):
                                n = 4 * j + t
                                ins = mm(PS[:, (6, 7, 0, 1)[j], P * t:P * t + P], ssv[:, n:n + 1].broadcast_to([P, P]), k["ident"][:, :],
                                         start=True, stop=True, skip_group_check=True)
                            ins.then_inc(S["rb"], 1)

                def operands(b, first):
                    if not first:
                        pe.wait_ge(S["maskB"], KS * b)
                    for t in range(TILES):
                        ins = mm(PS[:, 2 + t // 4, P * (t % 4):P * (t % 4) + P], xm[2][:, P * t:P * t + P], k["Wv"][:, :],
                                 start=True, stop=True, skip_group_check=True)
                    ins.then_inc(S["v"], 1)
                    for name, b0, Wn, x_, bank_free in (("vT", 6, "Wv", 2, 2), ("g", 0, "Wg", 3, 4)):
                        pe.wait_ge(S["qn"], 4 * b + bank_free)
                        for j in range(2):
                            ins = mm(PS[:, b0 + j, :], k[Wn][:, :], xm[x_][:, HALF * j:HALF * j + HALF], start=True, stop=True)
                        ins.then_inc(S[name], 1)
                    pe.wait_ge(S["xvc"], b + 1)
                    for name, b0, lo, hi, free in (("vc01", 2, 0, 2, "vsb"), ("vc23", 6, 2, 4, "vTsb"), ("vc4", 0, 4, 5, "gsb")):
                        pe.wait_ge(S[free], b + 1)
                        for l in range(lo, hi):
                            for g in range(UNITS):
                                ins = mm(PS[:, b0 + l - lo, P * g:P * g + P], xvc[:, l, P * g:P * g + P], k["Wv"][:, :],
                                         start=True, stop=True, skip_group_check=True)
                        ins.then_inc(S[name], 1)
                    pe.wait_ge(S["vcsb"], 3 * b + 1)
                    pe.wait_ge(S["kend"], b + 1)
                    for n in range(TILES - 1):
                        ins = nc.tensor.transpose(PS[:, 2 + n // 4, P * (n % 4):P * (n % 4) + P], kend[:, P * n:P * n + P], k["ident"][:, :])
                    ins.then_inc(S["kt"], 1)
                    pe.wait_ge(S["vcsb"], 3 * b + 2)
                    pe.wait_ge(S["qk"], b + 1)
                    for j in range(2):
                        ins = mm(PS[:, 6 + j, :], heads[:, :], near[0][:, HALF * j:HALF * j + HALF], start=True, stop=True)
                    ins.then_inc(S["nearp"], 1)
                    pe.wait_ge(S["vcsb"], 3 * b + 3)
                    pe.wait_ge(S["near1"], b + 1)
                    mm(PS[:, 0, :], heads[:, :], near[1][:, 0:HALF], start=True, stop=True)
                    mm(PS[:, 1, 0:n_near(1) - HALF], heads[:, :], near[1][:, HALF:n_near(1)], start=True, stop=True).then_inc(S["nearp"], 1)
                    pe.wait_ge(S["ktsb"], b + 1)
                    for n in range(TILES - 1):
                        ins = mm(PS[:, 2 + n // 4, P * (n % 4):P * (n % 4) + P], kendT[:, n, :], v[:, n, :], start=True, stop=True, skip_group_check=True)
                    ins.then_inc(S["u"], 1)
                    pe.wait_ge(S["nearc"], 3 * b + 1)
                    pe.wait_ge(S["qz"], b + 1)
                    mm(PS[:, 6, :], heads[:, :], near[2], start=True, stop=True)
                    mm(PS[:, 7, 0:n_near(3)], heads[:, :], near[3], start=True, stop=True).then_inc(S["nearp"], 1)
                    pe.wait_ge(S["nearc"], 3 * b + 2)
                    for t in range(TILES):
                        ins = mm(PS[:, 0, HEADS * t:HEADS * t + P], qz[:, P * t:P * t + P], pick[:, :], start=True, stop=True, skip_group_check=True)
                    ins.then_inc(S["Zs"], 1)
                    pe.wait_ge(S["rz"], b + 1)
                    pe.wait_ge(S["um"], b + 1)
                    for t in range(TILES):
                        for h in range(HEADS):
                            n = HEADS * t + h
                            ins = mm(PS[DH * h:DH * h + DH, 2 + t // 4, P * (t % 4):P * (t % 4) + P], rz[:, n:n + 1].broadcast_to([P, DH]),
                                     k["ident"][:, :], start=True, stop=True, skip_group_check=True)
                    ins.then_inc(S["rzb"], 1)

                def scores(k_, hs_, name):
                    g, (lo, hi) = k_ // 2, STEP[k_ % 2]
                    for l in range(lo, hi):
                        for h in hs_:
                            r = slice(DH * h, DH * h + DH)
                            ins = mm(PS[:, h, P * (l - lo):P * (l - lo) + P], kc[r, l, P * g:P * g + P], qc[r, l, P * g:P * g + P],
                                     start=True, stop=True, skip_group_check=True)
                    ins.then_inc(S[name], 1)

                def values(k_):
                    g, (lo, hi) = k_ // 2, STEP[k_ % 2]
                    dst = PS[:, 4 + g // 2, UNIT * (g % 2):UNIT * (g % 2) + UNIT]
                    for l in range(lo, hi):
                        later = right(dst, LEVELS[l])
                        for h in range(HEADS):
                            r = slice(DH * h, DH * h + DH)
                            ins = mm(later[r], vc[:, l, g, r], pm[k_ % 2][:, h, P * (l - lo):P * (l - lo) + P],
                                     start=False, stop=False, skip_group_check=True)
                    ins.then_inc(S["av"], 1)

                def core(b, first, last):
                    pe.wait_ge(S["kc"], b + 1)
                    pe.wait_ge(S["qc"], b + 1)
                    pe.wait_ge(S["qin"], b + 1)
                    pe.wait_ge(S["state"], b + 1)
                    if not first:
                        pe.wait_ge(S["x2"], 2 * b)
                    for k_ in range(KS):
                        for name, hs_ in (("A", (0, 1)), ("B", (2, 3))):
                            if k_:
                                pe.wait_ge(S["mask" + name], KS * b + k_)
                            elif name == "B":
                                pe.wait_ge(S["rg"], b + 1)
                            scores(k_, hs_, "score" + name)
                        if k_ % 4 == 0:
                            for n in range(k_, k_ + 4):
                                mm(PS[:, 4 + n // 4, P * (n % 4):P * (n % 4) + P], state[:, n, :], qin[:, P * n:P * n + P],
                                   start=(n % 4 == 0), stop=False, skip_group_check=True)
                        if k_:
                            values(k_ - 1)
                        if not last:
                            mix_part(b + 1, k_)
                    pe.wait_ge(S["maskB"], KS * b + KS)
                    values(KS - 1)
                    if not last:
                        mix_part(b + 1, KS)

                def gather_out(b):
                    pe.wait_ge(S["att"], b + 1)
                    for t in range(TILES):
                        ins = mm(PS[:, 4 + t // 4, P * (t % 4):P * (t % 4) + P], dv[:, P * t:P * t + P], k["Wo"][:, :],
                                 start=True, stop=True, skip_group_check=True)
                    ins.then_inc(S["wo"], 1)

                for k_ in range(KS + 1):
                    mix_part(0, k_)
                operands(0, True)
                core(0, True, False)
                gather_out(0)
                with pe.Fori(1, BATCH - 1) as b:
                    operands(b, False)
                    core(b, False, False)
                    gather_out(b)
                operands(BATCH - 1, False)
                core(BATCH - 1, False, True)
                gather_out(BATCH - 1)

            @block.vector
            def _(dve):
                TT, TS, STT = nc.vector.tensor_tensor, nc.vector.tensor_scalar, nc.vector.scalar_tensor_tensor

                def mix_part(st, b, k_):
                    if k_ == 0:
                        for t in range(TILES):
                            n = b * TILES + t
                            TS(X2[:, n, :], H[:, n, :], mean[:, bass.ds(n, 1)], rstd[:, bass.ds(n, 1)], ALU.subtract, ALU.mult)
                            ins = TS(xn[:, t, :], H[:, n, :], mean[:, bass.ds(n, 1)], rstd2[:, bass.ds(n, 1)], ALU.subtract, ALU.mult)
                        ins.then_inc(S["xn"], 1)
                    if k_ in (3, 4):
                        if k_ == 3:
                            dve.wait_ge(S["diff"], b + 1)
                        for j in range(2 * (k_ - 3), 2 * (k_ - 3) + 2):
                            STT(out=xm[j][:, :], in0=diff, scalar=(k["tm_q"], k["tm_k"], k["tm_v"], k["tm_g"])[j], in1=hs[:, 0:SEQ],
                                op0=ALU.mult, op1=ALU.add).then_inc(S["mix"], 1)
                    if k_ == 6:
                        dve.wait_ge(S["ss"], b + 1)
                        TS(ssv[:, :], PS[:, 6, 0:16], 1.0 / D, None, ALU.mult).then_inc(S["ssv"], 1)
                    if k_ == 7:
                        dve.wait_ge(S["root"], b + 1)
                        st.link(TS(root[:, :], root[:, :], 1e-8, None, ALU.add))
                        nc.vector.reciprocal(ssv[:, :], root[:, :]).then_inc(S["rms"], 1)
                    if k_ == 8:
                        for j in range(4):
                            a, c = (q, kk)[j // 2], slice(HALF * (j % 2), HALF * (j % 2) + HALF)
                            dve.wait_ge(S["rb"], 4 * b + j + 1)
                            TT(a[:, c], a[:, c], PS[:, (6, 7, 0, 1)[j], :], ALU.mult).then_inc(S["qn"], 1)

                def operands(b, first):
                    st = Steps(dve, S["dveO"], b, 10)
                    dve.wait_ge(S["exp"], 2 * b + 2)
                    st.link(nc.vector.tensor_tensor_scan(z[:, :], pw[:, 1:2].broadcast_to([P, SEQ]), kk[:, :], 0.0, ALU.mult, ALU.add))
                    pair = lambda d: STT(out=blocks_out(d), in0=blocks(q[:, :])[:, :, d:NEAR], scalar=pw[:, d:d + 1],
                                         in1=blocks(kk[:, :])[:, :, 0:NEAR - d], op0=ALU.mult, op1=ALU.mult)
                    blocks_out = lambda d: near[d].rearrange("p (n c) -> p n c", c=NEAR - d)
                    pair(1).then_inc(S["near1"], 1)
                    st.link(TT(qz[:, :], q[:, :], z[:, :], ALU.mult))
                    pair(2)
                    pair(3).then_inc(S["qz"], 1)
                    for l, h in enumerate(LEVELS):
                        ins = TT(qc[:, l, :].rearrange("p (n c) -> p n c", c=h), right(q[:, :], h),
                                 pw[:, 0:h].unsqueeze(1).broadcast_to([P, SEQ // (2 * h), h]), ALU.mult)
                    ins.then_inc(S["qc"], 1)
                    dve.wait_ge(S["nearp"], 3 * b + 1)
                    dve.wait_ge(S["vTsb"], b + 1)
                    TT(dv[:, :], vT[:, :], two_banks(6), ALU.mult).then_inc(S["nearc"], 1)
                    later = lambda d, t: blocks(t)[:, :, d:NEAR]
                    earlier = lambda d: blocks(vT[:, :])[:, :, 0:NEAR - d]
                    cut = lambda d, t: t.rearrange("p (n c) -> p n c", c=NEAR - d)
                    dve.wait_ge(S["nearp"], 3 * b + 2)
                    TT(cut(1, tmp), cut(1, two_banks(0, n_near(1))), earlier(1), ALU.mult).then_inc(S["nearc"], 1)
                    dve.wait_ge(S["nearc"], 3 * b + 2)
                    st.link(TT(later(1, dv[:, :]), later(1, dv[:, :]), cut(1, tmp), ALU.add))
                    dve.wait_ge(S["u"], b + 1)
                    TT(state[:, 1:TILES, :], two_banks(2, P * (TILES - 1)).rearrange("p (n c) -> p n c", c=P),
                       heads[:, :].unsqueeze(1).broadcast_to([P, TILES - 1, P]), ALU.mult).then_inc(S["um"], 1)
                    dve.wait_ge(S["um"], b + 1)
                    for n in range(1, TILES - 1):
                        ins = STT(out=state[:, n + 1, :], in0=state[:, n, :], scalar=pw[:, P:P + 1], in1=state[:, n + 1, :], op0=ALU.mult, op1=ALU.add)
                        if n < TILES - 2:
                            st.link(ins)
                        else:
                            ins.then_inc(S["state"], 1)
                    dve.wait_ge(S["Zs"], b + 1)
                    nc.vector.reciprocal(rz[:, :], PS[:, 0, 0:TILES * HEADS]).then_inc(S["rz"], 1)
                    dve.wait_ge(S["nearp"], 3 * b + 3)
                    tmp2, tmp3 = tmp[:, 0:n_near(2)], tmp[:, n_near(2):n_near(1)]
                    TT(cut(2, tmp2), cut(2, PS[:, 6, :]), earlier(2), ALU.mult)
                    TT(cut(3, tmp3), cut(3, PS[:, 7, 0:n_near(3)]), earlier(3), ALU.mult).then_inc(S["nearc"], 1)
                    dve.wait_ge(S["nearc"], 3 * b + 3)
                    st.link(TT(later(2, dv[:, :]), later(2, dv[:, :]), cut(2, tmp2), ALU.add))
                    st.link(TT(later(3, dv[:, :]), later(3, dv[:, :]), cut(3, tmp3), ALU.add))
                    dve.wait_ge(S["rzb"], b + 1)
                    dve.wait_ge(S["gsb"], b + 1)
                    STT(out=rg[:, :], in0=rg[:, :], scalar=1.0, in1=two_banks(2), op0=ALU.add, op1=ALU.mult).then_inc(S["rg"], 1)
                    st.close()

                def core(b, last):
                    st = Steps(dve, S["dveC"], b, 1)
                    stm = Steps(dve, S["dveM"], b + 1, 1)
                    for k_ in range(KS):
                        lo, hi = STEP[k_ % 2]
                        for name, h0, h1 in (("A", 0, 2), ("B", 2, HEADS)):
                            dve.wait_ge(S["score" + name], KS * b + k_ + 1)
                            if k_ >= 2:
                                dve.wait_ge(S["av"], KS * b + k_ - 1)
                            TT(pm[k_ % 2][:, h0:h1, :], PS[:, h0:h1, 0:(hi - lo) * P],
                               see[:, P * lo:P * hi].unsqueeze(1).broadcast_to([P, h1 - h0, (hi - lo) * P]), ALU.mult).then_inc(S["mask" + name], 1)
                        if not last:
                            mix_part(stm, b + 1, k_)
                    if not last:
                        mix_part(stm, b + 1, KS)
                    dve.wait_ge(S["av"], KS * b + KS)
                    dve.wait_ge(S["rg"], b + 1)
                    st.link(TT(dv[:, :], dv[:, :], two_banks(4), ALU.add))
                    TT(dv[:, :], dv[:, :], rg[:, :], ALU.mult).then_inc(S["att"], 1)

                def add_out(b):
                    dve.wait_ge(S["wo"], b + 1)
                    for j in range(2):
                        n = bass.ds(b * TILES + 4 * j, 4)
                        TT(X2[:, n, :], X2[:, n, :], PS[:, 4 + j, :].rearrange("p (a b) -> p a b", a=4), ALU.add).then_inc(S["x2"], 1)
                    dve.wait_ge(S["x2"], 2 * b + 2)
                    for t in range(TILES):
                        nc.vector.bn_stats(stats[:, b * TILES + t, :], X2[:, b * TILES + t, :])

                nc.vector.memset(hs[:, 0:1], 0.0)
                nc.vector.memset(state[:, 0, :], 0.0)
                TS(lnl[:, 0:1], k["time_decay"], 80.0, None, ALU.min).then_inc(S["lam"], 1)
                dve.wait_ge(S["lam"], 2)
                TS(lnl[:, 0:1], lnl[:, 1:2], -1.0, -1e4, ALU.mult, ALU.max).then_inc(S["lam"], 1)
                dve.wait_ge(S["lam"], 4)
                dve.wait_ge(S["in"], 80)
                st0 = Steps(dve, S["dveM"], 0, 1)
                for k_ in range(KS + 1):
                    mix_part(st0, 0, k_)
                operands(0, True)
                core(0, False)
                with dve.Fori(1, BATCH - 1) as b:
                    add_out(b - 1)
                    operands(b, False)
                    core(b, False)
                add_out(BATCH - 2)
                operands(BATCH - 1, False)
                core(BATCH - 1, True)
                add_out(BATCH - 1)


BF16 = mybir.dt.bfloat16
EXPERTS, FF, CAP = 8, 512, 1024
NBLK = CAP // P
ROW = P + EXPERTS


def mlp(nc, w, k, H, X2, mean, rstd, stats, acc):
    with ExitStack() as ctx:
        m = Mem(nc, ctx, "mlp", k["banks"])
        xn = [m.sb(f"xn{u}", [P, 4, P]) for u in range(2)]
        hT = [m.sb(f"hT{u}", [P, HALF]) for u in range(2)]
        hid = [m.sb(f"hid{u}", [P, 4, HALF]) for u in range(2)]
        pt = m.ps()
        pf = [m.ps() for f in range(4)]
        po = [m.ps((P, 4, P)) for u in range(2)]
        s_xn, s_turned, s_h, s_up, s_gelu, s_down, s_out = (m.sem(n) for n in ("xn", "turned", "h", "up", "gelu", "down", "out"))
        s_dve = m.sem("dve")
        s_acc = [m.sem(f"acc{u}") for u in range(2)]
        reset_used(nc)
        G = NT // 4
        acc_v = acc.rearrange("(n p) c -> p n c", p=P)
        with nc.Block() as block:
            @block.sync
            def _(sp):
                for g, u, first, last, lead in pairs(sp, G):
                    sp.wait_ge(s_out, g + 1)
                    sp.dma_start(acc_v[:, bass.ds(g * 4, 4), :], H[:, bass.ds(g * 4, 4), :]).then_inc(s_acc[u], 16)
                for u in range(2):
                    sp.wait_ge(s_acc[u], 8 * G)

            @block.vector
            def _(dve):
                def normalise(g, u):
                    after(dve, s_turned, g - 1)
                    for t in range(4):
                        n = g * 4 + t
                        ins = nc.vector.tensor_scalar(xn[u][:, t, :], X2[:, n, :], mean[:, bass.ds(n, 1)], rstd[:, bass.ds(n, 1)],
                                                      ALU.subtract, ALU.mult)
                    ins.then_inc(s_xn, 1)

                def add(g, u):
                    st = Steps(dve, s_dve, g, 1)
                    c = bass.ds(g * 4, 4)
                    st.link(nc.vector.tensor_tensor(H[:, c, :], H[:, c, :], X2[:, c, :], ALU.add))
                    dve.wait_ge(s_down, g + 1)
                    nc.vector.tensor_tensor(H[:, c, :], H[:, c, :], po[u][:, :, :], ALU.add).then_inc(s_out, 1)
                    dve.wait_ge(s_out, g + 1)
                    for t in range(4):
                        nc.vector.bn_stats(stats[:, g * 4 + t, :], H[:, g * 4 + t, :])
                    st.close()

                normalise(0, 0)
                for g, u, first, last, lead in pairs(dve, G):
                    if not last:
                        normalise(g + 1, 1 - u)
                    if not first:
                        add(g - 1, 1 - u)
                add(G - 1, 1)

            @block.scalar
            def _(act):
                def keep_turned(g, u):
                    act.wait_ge(s_turned, g + 1)
                    nc.scalar.activation(hT[u][:, :], pt[:, :], ACT.Identity, bias=k["ln2_b"], scale=k["ln2_g"]).then_inc(s_h, 1)

                keep_turned(0, 0)
                for g, u, first, last, lead in pairs(act, G):
                    for f in range(4):
                        act.wait_ge(s_up, 4 * g + f + 1)
                        nc.scalar.activation(hid[u][:, f, :], pf[f][:, :], ACT.Gelu).then_inc(s_gelu, 1)
                    if not last:
                        keep_turned(g + 1, 1 - u)

            @block.tensor
            def _(pe):
                def turn(g, u):
                    pe.wait_ge(s_xn, g + 1)
                    after(pe, s_h, g)
                    for t in range(4):
                        ins = nc.tensor.transpose(pt[:, P * t:P * t + P], xn[u][:, t, :], k["ident"][:, :])
                    ins.then_inc(s_turned, 1)

                def up(g, u):
                    pe.wait_ge(s_h, g + 1)
                    for f in range(4):
                        after(pe, s_gelu, 4 * g + f - 3)
                        nc.tensor.matmul(pf[f][:, :], k["W1T"][:, P * f:P * f + P], hT[u][:, :], start=True, stop=True).then_inc(s_up, 1)

                def down(g, u):
                    pe.wait_ge(s_gelu, 4 * g + 4)
                    after(pe, s_out, g - 1)
                    for t in range(4):
                        for f in range(4):
                            ins = nc.tensor.matmul(po[u][:, t, :], hid[u][:, f, P * t:P * t + P], k["W2T"][:, f, :],
                                                   start=(f == 0), stop=(f == 3), skip_group_check=True)
                    ins.then_inc(s_down, 1)

                turn(0, 0)
                for g, u, first, last, lead in pairs(pe, G):
                    up(g, u)
                    if not last:
                        turn(g + 1, 1 - u)
                    if not first:
                        down(g - 1, 1 - u)
                down(G - 1, 1)


def moe_tables():
    tri = np.triu(np.ones((P, P), np.float32), 1)
    nt = np.zeros((P, 2 * NT), np.float32)
    nt[:, 0:NT] = np.arange(NT)
    nt[:, NT:] = np.arange(P)[:, None]
    io = np.zeros((P, P), np.float32) + np.arange(P, dtype=np.float32)
    return {"c_before": tri, "c_ids": nt, "c_iota": io}


def moe_route(nc, w, k, H, mean, rstd, rows, lists, load_next):
    with ExitStack() as ctx:
        m = Mem(nc, ctx, "rt", k["banks"])
        Wr = m.sb("Wr", [P, EXPERTS])
        before, ids, iota = m.sb("before", [P, P]), m.sb("ids", [P, 2 * NT]), m.sb("iota", [P, P])
        xn = [m.sb(f"xn{u}", [P, 4, P]) for u in range(2)]
        xT = [m.sb(f"xT{u}", [P, HALF]) for u in range(2)]
        E8 = lambda n, dt=F32: m.sb(n, [P, EXPERTS], dt)
        EN = lambda n, dt=F32: m.sb(n, [P, EXPERTS, NT], dt)
        lg, below, mask, eq, pref, tot = EN("lg"), EN("below"), EN("mask"), EN("eq"), EN("pref"), EN("tot")
        expo, prob = EN("expo"), m.sb("prob", [P, NT, EXPERTS])
        part, blk = EN("part"), EN("blk")
        posi, parti, blki = EN("posi", I32), EN("parti", I32), EN("blki", I32)
        mx, cnt, rs, need = E8("mx"), E8("cnt"), E8("rs"), E8("need")
        mx8, dg = m.sb("mx8", [EXPERTS, 1]), m.sb("dg", [EXPERTS, EXPERTS])
        cand, bit, take = E8("cand", I32), E8("bit", I32), E8("take", I32)
        ROUNDS = 31
        bits = m.sb("bits", [P, ROUNDS + 1, EXPERTS], I32)
        onep = [m.sb(f"onep{u}", [P, 8, P], BF16) for u in range(2)]
        wide = [m.sb(f"wide{u}", [P, 8, P], BF16) for u in range(2)]
        iotab = m.sb("iotab", [P, 8, P], BF16)
        oneb = [m.sb(f"oneb{u}", [P, NT, 8]) for u in range(2)]
        rhs = [m.sb(f"rhs{u}", [P, NT, 16], BF16) for u in range(2)]
        half_id = m.sb("half_id", [P, 16])
        pt = [m.ps() for u in range(2)]
        pl = [m.ps((P, 4, P)) for u in range(2)]
        pa, pb, pc, pd = m.ps(), m.ps(), m.ps(), m.ps()
        two = lambda n: [m.sem(f"{n}{u}") for u in range(2)]
        s_xn, s_turned, s_xT, s_lg, s_lgc, s_wp = (m.sem(n) for n in ("xn", "turned", "xT", "lg", "lgc", "wp"))
        s_row, s_next = two("row"), m.sem("next")
        cnt16, ones16 = m.sb("cnt16", [P, EXPERTS], BF16), m.sb("ones16", [P, P], BF16)
        Wp = m.sb("Wp", [P, P])
        s_in, s_pe, s_dve, s_act, s_dve2, s_cnt, s_mask, s_dve3 = (m.sem(n) for n in (
            "in", "pe", "dve", "act", "dve2", "cnt", "mask", "dve3"))
        s_dve3b, s_dve4 = m.sem("dve3b"), m.sem("dve4")
        s_onep, s_oused, s_wide, s_rhs, s_dve5 = (m.sem(n) for n in ("onep", "oused", "wide", "rhs", "dve5"))
        CH = NT // 8
        G = NT // 4
        rows_v = rows.rearrange("(n p) c -> p n c", p=P)
        with nc.Block() as block:
            @block.sync
            def _(sp):
                for dst, src in ((Wr, "L0_ffn_Wr"), (before, "c_before"), (ids, "c_ids"), (iota, "c_iota")):
                    sp.dma_start(dst[:, :], w[src]).then_inc(s_in, 16)
                for g, u, first, last, lead in pairs(sp, G):
                    sp.wait_ge(s_xn, g + 1)
                    sp.dma_start(rows_v[:, bass.ds(g * 4, 4), 0:P], xn[u][:, :, :]).then_inc(s_row[u], 16)
                load_next(sp, s_next)
                for u in range(2):
                    sp.wait_ge(s_row[u], 8 * G)
                sp.wait_ge(s_in, 64)

            @block.vector
            def _(dve):
                def normalise(g, u):
                    after(dve, s_turned, g - 1)
                    after(dve, s_row[u], 8 * (g - u))
                    for t in range(4):
                        n = g * 4 + t
                        ins = nc.vector.tensor_scalar(xn[u][:, t, :], H[:, n, :], mean[:, bass.ds(n, 1)], rstd[:, bass.ds(n, 1)],
                                                      ALU.subtract, ALU.mult)
                    ins.then_inc(s_xn, 1)

                dve.wait_ge(s_in, 64)
                nc.vector.memset(Wp[:, :], 0.0).then_inc(s_wp, 1)
                dve.wait_ge(s_wp, 1)
                nc.vector.tensor_copy(Wp[:, 0:EXPERTS], Wr[:, :]).then_inc(s_wp, 1)
                normalise(0, 0)
                for g, u, first, last, lead in pairs(dve, G):
                    if not last:
                        normalise(g + 1, 1 - u)
                    dve.wait_ge(s_lg, g + 1)
                    nc.vector.tensor_copy(lg[:, :, bass.ds(g * 4, 4)], pl[u][:, :, 0:EXPERTS].rearrange("p t e -> p e t")).then_inc(s_lgc, 1)

            @block.scalar
            def _(act):
                for g, u, first, last, lead in pairs(act, G):
                    act.wait_ge(s_turned, g + 1)
                    nc.scalar.copy(xT[u][:, :], pt[u][:, :]).then_inc(s_xT, 1)

            @block.tensor
            def _(pe):
                def turn(g, u):
                    pe.wait_ge(s_xn, g + 1)
                    after(pe, s_xT, g - 1)
                    for t in range(4):
                        ins = nc.tensor.transpose(pt[u][:, P * t:P * t + P], xn[u][:, t, :], k["ident"][:, :])
                    ins.then_inc(s_turned, 1)

                turn(0, 0)
                pe.wait_ge(s_wp, 2)
                for g, u, first, last, lead in pairs(pe, G):
                    if not last:
                        turn(g + 1, 1 - u)
                    pe.wait_ge(s_xT, g + 1)
                    after(pe, s_lgc, g - 1)
                    for t in range(4):
                        ins = nc.tensor.matmul(pl[u][:, t, :], xT[u][:, P * t:P * t + P], Wp[:, :], start=True, stop=True, skip_group_check=True)
                    ins.then_inc(s_lg, 1)
        flat = lambda t: t[:, :, :].rearrange("p a b -> p (a b)")
        with nc.Block() as block:
            @block.tensor
            def _(pe):
                pe.wait_ge(s_dve, 1)
                nc.tensor.transpose(pa[0:EXPERTS, 0:P], mx[:, :], k["ident"][:, :]).then_inc(s_pe, 1)
                pe.wait_ge(s_dve, 3)
                nc.tensor.matmul(pb[:, 0:EXPERTS], k["ones"][0:EXPERTS, :], dg[:, :], start=True, stop=True).then_inc(s_pe, 1)
                pe.wait_ge(s_dve, 5)
                nc.tensor.matmul(pa[:, 0:EXPERTS], k["ones"][:, :], cnt[:, :], start=True, stop=True).then_inc(s_pe, 1)
                with pe.Fori(0, ROUNDS) as r:
                    pe.wait_ge(s_cnt, r + 1)
                    nc.tensor.matmul(pb[:, 0:EXPERTS], ones16[:, :], cnt16[:, :], start=True, stop=True).then_inc(s_mask, 1)
                pe.wait_ge(s_dve2, 1)
                nc.tensor.matmul(pa[:, 0:EXPERTS], k["ones"][:, :], cnt[:, :], start=True, stop=True)
                nc.tensor.matmul(pc[:, :], before[:, :], flat(eq), start=True, stop=True)
                nc.tensor.matmul(pd[:, :], k["ones"][:, :], flat(eq), start=True, stop=True).then_inc(s_pe, 1)
                pe.wait_ge(s_dve2, 2)
                nc.tensor.matmul(pa[:, :], before[:, :], flat(mask), start=True, stop=True)
                nc.tensor.matmul(pb[:, :], k["ones"][:, :], flat(mask), start=True, stop=True).then_inc(s_pe, 1)

            @block.scalar
            def _(act):
                act.wait_ge(s_dve, 4)
                nc.scalar.activation(flat(expo), flat(below), ACT.Exp, scale=-1.0).then_inc(s_act, 1)

            @block.vector
            def _(dve):
                st = Steps(dve, s_dve)
                st.link(nc.vector.tensor_reduce(mx[:, :], lg[:, :, :], AX.X, ALU.max))
                dve.wait_ge(s_pe, 1)
                st.link(nc.vector.tensor_reduce(mx8[:, :], pa[0:EXPERTS, 0:P], AX.X, ALU.max))
                st.link(nc.vector.tensor_scalar(dg[:, :], k["ident"][0:EXPERTS, 0:EXPERTS], mx8[:, 0:1], None, ALU.mult))
                dve.wait_ge(s_pe, 2)
                nc.vector.tensor_copy(mx[:, :], pb[:, 0:EXPERTS]).then_inc(s_dve3, 1)
                dve.wait_ge(s_dve3, 1)
                st.link(nc.vector.tensor_tensor(below[:, :, :], spread(mx[:, :], NT), lg[:, :, :], ALU.subtract))
                dve.wait_ge(s_act, 1)
                st.link(nc.vector.tensor_reduce(cnt[:, :], expo[:, :, :], AX.X, ALU.add))
                dve.wait_ge(s_pe, 3)
                st.link(nc.vector.reciprocal(rs[:, :], pa[:, 0:EXPERTS]))
                st.link(nc.vector.tensor_tensor(prob[:, :, :], expo[:, :, :].rearrange("p e t -> p t e"),
                                                rs[:, :].unsqueeze(1).broadcast_to([P, NT, EXPERTS]), ALU.mult))
                for r in range(ROUNDS):
                    nc.vector.memset(bits[:, r, :], 1 << (ROUNDS - 1 - r))
                nc.vector.memset(bits[:, ROUNDS, :], 0)
                nc.vector.memset(ones16[:, :], 1.0)
                st.link(nc.vector.memset(cand[:, :], 1 << (ROUNDS - 1)))
                with dve.Fori(0, ROUNDS) as r:
                    s2 = Steps(dve, s_dve3b, r, 3)
                    s2.link(nc.vector.tensor_tensor(mask[:, :, :], below[:, :, :], spread(cand[:, :].bitcast(F32), NT), ALU.is_lt))
                    with nc.allow_low_precision(reason="counts of up to 64, exact in bfloat16"):
                        nc.vector.tensor_reduce(cnt16[:, :], mask[:, :, :], AX.X, ALU.add).then_inc(s_cnt, 1)
                    nc.vector.tensor_tensor(take[:, :], cand[:, :], bits[:, r + 1, :], ALU.bitwise_or)
                    dve.wait_ge(s_mask, r + 1)
                    s2.link(nc.vector.scalar_tensor_tensor(out=bit[:, :], in0=pb[:, 0:EXPERTS], scalar=float(CAP), in1=bits[:, r, :],
                                                           op0=ALU.is_ge, op1=ALU.mult))
                    s2.link(nc.vector.tensor_tensor(cand[:, :], take[:, :], bit[:, :], ALU.bitwise_xor))
                    s2.close()
                T = spread(cand[:, :].bitcast(F32), NT)
                nc.vector.tensor_tensor(eq[:, :, :], below[:, :, :], T, ALU.is_equal)
                st.link(nc.vector.tensor_tensor(mask[:, :, :], below[:, :, :], T, ALU.is_lt))
                nc.vector.tensor_reduce(cnt[:, :], mask[:, :, :], AX.X, ALU.add).then_inc(s_dve2, 1)
                dve.wait_ge(s_pe, 4)
                nc.vector.tensor_scalar(need[:, :], pa[:, 0:EXPERTS], -1.0, float(CAP), ALU.mult, ALU.add)

                def ahead(within, whole):
                    st.link(nc.vector.tensor_copy(flat(tot), whole))
                    for e in range(EXPERTS):
                        ins = nc.vector.tensor_tensor_scan(pref[:, e, :], k["ones"][:, 0:1].broadcast_to([P, NT]), tot[:, e, :], 0.0, ALU.mult, ALU.add)
                    st.link(ins)
                    st.link(nc.vector.tensor_tensor(flat(pref), flat(pref), flat(tot), ALU.subtract))
                    st.link(nc.vector.tensor_tensor(flat(pref), flat(pref), within, ALU.add))

                ahead(pc[:, :], pd[:, :])
                st.link(nc.vector.tensor_tensor(pref[:, :, :], pref[:, :, :], spread(need[:, :], NT), ALU.is_lt))
                st.link(nc.vector.tensor_tensor(eq[:, :, :], eq[:, :, :], pref[:, :, :], ALU.mult))
                nc.vector.tensor_tensor(mask[:, :, :], mask[:, :, :], eq[:, :, :], ALU.add).then_inc(s_dve2, 1)
                dve.wait_ge(s_pe, 5)
                ahead(pa[:, :], pb[:, :])
                st.link(nc.vector.tensor_scalar(flat(eq), flat(mask), -65536.0, 65536.0, ALU.mult, ALU.add))
                st.link(nc.vector.tensor_tensor(flat(posi), flat(pref), flat(eq), ALU.add))
                nc.vector.tensor_scalar(flat(parti), flat(posi), P - 1, None, ALU.bitwise_and)
                st.link(nc.vector.tensor_scalar(flat(blki), flat(posi), 7, None, ALU.logical_shift_right))
                nc.vector.tensor_copy(flat(part), flat(parti))
                st.link(nc.vector.tensor_copy(flat(blk), flat(blki)))

            @block.sync
            def _(sp):
                sp.wait_ge(s_dve, 7)
                sp.dma_start(rows_v[:, :, P:ROW], prob[:, :, :]).then_inc(s_in, 16)
                sp.wait_ge(s_in, 80)
                sp.wait_ge(s_next, 16 * 13)
        with nc.Block() as block:
            @block.vector
            def _(dve):
                nc.vector.tensor_copy(iotab[:, :, :], iota[:, :].unsqueeze(1).broadcast_to([P, 8, P])).then_inc(s_wp, 1)
                dve.wait_ge(s_wp, 3)

                def blocks(e, u):
                    st = Steps(dve, s_dve4, e, 1)
                    st.link(nc.vector.tensor_tensor(oneb[u][:, :, :], iota[:, 0:8].unsqueeze(1).broadcast_to([P, NT, 8]),
                                                    spread(blk[:, e, :], 8), ALU.is_equal))
                    nc.vector.tensor_tensor(rhs[u][:, :, 0:8], oneb[u][:, :, :], spread(ids[:, 0:NT], 8), ALU.mult)
                    nc.vector.tensor_tensor(rhs[u][:, :, 8:16], oneb[u][:, :, :], spread(ids[:, NT:2 * NT], 8), ALU.mult).then_inc(s_rhs, 1)
                    st.close()

                def places(e):
                    for c in range(CH):
                        dve.wait_ge(s_wide, CH * e + c + 1)
                        after(dve, s_oused, CH * e + c - 1)
                        nc.vector.tensor_tensor(onep[c % 2][:, :, :], iotab[:, :, :], wide[c % 2][:, :, :], ALU.is_equal).then_inc(s_onep, 1)

                def take_list(e, u):
                    st = Steps(dve, s_dve5, e, 2)
                    dve.wait_ge(s_oused, CH * e + CH)
                    st.link(nc.vector.tensor_copy(half_id[:, :], (pa, pb)[u][:, 0:16]))
                    st.link(nc.vector.scalar_tensor_tensor(out=lists[:, e, :], in0=half_id[:, 0:8], scalar=float(P), in1=half_id[:, 8:16],
                                                           op0=ALU.mult, op1=ALU.add))
                    st.close()

                blocks(0, 0)
                for e, u, first, last, lead in pairs(dve, EXPERTS):
                    places(e)
                    if not last:
                        blocks(e + 1, 1 - u)
                    take_list(e, u)

            @block.scalar
            def _(act):
                for e, u, first, last, lead in pairs(act, EXPERTS):
                    for c in range(CH):
                        after(act, s_onep, CH * e + c - 1)
                        nc.scalar.copy(wide[c % 2][:, :, :], spread(part[:, e, bass.ds(8 * c, 8)], P)).then_inc(s_wide, 1)

            @block.tensor
            def _(pe):
                for e, u, first, last, lead in pairs(pe, EXPERTS):
                    pe.wait_ge(s_rhs, e + 1)
                    for c in range(CH):
                        pe.wait_ge(s_onep, CH * e + c + 1)
                        for t in range(8):
                            n = 8 * c + t
                            ins = nc.tensor.matmul((pa, pb)[u][:, 0:16], onep[c % 2][:, t, :], rhs[u][:, n, :], start=(n == 0), stop=(n == NT - 1))
                        ins.then_inc(s_oused, 1)


def moe_experts(nc, w, k, rows, acc, lists):
    with ExitStack() as ctx:
        m = Mem(nc, ctx, "ex", k["banks"])
        two = lambda n: [m.sem(f"{n}{u}") for u in range(2)]
        W1 = [m.sb(f"W1{u}", [P, FF]) for u in range(2)]
        W2 = [m.sb(f"W2{u}", [P, 4, D]) for u in range(2)]
        bs = [m.sb(f"bs{u}", [P, 4]) for u in range(2)]
        b1r, b1 = m.sb("b1r", [EXPERTS * 4, P]), m.sb("b1", [P, EXPERTS * 4])
        b2 = [m.sb(f"b2{u}", [P, D]) for u in range(2)]
        sel = [m.sb(f"sel{u}", [P, NBLK, ROW]) for u in range(2)]
        selT = [m.sb(f"selT{u}", [P, HALF]) for u in range(2)]
        hid = [m.sb(f"hid{u}", [P, 4, HALF]) for u in range(2)]
        y = [m.sb(f"y{u}", [P, NBLK, D]) for u in range(2)]
        wt = [m.sb(f"wt{u}", [P, NBLK]) for u in range(2)]
        pt = [m.ps() for u in range(2)]
        pf = [m.ps() for f in range(4)]
        po = [m.ps((P, 4, P)) for u in range(2)]
        s_w, s_gather, s_scatter = two("w"), two("gather"), two("scatter")
        s_turned, s_selT, s_up, s_gelu, s_down, s_out, s_wt, s_zero = (m.sem(n) for n in (
            "turned", "selT", "up", "gelu", "down", "out", "wt", "zero"))
        ADDS = 16 * NBLK
        W1_d, W2_d = w["L0_ffn_W1"], w["L0_ffn_W2"]
        s_b1 = m.sem("b1")
        with nc.Block() as block:
            @block.sync
            def _(sp):
                sp.dma_start(b1r[:, :], w["L0_ffn_b1"].rearrange("e (f p) -> (e f) p", p=P)).then_inc(s_b1, 16)

            @block.tensor
            def _(pe):
                pe.wait_ge(s_b1, 16)
                nc.tensor.transpose(pt[0][:, 0:EXPERTS * 4], b1r[:, :], k["ident"][0:EXPERTS * 4, 0:EXPERTS * 4]).then_inc(s_b1, 1)

            @block.vector
            def _(dve):
                for u in range(2):
                    nc.vector.memset(b2[u][:, :], 0.0)
                dve.wait_ge(s_b1, 17)
                nc.vector.tensor_copy(b1[:, :], pt[0][:, 0:EXPERTS * 4])
        with nc.Block() as block:
            @block.sync
            def _(sp):
                for e, u, first, last, lead in pairs(sp, EXPERTS):
                    after(sp, s_down, 2 * e - 2)
                    r = bass.ds(e, 1)
                    sp.dma_start(W1[u][:, :], W1_d[r].rearrange("a d f -> (a d) f")).then_inc(s_w[u], 16)
                    sp.dma_start(W2[u][:, :, :], W2_d[r].rearrange("a (f p) d -> p (a f) d", p=P)).then_inc(s_w[u], 16)
                    sp.dma_start(b2[u][0:1, :], w["L0_ffn_b2"][r, :]).then_inc(s_w[u], 16)
                for u in range(2):
                    sp.wait_ge(s_w[u], 48 * EXPERTS // 2)

            @block.gpsimd
            def _(pool):
                def gather(e):
                    for c in range(NBLK):
                        nc.gpsimd.indirect_dma_start(sel[e % 2][:, c, :], None, rows, bass.IndirectOffsetOnAxis(ap=lists[:, e, c:c + 1], axis=0)
                                                     ).then_inc(s_gather[e % 2], 16)

                for e in range(-3, EXPERTS):
                    if e >= -1 and e + 3 < EXPERTS:
                        pool.wait_ge(s_turned, 2 * (e + 1) + 2)
                        pool.wait_ge(s_wt, e + 2)
                    if e + 3 < EXPERTS:
                        gather(e + 3)
                    if e < 0:
                        continue
                    pool.wait_ge(s_out, 2 * e + 2)
                    if e:
                        pool.wait_ge(s_scatter[1 - e % 2], ADDS * ((e + 1) // 2))
                    for c in range(NBLK):
                        nc.gpsimd.indirect_dma_start(acc, bass.IndirectOffsetOnAxis(ap=lists[:, e, c:c + 1], axis=0), y[e % 2][:, c, :], None,
                                                     compute_op=ALU.add).then_inc(s_scatter[e % 2], 16)
                pool.wait_ge(s_scatter[1], ADDS * EXPERTS // 2)

            @block.vector
            def _(dve):
                def weights(e, u):
                    dve.wait_ge(s_gather[u], (e - u) * (ADDS // 2) + ADDS)
                    nc.vector.tensor_copy(bs[u][:, :], b1[:, bass.ds(e * 4, 4)])
                    nc.vector.tensor_copy(wt[u][:, :], sel[u][:, :, bass.ds(e + P, 1)].rearrange("p a b -> p (a b)")).then_inc(s_wt, 1)

                weights(0, 0)
                for e, u, first, last, lead in pairs(dve, EXPERTS):
                    after(dve, s_gelu, 8 * e)
                    after(dve, s_out, 2 * e)
                    if not last:
                        weights(e + 1, 1 - u)
                    dve.wait_ge(s_wt, e + 1)
                    after(dve, s_scatter[u], (e - u) * (ADDS // 2))
                    for h in range(2):
                        dve.wait_ge(s_down, 2 * e + h + 1)
                        for t in range(4):
                            c = 4 * h + t
                            ins = nc.vector.tensor_scalar(y[u][:, c, :], po[h][:, t, :], wt[u][:, c:c + 1], None, ALU.mult)
                        ins.then_inc(s_out, 1)

            @block.scalar
            def _(act):
                def keep_turned(e, u):
                    for h in range(2):
                        act.wait_ge(s_turned, 2 * e + h + 1)
                        nc.scalar.copy(selT[h][:, :], pt[h][:, :]).then_inc(s_selT, 1)

                keep_turned(0, 0)
                for e, u, first, last, lead in pairs(act, EXPERTS):
                    act.wait_ge(s_wt, e + 1)
                    for h in range(2):
                        for f in range(4):
                            act.wait_ge(s_up, 8 * e + 4 * h + f + 1)
                            nc.scalar.activation(hid[h][:, f, :], pf[f][:, :], ACT.Gelu, bias=bs[u][:, f:f + 1]).then_inc(s_gelu, 1)
                    if not last:
                        keep_turned(e + 1, 1 - u)

            @block.tensor
            def _(pe):
                def turn(e, u):
                    pe.wait_ge(s_gather[u], (e - u) * (ADDS // 2) + ADDS)
                    for h in range(2):
                        after(pe, s_selT, 2 * e + h - 1)
                        for t in range(4):
                            ins = nc.tensor.transpose(pt[h][:, P * t:P * t + P], sel[u][:, 4 * h + t, 0:P], k["ident"][:, :])
                        ins.then_inc(s_turned, 1)

                def up(e, u):
                    pe.wait_ge(s_w[u], (e - u) * 24 + 48)
                    for h in range(2):
                        pe.wait_ge(s_selT, 2 * e + h + 1)
                        for f in range(4):
                            after(pe, s_gelu, 8 * e + 4 * h + f - 3)
                            nc.tensor.matmul(pf[f][:, :], W1[u][:, P * f:P * f + P], selT[h][:, :], start=True, stop=True).then_inc(s_up, 1)

                def down(e, u):
                    for h in range(2):
                        pe.wait_ge(s_gelu, 8 * e + 4 * h + 4)
                        after(pe, s_out, 2 * e + h - 1)
                        for t in range(4):
                            for f in range(4):
                                nc.tensor.matmul(po[h][:, t, :], hid[h][:, f, P * t:P * t + P], W2[u][:, f, :],
                                                 start=(f == 0), stop=False, skip_group_check=True)
                            ins = nc.tensor.matmul(po[h][:, t, :], k["row0"][:, :], b2[u][:, :], start=False, stop=True, skip_group_check=True)
                        ins.then_inc(s_down, 1)

                turn(0, 0)
                for e, u, first, last, lead in pairs(pe, EXPERTS):
                    up(e, u)
                    if not last:
                        turn(e + 1, 1 - u)
                    down(e, u)


LORA, FEXP, SLOT = 16, 4, 32


def ffn(nc, w, k, H, mean, rstd, out):
    with ExitStack() as ctx:
        m = Mem(nc, ctx, "ff", k["banks"])
        two = lambda n: [m.sem(f"{n}{u}") for u in range(2)]
        ER = FEXP * SLOT
        raw = m.sb("raw", [P, 6, P])
        gw = m.sb("gw", [P, P])
        Ar = m.sb("Ar", [P, FEXP, LORA])
        A, BT, fc2T = m.sb("A", [P, FEXP, SLOT]), m.sb("BT", [P, FEXP, SLOT]), m.sb("fc2T", [P, FEXP, P])
        M = m.sb("M", [ER, D])
        xn = [m.sb(f"xn{u}", [P, 4, P]) for u in range(2)]
        xT = [m.sb(f"xT{u}", [P, HALF]) for u in range(2)]
        hid = [m.sb(f"hid{u}", [P, FEXP, HALF]) for u in range(2)]
        lg = [m.sb(f"lg{u}", [P, 4, 8]) for u in range(2)]
        ex = [m.sb(f"ex{u}", [P, 4, FEXP]) for u in range(2)]
        sg = [m.sb(f"sg{u}", [P, 4]) for u in range(2)]
        t4 = [m.sb(f"t4{u}", [P, 4]) for u in range(2)]
        wide = [m.sb(f"wide{u}", [P, 4, ER]) for u in range(2)]
        low = [m.sb(f"low{u}", [ER, HALF]) for u in range(2)]
        yo = [m.sb(f"yo{u}", [P, 4, D]) for u in range(2)]
        pt, pl, pg, pw = m.ps(), m.ps(), m.ps((P, 4, P)), m.ps()
        pf = [m.ps() for e in range(2)]
        po = [m.ps((P, 4, D)) for u in range(2)]
        s_in, s_t, s_tc, s_dve = m.sem("in"), m.sem("t"), m.sem("tc"), m.sem("dve")
        (s_xn, s_turned, s_xT, s_fc1, s_hid, s_low, s_lowc, s_gate, s_gatec, s_exp, s_weight, s_wide, s_wT, s_wl, s_o, s_y, s_dve2) = (m.sem(n) for n in (
            "xn", "turned", "xT", "fc1", "hid", "low", "lowc", "gate", "gatec", "exp", "weight", "wide", "wT", "wl", "o", "y", "dve2"))
        s_store = two("store")
        G = NT // 4
        out_v = out.rearrange("b (t p) d -> p (b t) d", p=P)
        with nc.Block() as block:
            @block.sync
            def _(sp):
                for e in range(FEXP):
                    sp.dma_start(raw[:, e, :], w["L1_ffn_fc2_w"][e]).then_inc(s_in, 16)
                sp.dma_start(raw[0:FEXP * LORA, 4, :], w["L1_ffn_lora_B"].rearrange("e r o -> (e r) o")).then_inc(s_in, 16)
                sp.dma_start(raw[0:FEXP, 5, :], w["L1_ffn_gate_w"]).then_inc(s_in, 16)
                sp.dma_start(raw[FEXP:FEXP + 1, 5, :], w["L1_ffn_thr_w"]).then_inc(s_in, 16)
                sp.dma_start(Ar[:, :, :], w["L1_ffn_lora_A"].rearrange("e h r -> h e r")).then_inc(s_in, 16)
                sp.wait_ge(s_in, 128)

            @block.tensor
            def _(pe):
                pe.wait_ge(s_in, 128)
                R_ = FEXP * LORA
                for e in range(FEXP):
                    nc.tensor.transpose(pt[:, P * e:P * e + P], raw[:, e, :], k["ident"][:, :])
                nc.tensor.transpose(pl[:, 0:R_], raw[0:R_, 4, :], k["ident"][0:R_, 0:R_])
                nc.tensor.transpose(pl[:, P:P + FEXP + 1], raw[0:FEXP + 1, 5, :], k["ident"][0:FEXP + 1, 0:FEXP + 1]).then_inc(s_t, 1)
                pe.wait_ge(s_tc, 7)
                for e in range(FEXP):
                    ins = nc.tensor.matmul(pw[SLOT * e:SLOT * e + SLOT, 0:D], BT[:, e, :], fc2T[:, e, :], start=True, stop=True, skip_group_check=True)
                ins.then_inc(s_t, 1)

            @block.vector
            def _(dve):
                for t in (A[:, :, :], BT[:, :, :], gw[:, :]):
                    nc.vector.memset(t, 0.0).then_inc(s_tc, 1)
                dve.wait_ge(s_tc, 3)
                dve.wait_ge(s_t, 1)
                dve.wait_ge(s_in, 128)
                nc.vector.tensor_copy(A[:, :, 0:LORA], Ar[:, :, :]).then_inc(s_tc, 1)
                nc.vector.tensor_copy(fc2T[:, :, :].rearrange("p a b -> p (a b)"), pt[:, :]).then_inc(s_tc, 1)
                nc.vector.tensor_copy(BT[:, :, 0:LORA], pl[:, 0:FEXP * LORA].rearrange("p (e r) -> p e r", e=FEXP)).then_inc(s_tc, 1)
                nc.vector.tensor_copy(gw[:, 0:FEXP + 1], pl[:, P:P + FEXP + 1]).then_inc(s_tc, 1)
                dve.wait_ge(s_t, 2)
                nc.vector.tensor_copy(M[:, :], pw[:, 0:D])
        with nc.Block() as block:
            @block.vector
            def _(dve):
                def normalise(g, u):
                    after(dve, s_turned, g - 1)
                    for t in range(4):
                        n = g * 4 + t
                        ins = nc.vector.tensor_scalar(xn[u][:, t, :], H[:, n, :], mean[:, bass.ds(n, 1)], rstd[:, bass.ds(n, 1)],
                                                      ALU.subtract, ALU.mult)
                    ins.then_inc(s_xn, 1)

                def logits(g, u):
                    st = Steps(dve, s_dve, g, 1)
                    dve.wait_ge(s_gate, g + 1)
                    st.link(nc.vector.tensor_reduce(t4[u][:, :], pg[:, :, 0:FEXP], AX.X, ALU.max))
                    nc.vector.tensor_tensor(lg[u][:, :, 0:FEXP], pg[:, :, 0:FEXP], spread(t4[u][:, :], FEXP), ALU.subtract)
                    nc.vector.tensor_copy(lg[u][:, :, FEXP:FEXP + 1], pg[:, :, FEXP:FEXP + 1]).then_inc(s_gatec, 1)
                    st.close()

                def weigh(g, u):
                    st = Steps(dve, s_dve2, g, 8)
                    TT, TS = nc.vector.tensor_tensor, nc.vector.tensor_scalar
                    e_, t_, g_ = ex[u][:, :, :], t4[u][:, :], sg[u][:, :]
                    dve.wait_ge(s_exp, g + 1)
                    TS(g_, g_, 0.5 / FEXP, 0.5 / FEXP, ALU.mult, ALU.add)
                    st.link(nc.vector.tensor_reduce(t_, e_, AX.X, ALU.add))
                    st.link(nc.vector.reciprocal(t_, t_))
                    st.link(TT(e_, e_, spread(t_, FEXP), ALU.mult))
                    st.link(TT(e_, e_, spread(g_, FEXP), ALU.subtract))
                    st.link(TS(e_, e_, 0.0, None, ALU.max))
                    st.link(nc.vector.tensor_reduce(t_, e_, AX.X, ALU.add))
                    st.link(nc.vector.scalar_tensor_tensor(out=t_, in0=t_, scalar=0.0, in1=t_, op0=ALU.is_equal, op1=ALU.add))
                    st.link(nc.vector.reciprocal(t_, t_))
                    TT(e_, e_, spread(t_, FEXP), ALU.mult).then_inc(s_weight, 1)
                    st.close()

                def product(g, u):
                    dve.wait_ge(s_wT, g + 1)
                    dve.wait_ge(s_lowc, g + 1)
                    nc.vector.tensor_tensor(low[u][:, :], low[u][:, :], pw[:, :], ALU.mult).then_inc(s_wl, 1)

                def add(g, u):
                    dve.wait_ge(s_o, g + 1)
                    after(dve, s_store[u], 8 * (g - u))
                    nc.vector.tensor_tensor(yo[u][:, :, :], H[:, bass.ds(g * 4, 4), :], po[u][:, :, :], ALU.add).then_inc(s_y, 1)

                normalise(0, 0)
                for g, u, first, last, lead in pairs(dve, G):
                    if not first:
                        logits(g - 1, 1 - u)
                    if not last:
                        normalise(g + 1, 1 - u)
                    if not lead:
                        add(g - 2, u)
                    if not first:
                        weigh(g - 1, 1 - u)
                        product(g - 1, 1 - u)
                logits(G - 1, 1)
                add(G - 2, 0)
                weigh(G - 1, 1)
                product(G - 1, 1)
                add(G - 1, 1)

            @block.gpsimd
            def _(pool):
                for g, u, first, last, lead in pairs(pool, G):
                    pool.wait_ge(s_weight, g + 1)
                    nc.gpsimd.tensor_tensor(wide[u][:, :, :].rearrange("p t (e r) -> p (t e) r", e=FEXP),
                                            spread(ex[u][:, :, :].rearrange("p t e -> p (t e)"), SLOT),
                                            spread(k["ones"][:, 0:4 * FEXP], SLOT), ALU.mult).then_inc(s_wide, 1)

            @block.scalar
            def _(act):
                def keep_turned(g, u):
                    act.wait_ge(s_turned, g + 1)
                    nc.scalar.copy(xT[u][:, :], pt[:, :]).then_inc(s_xT, 1)

                def relu(g, u, experts):
                    for e in experts:
                        act.wait_ge(s_fc1, FEXP * g + e + 1)
                        nc.scalar.activation(hid[u][:, e, :], pf[e % 2][:, :], ACT.Relu).then_inc(s_hid, 1)

                def exponent(g, u):
                    act.wait_ge(s_gatec, g + 1)
                    after(act, s_wide, g - 1)
                    nc.scalar.activation(ex[u][:, :, :], lg[u][:, :, 0:FEXP], ACT.Exp)
                    nc.scalar.activation(sg[u][:, :], lg[u][:, :, FEXP:FEXP + 1].rearrange("p a b -> p (a b)"), ACT.Tanh, scale=0.5).then_inc(s_exp, 1)

                def keep_low(g, u):
                    act.wait_ge(s_low, g + 1)
                    after(act, s_o, g - 1)
                    nc.scalar.copy(low[u][:, :], pl[:, :]).then_inc(s_lowc, 1)

                keep_turned(0, 0)
                for g, u, first, last, lead in pairs(act, G):
                    if not first:
                        keep_low(g - 1, 1 - u)
                    relu(g, u, (0, 1))
                    if not first:
                        exponent(g - 1, 1 - u)
                    relu(g, u, (2, 3))
                    if not last:
                        keep_turned(g + 1, 1 - u)
                keep_low(G - 1, 1)
                exponent(G - 1, 1)

            @block.tensor
            def _(pe):
                def turn(g, u):
                    pe.wait_ge(s_xn, g + 1)
                    after(pe, s_xT, g)
                    for t in range(4):
                        ins = nc.tensor.transpose(pt[:, P * t:P * t + P], xn[u][:, t, :], k["ident"][:, :])
                    ins.then_inc(s_turned, 1)

                def hidden(g, u):
                    pe.wait_ge(s_xT, g + 1)
                    for e in range(FEXP):
                        after(pe, s_hid, FEXP * g + e - 1)
                        nc.tensor.matmul(pf[e % 2][:, :], k["fc1T"][:, e, :], xT[u][:, :], start=True, stop=True).then_inc(s_fc1, 1)

                def gate(g, u):
                    after(pe, s_gatec, g)
                    for t in range(4):
                        ins = nc.tensor.matmul(pg[:, t, :], xT[u][:, P * t:P * t + P], gw[:, :], start=True, stop=True, skip_group_check=True)
                    ins.then_inc(s_gate, 1)

                def ranks(g, u):
                    pe.wait_ge(s_hid, FEXP * g + FEXP)
                    after(pe, s_lowc, g)
                    for e in range(FEXP):
                        ins = nc.tensor.matmul(pl[SLOT * e:SLOT * e + SLOT, :], A[:, e, :], hid[u][:, e, :], start=True, stop=True, skip_group_check=True)
                    ins.then_inc(s_low, 1)

                def turn_weights(g, u):
                    pe.wait_ge(s_wide, g + 1)
                    after(pe, s_wl, g)
                    for t in range(4):
                        ins = nc.tensor.transpose(pw[:, P * t:P * t + P], wide[u][:, t, :], k["ident"][:, :])
                    ins.then_inc(s_wT, 1)

                def output(g, u):
                    pe.wait_ge(s_wl, g + 1)
                    after(pe, s_y, g - 1)
                    for t in range(4):
                        ins = nc.tensor.matmul(po[u][:, t, :], low[u][:, P * t:P * t + P], M[:, :], start=True, stop=True, skip_group_check=True)
                    ins.then_inc(s_o, 1)

                turn(0, 0)
                for g, u, first, last, lead in pairs(pe, G):
                    hidden(g, u)
                    if not last:
                        turn(g + 1, 1 - u)
                    if not first:
                        turn_weights(g - 1, 1 - u)
                    gate(g, u)
                    ranks(g, u)
                    if not first:
                        output(g - 1, 1 - u)
                turn_weights(G - 1, 1)
                output(G - 1, 1)

            @block.sync
            def _(sp):
                for g, u, first, last, lead in pairs(sp, G):
                    sp.wait_ge(s_y, g + 1)
                    sp.dma_start(out_v[:, bass.ds(g * 4, 4), :], yo[u][:, :, :]).then_inc(s_store[u], 16)
                for u in range(2):
                    sp.wait_ge(s_store[u], 8 * G)


MODES = 64
LQ = SEQ // 2 // P
NF = 8
COMPLEX = range(2, NF)
C8 = float(np.sqrt(0.5))


def roots():
    return np.array([[2 * (P * (q % 2) + p) + q // 2 for p in range(P)] for q in range(LQ)])


def freqs():
    f = [8 * np.arange(P), 4 + 8 * np.arange(P)]
    for f1 in (1, 2, 3):
        f += [f1 + 8 * np.arange(P), f1 + 8 * np.arange(P, 2 * P)]
    return np.array(f)


def ssm_tables():
    l = roots()
    tau = np.tan(np.pi * l / SEQ)
    t = np.arange(SEQ // 2)
    ang = 2 * np.pi * ((l[:, :, None] * t) % SEQ) / SEQ
    wt = np.where(l == 0, 0.5, 1.0)[:, :, None] / SEQ
    tau_cols = np.concatenate([tau.T, (tau ** 2).T, -tau.T], 1)
    halves = np.zeros((P, 4))
    halves[0:64, 0] = halves[64:, 1] = 1
    halves[0:64, 2] = halves[64:, 3] = -1
    n = 2 * SEQ
    fwd, inv = [], []
    F = freqs()
    for c in range(NF):
        for wt_ in range(2):
            tt = np.arange(P) + P * wt_
            a = 2 * np.pi * ((tt[:, None] * F[c][None, :]) % n) / n
            C, S = np.cos(a), np.sin(a)
            mats = [C, -S] + ([-C] if c in COMPLEX else [])
            g = np.full(P, 2.0 / n)
            if c == 0:
                mats[1][:, 0] = (-1.0) ** tt
                g[0] = 1.0 / n
            fwd += mats
            IC, IS = (C * g).T, (-S * g).T
            if c == 0:
                IC, IS = (np.cos(a) * g).T, (-np.sin(a) * g).T
                IS[0, :] = (-1.0) ** tt / n
            inv += [IC, IS] + ([-IS] if c in COMPLEX else [])
    f32 = lambda a: np.ascontiguousarray(a, dtype=np.float32)
    return {"c_tau2": f32(np.tile((tau.reshape(-1) ** 2), (P, 1))), "c_tau": f32(tau_cols), "c_halves": f32(halves),
            "c_kcos": f32((np.cos(ang) * wt).transpose(1, 0, 2)), "c_ksin": f32((-np.sin(ang) * wt).transpose(1, 0, 2)),
            "c_alt": f32(((-1.0) ** np.arange(P))[None] / SEQ),
            "c_fwd": f32(np.array(fwd).transpose(1, 0, 2)), "c_inv": f32(np.array(inv).transpose(1, 0, 2))}


def matrix_at():
    at, n = {}, 0
    for c in range(NF):
        for h in range(2):
            at[c, h] = n
            n += 3 if c in COMPLEX else 2
    return at, n


EARLY = matrix_at()[0][4, 0]


def ssm_inputs(m):
    return {"rl": m.sb("rl", [64, 2, P]),
            "r3": m.sb("r3", [64, 3, 2 * P]),
            "rs": m.sb("rs", [2, 64]), "Drow": m.sb("Drow", [1, P]),
            "tau2": m.sb("tau2", [P, HALF]), "tau": m.sb("tau", [P, 12]), "halves": m.sb("halves", [P, 4]), "alt": m.sb("alt", [1, P]),
            "kcos": m.sb("kcos", [P, LQ, SEQ // 2]), "ksin": m.sb("ksin", [P, LQ, SEQ // 2])}


def load_ssm_inputs(sp, w, b, sem):
    for j, n in enumerate(("re", "im")):
        sp.dma_start(b["rl"][:, j, :].rearrange("p (a n) -> p a n", a=2), w[f"L1_attn_Lambda_{n}"].rearrange("(a p) n -> p a n", a=2)).then_inc(sem, 16)
    for j, n in enumerate("PBC"):
        sp.dma_start(b["r3"][:, j, :].rearrange("p (a x) -> p a x", a=2), w[f"L1_attn_{n}"].rearrange("(a p) n c -> p a (n c)", a=2)).then_inc(sem, 16)
    sp.dma_start(b["rs"][:, :], w["L1_attn_log_step"].rearrange("(a p) -> a p", a=2)).then_inc(sem, 16)
    sp.dma_start(b["Drow"][:, :], w["L1_attn_D"].rearrange("(a p) -> a p", a=1)).then_inc(sem, 16)
    for n in ("tau2", "tau", "halves", "alt"):
        sp.dma_start(b[n][:, :], w["c_" + n]).then_inc(sem, 16)
    for n in ("kcos", "ksin"):
        sp.dma_start(b[n][:, :, :], w["c_" + n]).then_inc(sem, 16)


def ssm_kernel(nc, w, k, Kt, b, H, acc, stats, fwd_early):
    rl, r3, rs, Drow, tau2, tau, halves, alt, kcos, ksin = (b[n] for n in "rl r3 rs Drow tau2 tau halves alt kcos ksin".split())
    with ExitStack() as ctx:
        m = Mem(nc, ctx, "sk", k["banks"])
        NA = 9
        rsT, sb_ = m.sb("rsT", [64, 2]), m.sb("sbc", [64, 2, 64])
        V = m.sb("V", [P, NA, 64])
        g = lambda n: m.sb(n, [P, 64])
        lr, li, mr, mi, q2, ns = g("lr"), g("li"), g("mr"), g("mi"), g("q2"), g("ns")
        WW = m.sb("WW", [P, 4, 4, 2, 64])
        t1, t2 = m.sb("t1", [P, 4, 2, 64]), m.sb("t2", [P, 4, 2, 64])
        SQUARE_READY, PRODUCTS_READY = 6, 9
        W2 = m.sb("W2", [P, 64, 2, 32])
        p512 = m.sb("p512", [1, P])
        SS = m.sb("SS", [P, LQ, 64, 64])
        late = [m.sb(f"late{j}", [P, 4, HALF]) for j in range(3)]
        sqr, guess, R = ([t[:, u, :] for u in range(4)] for t in late)
        A, B = ([W2[:, 32 * j + 16 * u:32 * j + 16 * u + 16, :, :].rearrange("p n a s -> p (n a s)").rearrange("p (h s) -> p h s", s=8)
                 for u in range(2)] for j in range(2))
        KP = [late[u][:, :, :].rearrange("p (a b) (c d) -> p a b c d", a=2, c=4) for u in range(2)]
        tmp = ([late[2][:, j, :].rearrange("p (u a b) -> p u a b", u=2, a=2) for j in range(4)]
               + [WW[:, j].rearrange("p v c n -> p (v c n)").rearrange("p (u a b) -> p u a b", u=2, a=2) for j in range(4)])
        PQ = m.sb("PQ", [P, LQ, 2, P])
        odd = late[0][:, 0, :]
        pa, pb, pc, pd = m.ps(), m.ps(), m.ps(), m.ps()
        ps = [m.ps((P, LQ, 64)) for u in range(2)]
        s_pe, s_dve, s_act, s_k = m.sem("pe"), m.sem("dve"), m.sem("act"), m.sem("k")
        two = lambda n: [m.sem(f"{n}{u}") for u in range(2)]
        s_guess, s_R = [m.sem(f"guess{u}") for u in range(2)], [m.sem(f"R{u}") for u in range(4)]
        s_S, s_Sc, s_act2, s_dve5 = two("S"), two("Sc"), m.sem("act2"), m.sem("dve5")
        flat = lambda t: t[:, :, :].rearrange("p a b -> p (a b)")
        CHUNKS = 4
        per = NT // CHUNKS
        s_H = [m.sem(f"H{c}") for c in range(CHUNKS)]
        s_early = m.sem("early")
        acc_v = acc.rearrange("(n p) c -> p n c", p=P)
        with nc.Block() as block:
            @block.sync
            def _(sp):
                for c in range(CHUNKS):
                    sp.dma_start(H[:, per * c:per * c + per, :], acc_v[:, per * c:per * c + per, :]).then_inc(s_H[c], 16)
                sp.dma_start(fwd_early[:, :, :], w["c_fwd"][:, 0:EARLY, :]).then_inc(s_early, 16)
                for c in range(CHUNKS):
                    sp.wait_ge(s_H[c], 16)
                sp.wait_ge(s_early, 16)

            @block.tensor
            def _(pe):
                nc.tensor.transpose(pa[0:64, 0:2], rs[:, :], k["ident"][0:2, 0:2]).then_inc(s_pe, 1)
                pe.wait_ge(s_dve, 2)
                I64 = k["ident"][0:64, 0:64]
                nc.tensor.transpose(pa[:, 64:128], sb_[:, :, :].rearrange("p a b -> p (a b)"), I64)
                for j in range(2):
                    nc.tensor.transpose(pb[:, 64 * j:64 * j + 64], rl[:, j, :], I64)
                for n, j in enumerate((2, 1, 0)):
                    for c in range(2):
                        ins = nc.tensor.transpose(pb[:, 64 * (2 + 2 * n + c):64 * (3 + 2 * n + c)], r3[:, j, c::2], I64)
                ins.then_inc(s_pe, 1)
                pe.wait_ge(s_dve, PRODUCTS_READY)
                for a in range(2):
                    ins = nc.tensor.matmul(pa[0:1, 64 * a:64 * a + 64], halves[:, 2 + a:3 + a], WW[:, 2, 0, 0, :], start=True, stop=True, skip_group_check=True)
                ins.then_inc(s_pe, 1)
                pe.wait_ge(s_k, 1)
                for i in passes(pe, MODES // 4):
                    for u in range(4):
                        pe.wait_ge(s_R[u], i + 1)
                        pe.wait_ge(s_Sc[u % 2], 2 * i + u // 2)
                        for q in range(LQ):
                            ins = nc.tensor.matmul(ps[u % 2][:, q, :], R[u][:, P * q:P * q + P], W2[:, i * 4 + u, :, :].rearrange("p a b -> p (a b)"),
                                                   start=True, stop=True, skip_group_check=True)
                        ins.then_inc(s_S[u % 2], 1)
                pe.wait_ge(s_k, 2)
                for t in range(4):
                    c = slice(P * t, P * t + P)
                    for q in range(LQ):
                        dst = (pc, pd)[q // 2][:, c]
                        nc.tensor.matmul(dst, kcos[:, q, c], PQ[:, q, 0, :], start=(q % 2 == 0), stop=False, skip_group_check=True)
                        ins = nc.tensor.matmul(dst, ksin[:, q, c], PQ[:, q, 1, :], start=False, stop=(q == 3), skip_group_check=True)
                        if q == 1:
                            nc.tensor.matmul(dst, alt[:, :], p512[:, :], start=False, stop=True, skip_group_check=True)
                ins.then_inc(s_pe, 1)

            @block.scalar
            def _(act):
                act.wait_ge(s_dve, 1)
                nc.scalar.activation(rsT[:, :], rsT[:, :], ACT.Exp).then_inc(s_act, 1)
                nc.scalar.preload_act_table_set("natural_log_exp_and_others")
                act.wait_ge(s_dve, SQUARE_READY)
                for i in passes(act, MODES // 4):
                    st = Steps(act, s_act2, i, 4)
                    for v in range(2):
                        pair = (2 * v, 2 * v + 1)
                        for u in pair:
                            act.wait_ge(s_R[u], i)
                            ins = nc.scalar.activation(sqr[u], tau2[:, :], ACT.Square, bias=mr[:, bass.ds(i * 4 + u, 1)])
                        st.link(ins)
                        for u in pair:
                            ins = nc.scalar.activation(guess[u], sqr[u], ACT.Ln, bias=q2[:, bass.ds(i * 4 + u, 1)])
                        st.link(ins)
                        for u in pair:
                            ins = nc.scalar.activation(guess[u], guess[u], ACT.Exp, scale=-1.0)
                        ins.then_inc(s_guess[v], 1)
                    st.close()

            @block.vector
            def _(dve):
                st = Steps(dve, s_dve)
                dve.wait_ge(s_pe, 1)
                st.link(nc.vector.tensor_copy(rsT[:, :], pa[0:64, 0:2]))
                dve.wait_ge(s_act, 1)
                st.link(nc.vector.tensor_scalar(sb_[:, :, :], spread(rsT[:, :], 64), 0.5, None, ALU.mult))
                dve.wait_ge(s_pe, 2)
                nc.vector.tensor_copy(V[:, 8, :], pa[:, 64:128])
                st.link(nc.vector.tensor_copy(V[:, 0:8, :].rearrange("p a b -> p (a b)"), pb[:, :]))
                TT, MUL = nc.vector.tensor_tensor, ALU.mult
                s = V[:, 8, :]
                nc.vector.scalar_tensor_tensor(out=lr[:, :], in0=V[:, 0, :], scalar=-1e-4, in1=s, op0=ALU.min, op1=MUL)
                nc.vector.tensor_scalar(ns[:, :], s, -1.0, None, MUL)
                st.link(TT(li[:, :], V[:, 1, :], s, MUL))
                TT(t1[:, 0, 0, :], lr[:, :], lr[:, :], MUL)
                TT(t1[:, 0, 1, :], li[:, :], li[:, :], MUL)
                st.link(nc.vector.scalar_tensor_tensor(out=mi[:, :], in0=lr[:, :], scalar=2.0, in1=li[:, :], op0=MUL, op1=MUL))
                TT(mr[:, :], t1[:, 0, 0, :], t1[:, 0, 1, :], ALU.subtract)
                st.link(TT(q2[:, :], mi[:, :], mi[:, :], MUL))
                assert st.n == SQUARE_READY
                left = lambda c: V[:, 2 + c:8:4, :].unsqueeze(2).broadcast_to([P, 2, 2, 64])
                right_ = lambda c: V[:, 4 + c:8:2, :].unsqueeze(1).broadcast_to([P, 2, 2, 64])
                four = lambda t, c: t[:, :, c, :].rearrange("p (a b) n -> p a b n", a=2)
                over = lambda a: a[:, :].unsqueeze(1).unsqueeze(1).broadcast_to([P, 4, 2, 64]) 
                cr, ci = WW[:, 2, :, 0, :], WW[:, 2, :, 1, :]
                TT(four(t1, 0), left(0), right_(0), MUL)
                TT(four(t2, 0), left(1), right_(1), MUL)
                TT(four(t1, 1), left(0), right_(1), MUL)
                st.link(TT(four(t2, 1), left(1), right_(0), MUL))
                TT(cr, t1[:, :, 0, :], t2[:, :, 0, :], ALU.add)
                st.link(TT(ci, t1[:, :, 1, :], t2[:, :, 1, :], ALU.subtract))
                st.link(TT(WW[:, 2], WW[:, 2], over(ns), MUL))
                assert st.n == PRODUCTS_READY

                def times(out, x, yr, yi, conj):
                    TT(t1[:, :, :, :], WW[:, x], over(yr), MUL)
                    st.link(TT(t2[:, :, :, :], WW[:, x], over(yi), MUL))
                    TT(WW[:, out, :, 0, :], t1[:, :, 0, :], t2[:, :, 1, :], ALU.add if conj else ALU.subtract)
                    st.link(TT(WW[:, out, :, 1, :], t1[:, :, 1, :], t2[:, :, 0, :], ALU.subtract if conj else ALU.add))

                times(0, 2, lr, li, False)
                times(1, 0, mr, mi, True)
                times(3, 2, mr, mi, True)
                for a in range(2):
                    ins = nc.vector.tensor_scalar(W2[:, :, a, :], WW[:, :, :, :, :].rearrange("p k v c n -> p n (k v c)"), halves[:, 2 + a:3 + a], None, MUL)
                dve.wait_ge(s_pe, 3)
                nc.vector.tensor_copy(p512[:, :], pa[0:1, 0:P]).then_inc(s_k, 1)
                STT = nc.vector.scalar_tensor_tensor

                def keep_sums(i, pair):
                    for u in pair:
                        dve.wait_ge(s_S[u % 2], 2 * i + u // 2 + 1)
                        nc.vector.tensor_copy(SS[:, :, i * 4 + u, :], ps[u % 2][:, :, :]).then_inc(s_Sc[u % 2], 1)

                TILES_EACH = NT // (MODES // 4)

                def reciprocals(i):
                    s5 = Steps(dve, s_dve5, i, 2)
                    for v in range(2):
                        dve.wait_ge(s_guess[v], i + 1)
                        for u in (2 * v, 2 * v + 1):
                            ins = STT(out=sqr[u], in0=sqr[u], scalar=q2[:, bass.ds(i * 4 + u, 1)], in1=guess[u], op0=ALU.add, op1=MUL)
                        s5.link(ins)
                        for u in (2 * v, 2 * v + 1):
                            STT(out=R[u], in0=sqr[u], scalar=-2.0, in1=guess[u], op0=ALU.add, op1=MUL).then_inc(s_R[u], 1)
                        for n in range(TILES_EACH // 2):
                            n = i * TILES_EACH + v * (TILES_EACH // 2) + n
                            nc.vector.bn_stats(stats[:, n, :], H[:, n, :])
                        if v:
                            keep_sums(i, (0, 1))
                        elif not isinstance(i, int):
                            keep_sums(i - 1, (2, 3))
                    s5.close()
                for c in range(CHUNKS):
                    dve.wait_ge(s_H[c], 16)
                for i in passes(dve, MODES // 4):
                    reciprocals(i)
                keep_sums(MODES // 4 - 1, (2, 3))
                for u in range(2):
                    dve.wait_ge(s_Sc[u], MODES // 2)
                kr, ki = ([KP[u][:, :, c, v, :] for u in range(2) for v in range(4)] for c in range(2))
                a0, a1, a2, a3, a4, a5, a6, a7 = (x[:, :, :, :] for x in tmp)

                def both(out, x, vx, y, vy, op):
                    for u in range(2):
                        ins = TT(out[:, u], x[4 * u + vx], y[4 * u + vy], op)
                    return ins

                def with_product(out, x, y, vy, op):
                    for u in range(2):
                        ins = TT(out[:, u], x[:, u], y[4 * u + vy], op)
                    return ins

                for v in range(LQ // 2):
                    pair = [(u, 2 * v + u) for u in range(2)]
                    T, T2, NT_ = (lambda q: tau[:, q:q + 1]), (lambda q: tau[:, 4 + q:5 + q]), (lambda q: tau[:, 8 + q:9 + q])
                    for u, q in pair:
                        sums = lambda kk: SS[:, q, :, :].rearrange("p n (a s) -> p (n a) s", a=2)[:, :, 8 * kk:8 * kk + 8]
                        STT(out=A[u], in0=sums(0), scalar=T2(q), in1=sums(1), op0=MUL, op1=ALU.add)
                        ins = STT(out=B[u], in0=sums(2), scalar=T2(q), in1=sums(3), op0=MUL, op1=ALU.add)
                    st.link(ins)
                    for u, q in pair:
                        pick = lambda X, c: X[u].rearrange("p h (v c) -> p v c h", c=2)[:, :, c, :]
                        STT(out=KP[u][:, 0, 0], in0=pick(B, 1), scalar=NT_(q), in1=pick(A, 0), op0=MUL, op1=ALU.add)
                        STT(out=KP[u][:, 0, 1], in0=pick(B, 0), scalar=T(q), in1=pick(A, 1), op0=MUL, op1=ALU.add)
                        STT(out=KP[u][:, 1, 0], in0=pick(B, 1), scalar=T(q), in1=pick(A, 0), op0=MUL, op1=ALU.add)
                        ins = STT(out=KP[u][:, 1, 1], in0=pick(B, 0), scalar=NT_(q), in1=pick(A, 1), op0=MUL, op1=ALU.add)
                    st.link(ins)
                    both(a0, kr, 1, kr, 2, MUL)
                    both(a1, ki, 1, ki, 2, MUL)
                    both(a2, kr, 1, ki, 2, MUL)
                    both(a3, ki, 1, kr, 2, MUL)
                    for u in range(2):
                        nc.vector.tensor_scalar(a4[:, u], kr[4 * u + 3], 1.0, None, ALU.add)
                    st.link(both(a6, ki, 3, ki, 3, MUL))
                    TT(a5, a4, a4, MUL)
                    TT(a0, a0, a1, ALU.subtract)
                    st.link(TT(a2, a2, a3, ALU.add))
                    TT(a5, a5, a6, ALU.add)
                    TT(a1, a0, a4, MUL)
                    st.link(with_product(a3, a2, ki, 3, MUL))
                    nc.vector.reciprocal(a5, a5)
                    TT(a6, a2, a4, MUL)
                    st.link(with_product(a7, a0, ki, 3, MUL))
                    TT(a1, a1, a3, ALU.add)
                    st.link(TT(a6, a6, a7, ALU.subtract))
                    TT(a1, a1, a5, MUL)
                    st.link(TT(a6, a6, a5, MUL))
                    for u in range(2):
                        TT(a1[:, u], kr[4 * u], a1[:, u], ALU.subtract)
                    for u in range(2):
                        ins = TT(a6[:, u], ki[4 * u], a6[:, u], ALU.subtract)
                    st.link(ins)
                    TT(a0[:, :, 0], a1[:, :, 0], a1[:, :, 1], ALU.add)
                    st.link(TT(a0[:, :, 1], a6[:, :, 0], a6[:, :, 1], ALU.subtract))
                    unpair = lambda x: x.rearrange("p (n a) -> p a n", a=2)
                    for u, q in pair:
                        out = lambda c: PQ[:, q, c, :].rearrange("p (a n) -> p a n", a=2)
                        STT(out=out(0), in0=unpair(a0[:, u, 1, :]), scalar=NT_(q), in1=unpair(a0[:, u, 0, :]), op0=MUL, op1=ALU.add)
                        ins = STT(out=out(1), in0=unpair(a0[:, u, 0, :]), scalar=T(q), in1=unpair(a0[:, u, 1, :]), op0=MUL, op1=ALU.add)
                    if v < LQ // 2 - 1:
                        st.link(ins)
                ins.then_inc(s_k, 1)
                dve.wait_ge(s_pe, 4)
                st.link(nc.vector.tensor_copy(odd, pd[:, :]))
                TT(Kt[:, 0:4, :].rearrange("p a b -> p (a b)"), pc[:, :], odd, ALU.add)
                st.link(TT(Kt[:, 4:8, :].rearrange("p a b -> p (a b)"), pc[:, :], odd, ALU.subtract))
                st.link(TT(Kt[0:1, 0, :], Kt[0:1, 0, :], Drow[:, :], ALU.add))


def ssm_convolve(nc, w, k, H, mean, rstd, Kt, stats, fwd_early):
    with ExitStack() as ctx:
        m = Mem(nc, ctx, "sc", k["banks"])
        at, NM = matrix_at()
        fwd_late, inv = m.sb("fwd_late", [P, NM - EARLY, P]), m.sb("inv", [P, NM, P])
        fwd = lambda n: fwd_early[:, n, :] if n < EARLY else fwd_late[:, n - EARLY, :]
        NB = 2
        W_ = NB * P
        xu = m.sb("xu", [P, 4, 2, NB, P])
        names = "s02 d02 s13 d13 f0 f4 r1 n1 r3 n3".split()
        Y = {n: m.sb(n, [P, 2 * W_]) for n in names}
        KA, KB = m.sb("KA", [P, NF, 2, P]), m.sb("KB", [P, NF, P])
        dc = m.sb("dc", [P, 1])
        T1 = [m.sb(f"T1{u}", [P, 2, NB, P]) for u in range(2)]
        T2 = [m.sb(f"T2{u}", [P, 2, NB, P]) for u in range(2)]
        YF = m.sb("YF", [P, NF, 2, W_])
        Z = [m.sb(f"Z{j}", [P, 2 * W_]) for j in range(8)]
        F = [m.sb(f"F{j}", [P, 2 * W_]) for j in range(8)]
        pf = [m.ps() for j in range(4)]
        pz = [m.ps() for j in range(4)]
        s_inv, s_xu = m.sem("inv"), m.sem("xu")
        s_in, s_f, s_kf, s_dve, s_dve2, s_ka = m.sem("in"), m.sem("f"), m.sem("kf"), m.sem("dve"), m.sem("dve2"), m.sem("ka")
        s_y, s_tile, s_used, s_z, s_zc, s_h, s_prod, s_dve3 = (m.sem(n) for n in ("y", "tile", "used", "z", "zc", "h", "prod", "dve3"))
        TT, MUL, ADD, SUB = nc.vector.tensor_tensor, ALU.mult, ALU.add, ALU.subtract
        STT = nc.vector.scalar_tensor_tensor
        inputs = {0: ("f0", None), 1: ("f4", None), 2: ("r1", "n1"), 3: ("r1", "n1"), 4: ("d02", "d13"), 5: ("d02", "d13"),
                  6: ("r3", "n3"), 7: ("r3", "n3")}
        results = [((0,), 0), ((1,), 0), ((2, 3), 0), ((2, 3), 1), ((4, 5), 0), ((4, 5), 1), ((6, 7), 0), ((6, 7), 1)]

        def split(x, nb, st):
            y = {n: Y[n][:, 0:2 * nb * P] for n in names}
            TT(y["s02"], x(0), x(2), ADD)
            TT(y["d02"], x(0), x(2), SUB)
            TT(y["s13"], x(1), x(3), ADD)
            st.link(TT(y["d13"], x(1), x(3), SUB))
            TT(y["f0"], y["s02"], y["s13"], ADD)
            TT(y["f4"], y["s02"], y["s13"], SUB)
            STT(out=y["r1"], in0=y["d13"], scalar=C8, in1=x(0), op0=MUL, op1=ADD)
            STT(out=y["r3"], in0=y["d13"], scalar=-C8, in1=x(0), op0=MUL, op1=ADD)
            STT(out=y["n1"], in0=y["s13"], scalar=C8, in1=x(2), op0=MUL, op1=ADD)
            return STT(out=y["n3"], in0=y["s13"], scalar=C8, in1=x(2), op0=MUL, op1=SUB)

        def forward(c, dst, nb):
            a, b = inputs[c]
            terms = [(0, a), (1, b)] if b else [(0, a)]
            for part in range(2):
                n = 0
                for h in range(2):
                    for j, name in terms:
                        ins = nc.tensor.matmul(dst(part), fwd(at[c, h] + part + j), Y[name][:, h * nb * P:(h + 1) * nb * P],
                                               start=(n == 0), stop=(n == 2 * len(terms) - 1), skip_group_check=True)
                        n += 1
            return ins

        def spectrum_part(c, part):
            return pz[2 * part + c // 4][:, P * (c % 4):P * (c % 4) + P]

        with nc.Block() as block:
            @block.sync
            def _(sp):
                sp.dma_start(fwd_late[:, :, :], w["c_fwd"][:, EARLY:NM, :]).then_inc(s_in, 16)
                sp.dma_start(inv[:, :, :], w["c_inv"]).then_inc(s_inv, 16)
                sp.wait_ge(s_inv, 16)

            @block.tensor
            def _(pe):
                pe.wait_ge(s_kf, 1)
                for c in range(NF):
                    if c == 4:
                        pe.wait_ge(s_in, 16)
                    ins = forward(c, lambda p_: spectrum_part(c, p_), 1)
                ins.then_inc(s_f, 1)

                def back(i):
                    pe.wait_ge(s_prod, NF * i + NF)
                    for j, (cs_, kind) in enumerate(results):
                        if j >= 4:
                            pe.wait_ge(s_zc, 8 * i + j - 3)
                        elif not isinstance(i, int):
                            pe.wait_ge(s_zc, 8 * (i - 1) + j + 5)
                        for h in range(2):
                            n = 0
                            for c in cs_:
                                for src, mat in (((0, 0), (1, 1)), ((0, 2), (1, 0)))[kind]:
                                    ins = nc.tensor.matmul(pz[j % 4][:, W_ * h:W_ * h + W_], inv[:, at[c, h] + mat, :], YF[:, c, src, :],
                                                           start=(n == 0), stop=(n == 2 * len(cs_) - 1), skip_group_check=True)
                                    n += 1
                        ins.then_inc(s_z, 1)

                def spectrum(i):
                    pe.wait_ge(s_y, i + 1)
                    for c in range(NF):
                        if c >= 4:
                            pe.wait_ge(s_used, NF * i + c - 3)
                        elif not isinstance(i, int):
                            pe.wait_ge(s_used, NF * (i - 1) + c + 5)
                        forward(c, lambda p_: pf[c % 4][:, W_ * p_:W_ * p_ + W_], NB).then_inc(s_tile, 1)

                spectrum(0)
                pe.wait_ge(s_inv, 16)
                for i in passes(pe, BATCH // NB - 1):
                    back(i)
                    spectrum(i + 1)
                back(BATCH // NB - 1)

            @block.scalar
            def _(act):
                act.wait_ge(s_f, 1)
                for c in range(NF):
                    for j in range(2 if c else 1):
                        ins = nc.scalar.copy(KA[:, c, j, :], spectrum_part(c, 0))
                ins.then_inc(s_ka, 1)
                for i in passes(act, BATCH // NB):
                    if not isinstance(i, int):
                        act.wait_ge(s_h, i)
                    for j in range(8):
                        act.wait_ge(s_z, 8 * i + j + 1)
                        nc.scalar.copy(Z[j][:, :], pz[j % 4][:, :]).then_inc(s_zc, 1)

            @block.gpsimd
            def _(pool):
                for i in passes(pool, BATCH // NB):
                    for c in range(NF):
                        pool.wait_ge(s_used, NF * i + c + 1)
                        u = c % 2
                        o = lambda p_: YF[:, c, p_, :].rearrange("p (b h) -> p b h", b=NB)
                        nc.gpsimd.tensor_tensor(o(0), T1[u][:, 0], T2[u][:, 1], SUB)
                        nc.gpsimd.tensor_tensor(o(1), T1[u][:, 1], T2[u][:, 0], ADD).then_inc(s_prod, 1)

            @block.vector
            def _(dve):
                def inputs_of(i, again=True):
                    s2 = Steps(dve, s_dve2, i, 1)
                    if again:
                        normalise(i)
                    dve.wait_ge(s_xu, i + 1)
                    split(lambda j: xu[:, j].rearrange("p w b h -> p (w b h)"), NB, s2).then_inc(s_y, 1)
                    s2.close()

                def normalise(i):
                    for b in range(NB):
                        for t in range(TILES):
                            n = (i * NB + b) * TILES + t
                            ins = nc.vector.tensor_scalar(xu[:, t // 2, t % 2, b, :], H[:, n, :], mean[:, bass.ds(n, 1)], rstd[:, bass.ds(n, 1)], SUB, MUL)
                    ins.then_inc(s_xu, 1)

                st = Steps(dve, s_dve)
                st.link(nc.vector.memset(dc[:, :], 1.0))
                st.link(nc.vector.memset(dc[0:1, :], 0.0))
                split(lambda j: Kt[:, 2 * j:2 * j + 2, :].rearrange("p a b -> p (a b)"), 1, st).then_inc(s_kf, 1)
                normalise(0)
                dve.wait_ge(s_f, 1)
                inputs_of(0, again=False)
                nc.vector.tensor_scalar(KB[:, 0, :], spectrum_part(0, 1), dc[:, 0:1], None, MUL)
                for c in range(1, NF):
                    nc.vector.tensor_copy(KB[:, c, :], spectrum_part(c, 1))
                dve.wait_ge(s_ka, 1)
                st.link(nc.vector.tensor_scalar(KA[:, 0, 1, :], KA[:, 0, 0, :], dc[:, 0:1], None, MUL))
                st.link(nc.vector.tensor_copy(KA[0:1, 0, 1, :], spectrum_part(0, 1)[0:1, :]))

                def products(i, c):
                    dve.wait_ge(s_tile, NF * i + c + 1)
                    if c >= 2:
                        dve.wait_ge(s_prod, NF * i + c - 1)
                    elif not isinstance(i, int):
                        dve.wait_ge(s_prod, NF * (i - 1) + c + 7)
                    u = c % 2
                    src = pf[c % 4][:, :].rearrange("p (c b h) -> p c b h", c=2, b=NB)
                    TT(T1[u][:, :, :, :], src, KA[:, c, :, :].unsqueeze(2).broadcast_to([P, 2, NB, P]), MUL)
                    TT(T2[u][:, :, :, :], src, KB[:, c, :].unsqueeze(1).unsqueeze(1).broadcast_to([P, 2, NB, P]), MUL).then_inc(s_used, 1)

                def outputs(i, part, s3):
                    z0, z4, r1, i1, r2, i2, r3, i3 = (z[:, :] for z in Z)
                    sA, dA, sr, dr, si, di, y2, y6 = (x[:, :] for x in F)
                    have = lambda n: dve.wait_ge(s_zc, 8 * i + n)
                    if part == 0:
                        have(2)
                        TT(sA, z0, z4, ADD)
                        s3.link(TT(dA, z0, z4, SUB))
                    if part == 1:
                        have(5)
                        TT(z0, sA, r2, ADD)
                        TT(z4, sA, r2, SUB)
                    if part == 2:
                        have(6)
                        TT(y2, dA, i2, SUB)
                        TT(y6, dA, i2, ADD)
                        have(7)
                        TT(sr, r1, r3, ADD)
                    if part == 3:
                        TT(dr, r1, r3, SUB)
                        have(8)
                        TT(si, i1, i3, ADD)
                        s3.link(TT(di, i1, i3, SUB))
                    if part == 4:
                        TT(r3, dr, si, SUB)
                        TT(i3, dr, si, ADD)
                        TT(z0, z0, sr, ADD)
                        s3.link(TT(z4, z4, di, SUB))
                    if part == 5:
                        STT(out=y2, in0=r3, scalar=C8, in1=y2, op0=MUL, op1=ADD)
                        s3.link(STT(out=y6, in0=i3, scalar=-C8, in1=y6, op0=MUL, op1=ADD))
                    if part in (6, 7):
                        for j in (0, 1) if part == 6 else (2, 3):
                            y = (z0, y2, z4, y6)[j]
                            for b in range(NB):
                                dst = H[:, bass.ds((i * NB + b) * TILES + 2 * j, 2), :]
                                ins = TT(dst, dst, y.rearrange("p (w b h) -> p w b h", w=2, b=NB)[:, :, b, :], ADD)
                        if part == 7:
                            s3.link(ins)
                            for n in range(NB * TILES):
                                ins = nc.vector.bn_stats(stats[:, i * (NB * TILES) + n, :], H[:, i * (NB * TILES) + n, :])
                            ins.then_inc(s_h, 1)

                for c in range(NF):
                    products(0, c)
                for i in passes(dve, BATCH // NB - 1):
                    s3 = Steps(dve, s_dve3, i, 5)
                    inputs_of(i + 1)
                    for c in range(NF):
                        products(i + 1, c)
                        outputs(i, c, s3)
                    s3.close()
                s3 = Steps(dve, s_dve3, BATCH // NB - 1, 5)
                for c in range(NF):
                    outputs(BATCH // NB - 1, c, s3)


def tables():
    return {**attention_tables(), **moe_tables(), **ssm_tables()}


def tower(nc, w, out):
    USED.clear()
    rows = nc.dram_tensor("rows", (TOK, ROW), F32).ap()
    acc = nc.dram_tensor("acc", (TOK, D), F32).ap()
    with ExitStack() as ctx:
        m = Mem(nc, ctx, "all")
        k = constants(nc, m)
        H = m.sb("H", [P, NT, D])
        mean, rstd = m.sb("mean", [P, NT]), m.sb("rstd", [P, NT])
        stats = m.sb("stats", [P, NT, 6])
        load_constants(nc, w, k)
        embed_tokens(nc, w, k, H, stats)
        with ExitStack() as ctx2:
            X2 = Mem(nc, ctx2, "x2").sb("X2", [P, NT, D])
            attention(nc, w, k, H, X2, mean, rstd, stats)
            row_stats(nc, k, stats, mean, rstd, "st_mlp")
            mlp(nc, w, k, H, X2, mean, rstd, stats, acc)
        row_stats(nc, k, stats, mean, rstd, "st_moe")
        Kt = m.sb("Kt", [P, TILES, P])
        fwd_early = m.sb("fwd_early", [P, EARLY, P])
        with ExitStack() as ctx2:
            ssm = ssm_inputs(Mem(nc, ctx2, "si"))
            with ExitStack() as ctx3:
                lists = Mem(nc, ctx3, "moe").sb("lists", [P, EXPERTS, NBLK], U32)
                moe_route(nc, w, k, H, mean, rstd, rows, lists, lambda sp, sem: load_ssm_inputs(sp, w, ssm, sem))
                moe_experts(nc, w, k, rows, acc, lists)
            ssm_kernel(nc, w, k, Kt, ssm, H, acc, stats, fwd_early)
        row_stats(nc, k, stats, mean, rstd, "st_ssm")
        ssm_convolve(nc, w, k, H, mean, rstd, Kt, stats, fwd_early)
        row_stats(nc, k, stats, mean, rstd, "st_ffn")
        ffn(nc, w, k, H, mean, rstd, out)


def kernel(**inputs):
    import numpy as _np
    import concourse.bacc as _bacc
    from concourse import mybir as _mybir
    from concourse.bass_utils import run_bass_kernel_spmd as _run

    nc = _bacc.Bacc("TRN2", target_bir_lowering=False, num_devices=1)
    arrays, args = {}, {}
    for name, a in {**inputs, **tables()}.items():
        a = _np.ascontiguousarray(a)
        arrays[f"in_{name}"] = a
        args[name] = nc.dram_tensor(f"in_{name}", a.shape, _mybir.dt.from_np(a.dtype), kind="ExternalInput").ap()
    out = nc.dram_tensor("out_0", (BATCH, SEQ, D), F32, kind="ExternalOutput").ap()
    tower(nc, args, out)
    r = _run(nc, [arrays], core_ids=[0])
    return r.results[0]["out_0"]
```
